# Optimizing a Trainium2 kernel written in Bass

```python
import numpy as np
import jax
import jax.numpy as jnp

def _softmax(x, axis=-1):
    return jax.nn.softmax(x, axis=axis)

def _gelu(x):
    return jax.nn.gelu(x, approximate=True)

def _silu(x):
    return jax.nn.silu(x)

def _sigmoid(x):
    return jax.nn.sigmoid(x)

def _layernorm(x, axis=-1, eps=1e-05):
    m = jnp.mean(x, axis=axis, keepdims=True)
    v = jnp.var(x, axis=axis, keepdims=True)
    return (x - m) / jnp.sqrt(v + eps)

def _scatter_add(tgt, idx, src, axis=0):
    return tgt.at[idx].add(src)

def _segment_sum(src, seg, n):
    return jax.ops.segment_sum(src, seg, n)
kernel_name = 'mk_xattn_ffn_d2_seqx_r8_9a0997'

def setup_inputs(seed: int=0):
    np.random.seed(seed)
    _w = jnp.asarray

    def _rec_inputs():
        import jax
        import jax.numpy as jnp
        _rk = jax.random.key(seed)
        x = 7.22e-05 + 1 * jax.random.normal(jax.random.fold_in(_rk, 1), (8, 256, 128), jnp.float32)
        _lenS = 256 - jax.random.randint(jax.random.fold_in(_rk, 7), (8,), 0, max(1, 256 // 4) + 1, jnp.int32)
        _lenS2 = 256 - jax.random.randint(jax.random.fold_in(_rk, 8), (8,), 0, max(1, 256 // 4) + 1, jnp.int32)
        _ctx_1024P = jax.random.normal(jax.random.fold_in(_rk, 11), (8, 16, 128), jnp.float32)
        _ctx_1024c = jax.random.dirichlet(jax.random.fold_in(_rk, 511), 0.3 * jnp.ones((16,), jnp.float32), (8, 256))
        _ctx_1024t = jnp.einsum('bsk,bkd->bsd', _ctx_1024c, _ctx_1024P)
        _ctx_1024t = _ctx_1024t * jax.lax.rsqrt(jnp.mean(jnp.square(_ctx_1024t)) + 1e-12) * 0.953939
        ctx_1024 = 4.13588e-05 + 0.999923 * (_ctx_1024t + 0.3 * jax.random.normal(jax.random.fold_in(_rk, 611), (8, 256, 128), jnp.float32))
        return (x, ctx_1024)
    x, ctx_1024 = _rec_inputs()

    def _L0_xattn_setup():
        import jax, jax.numpy as jnp
        import numpy as np
        EMBED = 128
        HEADS = 16
        HEAD_DIM = EMBED // HEADS
        WINDOW = 128
        HALF = WINDOW // 2
        SCALE = HEAD_DIM ** (-0.5)
        B, T = (2, 512)

        def _sliding_window_attn(q, k, v):
            Bq, H, Tq, D = q.shape
            Bk = HALF
            nb = Tq // Bk
            qb = q.reshape(Bq, H, nb, Bk, D)

            def ctx(x):
                xb = x.reshape(Bq, H, nb, Bk, D)
                prev = jnp.concatenate([jnp.zeros_like(xb[:, :, :1]), xb[:, :, :-1]], axis=2)
                return jnp.concatenate([prev, xb], axis=3)
            kc, vc = (ctx(k), ctx(v))
            scores = jnp.einsum('bhnrd,bhncd->bhnrc', qb, kc)
            r = jnp.arange(Bk)[:, None]
            c = jnp.arange(2 * Bk)[None, :]
            band = (c >= r) & (c <= r + Bk)
            b_idx = jnp.arange(nb)[:, None, None]
            valid = band[None] & ((b_idx > 0) | (c[None] >= Bk))
            neg_inf = jnp.finfo(jnp.float32).min
            scores = jnp.where(valid[None, None], scores.astype(jnp.float32), neg_inf)
            attn = jax.nn.softmax(scores, axis=-1).astype(q.dtype)
            out = jnp.einsum('bhnrc,bhncd->bhnrd', attn, vc)
            return out.reshape(Bq, H, Tq, D)
        key = jax.random.key(seed)
        ks = jax.random.split(key, 11)
        f = jnp.float32
        return {'query': jax.random.normal(ks[0], (B, T, EMBED), f), 'key': jax.random.normal(ks[1], (B, T, EMBED), f), 'value': jax.random.normal(ks[2], (B, T, EMBED), f), 'wq': jax.random.normal(ks[3], (EMBED, EMBED), f) * 0.02, 'bq': jax.random.normal(ks[4], (EMBED,), f) * 0.02, 'wk': jax.random.normal(ks[5], (EMBED, EMBED), f) * 0.02, 'bk': jax.random.normal(ks[6], (EMBED,), f) * 0.02, 'wv': jax.random.normal(ks[7], (EMBED, EMBED), f) * 0.02, 'bv': jax.random.normal(ks[8], (EMBED,), f) * 0.02, 'wo': jax.random.normal(ks[9], (EMBED, EMBED), f) * 0.02, 'bo': jax.random.normal(ks[10], (EMBED,), f) * 0.02}
    _L0_xattn_all = _L0_xattn_setup()
    _L0_xattn_in = {k: v for k, v in _L0_xattn_all.items() if k in ('wq', 'bq', 'wk', 'bk', 'wv', 'bv', 'wo', 'bo')}
    del _L0_xattn_all

    def _L0_ffn_setup():
        import jax, jax.numpy as jnp
        import numpy as np
        B, S, D_MODEL, D_HIDDEN = (4, 256, 128, 512)

        def act_quant(x):
            scale = 127.0 / jnp.clip(jnp.max(jnp.abs(x), axis=-1, keepdims=True), 1e-05)
            return jnp.clip(jnp.round(x * scale), -128, 127) / scale

        def weight_quant(w):
            scale = 1.0 / jnp.clip(jnp.mean(jnp.abs(w)), 1e-05)
            return jnp.clip(jnp.round(w * scale), -1, 1) / scale

        def bit_linear(x, w):
            xq = x + jax.lax.stop_gradient(act_quant(x) - x)
            wq = w + jax.lax.stop_gradient(weight_quant(w) - w)
            return jnp.einsum('bsd,hd->bsh', xq, wq)

        def depthwise_conv1d(x_bcl, w, b):
            y = jax.lax.conv_general_dilated(x_bcl, w, window_strides=(1,), padding=[(1, 1)], dimension_numbers=('NCH', 'OIH', 'NCH'), feature_group_count=x_bcl.shape[1])
            return y + b[None, :, None]
        key = jax.random.key(seed)
        ks = jax.random.split(key, 5)
        lim1 = 1.0 / np.sqrt(D_MODEL)
        lim2 = 1.0 / np.sqrt(D_HIDDEN)
        limc = 1.0 / np.sqrt(3.0)
        return {'x': jax.random.normal(ks[0], (B, S, D_MODEL), dtype=jnp.float32), 'w1': jax.random.uniform(ks[1], (D_HIDDEN, D_MODEL), jnp.float32, -lim1, lim1), 'conv_w': jax.random.uniform(ks[2], (D_HIDDEN, 1, 3), jnp.float32, -limc, limc), 'conv_b': jax.random.uniform(ks[3], (D_HIDDEN,), jnp.float32, -limc, limc), 'w2': jax.random.uniform(ks[4], (D_MODEL, D_HIDDEN), jnp.float32, -lim2, lim2)}
    _L0_ffn_all = _L0_ffn_setup()
    _L0_ffn_in = {k: v for k, v in _L0_ffn_all.items() if k in ('w1', 'conv_w', 'conv_b', 'w2')}
    del _L0_ffn_all

    def _L1_xattn_setup():
        import jax, jax.numpy as jnp
        import numpy as np
        NUM_HEADS = 16
        HIDDEN_DIM = 64
        INPUT_DIM = 128
        key = jax.random.key(seed)
        ks = jax.random.split(key, 11)
        B, S = (4, 256)
        D, H = (INPUT_DIM, NUM_HEADS * HIDDEN_DIM)
        s_in = 1.0 / np.sqrt(D)
        s_out = 1.0 / np.sqrt(H)
        return {'query': jax.random.normal(ks[0], (B, S, D), jnp.float32), 'key': jax.random.normal(ks[1], (B, S, D), jnp.float32), 'value': jax.random.normal(ks[2], (B, S, D), jnp.float32), 'Wq': jax.random.uniform(ks[3], (D, H), jnp.float32, -s_in, s_in), 'bq': jax.random.uniform(ks[4], (H,), jnp.float32, -s_in, s_in), 'Wk': jax.random.uniform(ks[5], (D, H), jnp.float32, -s_in, s_in), 'bk': jax.random.uniform(ks[6], (H,), jnp.float32, -s_in, s_in), 'Wv': jax.random.uniform(ks[7], (D, H), jnp.float32, -s_in, s_in), 'bv': jax.random.uniform(ks[8], (H,), jnp.float32, -s_in, s_in), 'Wo': jax.random.uniform(ks[9], (H, D), jnp.float32, -s_out, s_out), 'bo': jax.random.uniform(ks[10], (D,), jnp.float32, -s_out, s_out)}
    _L1_xattn_all = _L1_xattn_setup()
    _L1_xattn_in = {k: v for k, v in _L1_xattn_all.items() if k in ('Wq', 'bq', 'Wk', 'bk', 'Wv', 'bv', 'Wo', 'bo')}
    del _L1_xattn_all

    def _L1_ffn_setup():
        import jax, jax.numpy as jnp
        import numpy as np
        H = 128
        M = 64
        E = 16
        TOP_K = 4
        N_GROUP = 4
        TOPK_GROUP = 2
        SCALE = 2.5
        B, S = (2, 128)

        def _gate(x2d, gate_kernel, gate_bias):
            n = x2d.shape[0]
            logits = jnp.dot(x2d.astype(jnp.float32), gate_kernel.astype(jnp.float32))
            scores = jax.nn.sigmoid(logits)
            scores_for_choice = scores + gate_bias
            group_scores = scores_for_choice.reshape(n, N_GROUP, E // N_GROUP)
            top2 = jax.lax.top_k(group_scores, k=2)[0]
            group_sum = jnp.sum(top2, axis=-1)
            group_idx = jax.lax.top_k(group_sum, k=TOPK_GROUP)[1]
            group_mask = jnp.zeros_like(group_sum).at[jnp.arange(n)[:, None], group_idx].set(1.0)
            score_mask = jnp.repeat(group_mask[:, :, None], E // N_GROUP, axis=2).reshape(n, E)
            masked_scores = jnp.where(score_mask > 0, scores_for_choice, 0.0)
            topk_weight, topk_idx = jax.lax.top_k(masked_scores, k=TOP_K)
            topk_weight = topk_weight / (jnp.sum(topk_weight, axis=-1, keepdims=True) + 1e-20)
            topk_weight = topk_weight * SCALE
            return (topk_idx, topk_weight)
        key = jax.random.key(seed)
        ks = jax.random.split(key, 9)
        sc_h = 1.0 / np.sqrt(H)
        sc_m = 1.0 / np.sqrt(M)
        return {'hidden_states': jax.random.normal(ks[0], (B, S, H), jnp.float32), 'gate_kernel': jax.random.normal(ks[1], (H, E), jnp.float32) * sc_h, 'gate_bias': jax.random.normal(ks[2], (E,), jnp.float32) * 0.01, 'w_gate': jax.random.normal(ks[3], (E, H, M), jnp.float32) * sc_h, 'w_up': jax.random.normal(ks[4], (E, H, M), jnp.float32) * sc_h, 'w_down': jax.random.normal(ks[5], (E, M, H), jnp.float32) * sc_m, 'sw_gate': jax.random.normal(ks[6], (H, 2 * M), jnp.float32) * sc_h, 'sw_up': jax.random.normal(ks[7], (H, 2 * M), jnp.float32) * sc_h, 'sw_down': jax.random.normal(ks[8], (2 * M, H), jnp.float32) * (1.0 / np.sqrt(2 * M))}
    _L1_ffn_all = _L1_ffn_setup()
    _L1_ffn_in = {k: v for k, v in _L1_ffn_all.items() if k in ('gate_kernel', 'gate_bias', 'w_gate', 'w_up', 'w_down', 'sw_gate', 'sw_up', 'sw_down')}
    del _L1_ffn_all
    return {'x': x, 'ctx_1024': ctx_1024, 'L0_xattn_wq': _L0_xattn_in['wq'], 'L0_xattn_bq': _L0_xattn_in['bq'], 'L0_xattn_wk': _L0_xattn_in['wk'], 'L0_xattn_bk': _L0_xattn_in['bk'], 'L0_xattn_wv': _L0_xattn_in['wv'], 'L0_xattn_bv': _L0_xattn_in['bv'], 'L0_xattn_wo': _L0_xattn_in['wo'], 'L0_xattn_bo': _L0_xattn_in['bo'], 'L0_ffn_w1': _L0_ffn_in['w1'], 'L0_ffn_conv_w': _L0_ffn_in['conv_w'], 'L0_ffn_conv_b': _L0_ffn_in['conv_b'], 'L0_ffn_w2': _L0_ffn_in['w2'], 'L1_xattn_Wq': _L1_xattn_in['Wq'], 'L1_xattn_bq': _L1_xattn_in['bq'], 'L1_xattn_Wk': _L1_xattn_in['Wk'], 'L1_xattn_bk': _L1_xattn_in['bk'], 'L1_xattn_Wv': _L1_xattn_in['Wv'], 'L1_xattn_bv': _L1_xattn_in['bv'], 'L1_xattn_Wo': _L1_xattn_in['Wo'], 'L1_xattn_bo': _L1_xattn_in['bo'], 'L1_ffn_gate_kernel': _L1_ffn_in['gate_kernel'], 'L1_ffn_gate_bias': _L1_ffn_in['gate_bias'], 'L1_ffn_w_gate': _L1_ffn_in['w_gate'], 'L1_ffn_w_up': _L1_ffn_in['w_up'], 'L1_ffn_w_down': _L1_ffn_in['w_down'], 'L1_ffn_sw_gate': _L1_ffn_in['sw_gate'], 'L1_ffn_sw_up': _L1_ffn_in['sw_up'], 'L1_ffn_sw_down': _L1_ffn_in['sw_down']}

def reference(x, ctx_1024, L0_xattn_wq, L0_xattn_bq, L0_xattn_wk, L0_xattn_bk, L0_xattn_wv, L0_xattn_bv, L0_xattn_wo, L0_xattn_bo, L0_ffn_w1, L0_ffn_conv_w, L0_ffn_conv_b, L0_ffn_w2, L1_xattn_Wq, L1_xattn_bq, L1_xattn_Wk, L1_xattn_bk, L1_xattn_Wv, L1_xattn_bv, L1_xattn_Wo, L1_xattn_bo, L1_ffn_gate_kernel, L1_ffn_gate_bias, L1_ffn_w_gate, L1_ffn_w_up, L1_ffn_w_down, L1_ffn_sw_gate, L1_ffn_sw_up, L1_ffn_sw_down):
    import jax
    import jax.numpy as jnp

    def _L0_xattn_ref(query, key, value, wq, bq, wk, bk, wv, bv, wo, bo):
        import jax, jax.numpy as jnp
        import numpy as np
        EMBED = 128
        HEADS = 16
        HEAD_DIM = EMBED // HEADS
        WINDOW = 128
        HALF = WINDOW // 2
        SCALE = HEAD_DIM ** (-0.5)
        B, T = (2, 512)

        def _sliding_window_attn(q, k, v):
            Bq, H, Tq, D = q.shape
            Bk = HALF
            nb = Tq // Bk
            qb = q.reshape(Bq, H, nb, Bk, D)

            def ctx(x):
                xb = x.reshape(Bq, H, nb, Bk, D)
                prev = jnp.concatenate([jnp.zeros_like(xb[:, :, :1]), xb[:, :, :-1]], axis=2)
                return jnp.concatenate([prev, xb], axis=3)
            kc, vc = (ctx(k), ctx(v))
            scores = jnp.einsum('bhnrd,bhncd->bhnrc', qb, kc)
            r = jnp.arange(Bk)[:, None]
            c = jnp.arange(2 * Bk)[None, :]
            band = (c >= r) & (c <= r + Bk)
            b_idx = jnp.arange(nb)[:, None, None]
            valid = band[None] & ((b_idx > 0) | (c[None] >= Bk))
            neg_inf = jnp.finfo(jnp.float32).min
            scores = jnp.where(valid[None, None], scores.astype(jnp.float32), neg_inf)
            attn = jax.nn.softmax(scores, axis=-1).astype(q.dtype)
            out = jnp.einsum('bhnrc,bhncd->bhnrd', attn, vc)
            return out.reshape(Bq, H, Tq, D)
        Bq, Tq, C = query.shape
        split = lambda x: x.reshape(Bq, Tq, HEADS, HEAD_DIM).transpose(0, 2, 1, 3)
        q = split(jnp.einsum('btc,oc->bto', query, wq) + bq) * SCALE
        k = split(jnp.einsum('btc,oc->bto', key, wk) + bk)
        v = split(jnp.einsum('btc,oc->bto', value, wv) + bv)
        o = _sliding_window_attn(q, k, v)
        o = o.transpose(0, 2, 1, 3).reshape(Bq, Tq, C)
        return jnp.einsum('btc,oc->bto', o, wo) + bo

    def _L0_ffn_ref(x, w1, conv_w, conv_b, w2):
        import jax, jax.numpy as jnp
        import numpy as np
        B, S, D_MODEL, D_HIDDEN = (4, 256, 128, 512)

        def act_quant(x):
            scale = 127.0 / jnp.clip(jnp.max(jnp.abs(x), axis=-1, keepdims=True), 1e-05)
            return jnp.clip(jnp.round(x * scale), -128, 127) / scale

        def weight_quant(w):
            scale = 1.0 / jnp.clip(jnp.mean(jnp.abs(w)), 1e-05)
            return jnp.clip(jnp.round(w * scale), -1, 1) / scale

        def bit_linear(x, w):
            xq = x + jax.lax.stop_gradient(act_quant(x) - x)
            wq = w + jax.lax.stop_gradient(weight_quant(w) - w)
            return jnp.einsum('bsd,hd->bsh', xq, wq)

        def depthwise_conv1d(x_bcl, w, b):
            y = jax.lax.conv_general_dilated(x_bcl, w, window_strides=(1,), padding=[(1, 1)], dimension_numbers=('NCH', 'OIH', 'NCH'), feature_group_count=x_bcl.shape[1])
            return y + b[None, :, None]
        h = bit_linear(x, w1)
        h = depthwise_conv1d(h.transpose(0, 2, 1), conv_w, conv_b)
        h = h.transpose(0, 2, 1)
        h = jax.nn.silu(h)
        return bit_linear(h, w2)

    def _L1_xattn_ref(query, key, value, Wq, bq, Wk, bk, Wv, bv, Wo, bo):
        import jax, jax.numpy as jnp
        import numpy as np
        NUM_HEADS = 16
        HIDDEN_DIM = 64
        INPUT_DIM = 128
        B, S, _ = query.shape
        h, d = (NUM_HEADS, HIDDEN_DIM)

        def proj(x, W, b):
            return (x @ W + b).reshape(B, -1, h, d).transpose(0, 2, 1, 3)
        q = proj(query, Wq, bq)
        k = proj(key, Wk, bk)
        v = proj(value, Wv, bv)
        scale = jnp.asarray(1.0 / np.sqrt(d), q.dtype)
        scores = jnp.einsum('bhqd,bhkd->bhqk', q, k) * scale
        attn_out = jnp.einsum('bhqk,bhkd->bhqd', scores, v)
        attn_out = attn_out.transpose(0, 2, 1, 3).reshape(B, S, h * d)
        return attn_out @ Wo + bo

    def _L1_ffn_ref(hidden_states, gate_kernel, gate_bias, w_gate, w_up, w_down, sw_gate, sw_up, sw_down):
        import jax, jax.numpy as jnp
        import numpy as np
        H = 128
        M = 64
        E = 16
        TOP_K = 4
        N_GROUP = 4
        TOPK_GROUP = 2
        SCALE = 2.5
        B, S = (2, 128)

        def _gate(x2d, gate_kernel, gate_bias):
            n = x2d.shape[0]
            logits = jnp.dot(x2d.astype(jnp.float32), gate_kernel.astype(jnp.float32))
            scores = jax.nn.sigmoid(logits)
            scores_for_choice = scores + gate_bias
            group_scores = scores_for_choice.reshape(n, N_GROUP, E // N_GROUP)
            top2 = jax.lax.top_k(group_scores, k=2)[0]
            group_sum = jnp.sum(top2, axis=-1)
            group_idx = jax.lax.top_k(group_sum, k=TOPK_GROUP)[1]
            group_mask = jnp.zeros_like(group_sum).at[jnp.arange(n)[:, None], group_idx].set(1.0)
            score_mask = jnp.repeat(group_mask[:, :, None], E // N_GROUP, axis=2).reshape(n, E)
            masked_scores = jnp.where(score_mask > 0, scores_for_choice, 0.0)
            topk_weight, topk_idx = jax.lax.top_k(masked_scores, k=TOP_K)
            topk_weight = topk_weight / (jnp.sum(topk_weight, axis=-1, keepdims=True) + 1e-20)
            topk_weight = topk_weight * SCALE
            return (topk_idx, topk_weight)
        orig_shape = hidden_states.shape
        x = hidden_states.reshape(-1, orig_shape[-1])
        topk_idx, topk_weight = _gate(x, gate_kernel, gate_bias)
        onehot = (topk_idx[:, :, None] == jnp.arange(E)[None, None, :]).astype(topk_weight.dtype)
        combine = jnp.einsum('nke,nk->ne', onehot, topk_weight)
        g = jnp.einsum('nh,ehm->enm', x, w_gate)
        u = jnp.einsum('nh,ehm->enm', x, w_up)
        inter = jax.nn.silu(g) * u
        y_e = jnp.einsum('enm,emh->enh', inter, w_down)
        y = jnp.einsum('ne,enh->nh', combine, y_e)
        shared = jnp.dot(jax.nn.silu(jnp.dot(x, sw_gate)) * jnp.dot(x, sw_up), sw_down)
        return (y + shared).reshape(orig_shape)
    x = x + _L0_xattn_ref(_layernorm(x, axis=-1), ctx_1024, ctx_1024, L0_xattn_wq, L0_xattn_bq, L0_xattn_wk, L0_xattn_bk, L0_xattn_wv, L0_xattn_bv, L0_xattn_wo, L0_xattn_bo)
    x = x + _L0_ffn_ref(_layernorm(x, axis=-1), L0_ffn_w1, L0_ffn_conv_w, L0_ffn_conv_b, L0_ffn_w2)
    x = x + _L1_xattn_ref(_layernorm(x, axis=-1), ctx_1024, ctx_1024, L1_xattn_Wq, L1_xattn_bq, L1_xattn_Wk, L1_xattn_bk, L1_xattn_Wv, L1_xattn_bv, L1_xattn_Wo, L1_xattn_bo)
    x = x + _L1_ffn_ref(_layernorm(x, axis=-1), L1_ffn_gate_kernel, L1_ffn_gate_bias, L1_ffn_w_gate, L1_ffn_w_up, L1_ffn_w_down, L1_ffn_sw_gate, L1_ffn_sw_up, L1_ffn_sw_down)
    return x

_drawn_inputs = setup_inputs


def setup_inputs(seed=0):
    import zlib

    import numpy as np

    out = dict(_drawn_inputs(seed))
    spreads = {}
    factors = {'L0_xattn_wq': 8.0,
     'L0_xattn_bq': 64.0,
     'L0_xattn_wk': 8.0,
     'L0_xattn_bk': 64.0,
     'L0_xattn_bv': 6.906,
     'L1_xattn_bo': 22.799,
     'L1_ffn_gate_bias': 3.752}
    for name, (base, spread) in spreads.items():
        noise = np.random.default_rng([zlib.crc32(name.encode()), seed]).standard_normal(out[name].shape)
        drawn = base * np.exp(spread * noise) if base else spread * noise
        out[name] = jnp.asarray(drawn.astype(out[name].dtype))
    for name, factor in factors.items():
        out[name] = (out[name] * factor).astype(out[name].dtype)
    return out
```

```python
from contextlib import ExitStack

import numpy as np
import concourse.bass as bass
from concourse import mybir

F32 = mybir.dt.float32
BF16 = mybir.dt.bfloat16
ALU = mybir.AluOpType
ACT = mybir.ActivationFunctionType
AX = mybir.AxisListType

P = 128
B, S = 8, 256
T = S // P
H0, D0 = 16, 8
WIN = 64
NB = S // WIN
KEYS = 2 * WIN
QT = 32
KT = WIN + QT
HG = 4
PARTS = 3
COMBOS = [(0, 0), (0, 1), (1, 0), (0, 2), (2, 0), (1, 1)]
ROWS = len(COMBOS) * D0
HC = 4
H1, D1 = 16, 64
C1 = H1 * D1 // P
E, M1 = 16, 64
EC = E * M1 // P
MC = EC + 1
TOPK, GROUPS, TOPG, GSCALE = 4, 4, 2, 2.5
EG = E // GROUPS
LN_EPS, Q_EPS = 1e-5, 1e-5
MAGIC = 1.5 * 2.0 ** 23
MASKED = -1e30
GONE = -1e30
PICKED = -2e30
SCALE0 = float(D0) ** -0.5
SCALE1 = float(D1) ** -0.5

INPUTS = ["x", "ctx", "ctxT", "wq", "bq", "wk", "bk", "wv", "bv", "wo", "bo",
          "w1", "cw", "cb", "w2", "Wq", "bq1", "Wk", "bk1", "Wv", "bv1", "Wo", "bo1",
          "gk", "gb", "mg", "mu", "md"]

COUNT = {"x_in": 16, "ctxT_in": 16, "ctx_in": 16, "qk_rows": 16 * 2 * len(COMBOS), "max_rows": 32, "out_st": 16,
         "xres": 1, "xnT_ps": 1, "xnT_sb": 1, "qk_ps": 1, "qk_sb": 4, "split_r": 1, "split_mid": 1, "parts": 1,
         "v_ps": 1, "v_sb": 1, "s_ps": 8, "rowmax": 8, "maxT_ps": 1, "max_hi": 1, "max_lo": 1,
         "st_ps": 8, "probs": 8, "pv_ps": NB, "rden": 1, "o_div": 1, "o_sb": 1, "op_ps": 1, "x1": 1,
         "q1_max": 1, "q1_clip": 1, "q1_rec": 1, "q1_s": 1, "q1_inv": 1, "q1_big": 2, "q1_int": 1, "q1T_ps": 1, "q1b_ps": 1,
         "q1T_sb": 1, "q1b_sb": 1, "h_ps": 2, "h_sb": 2, "c_mid": HC, "c_left": HC, "c_all": HC, "th": 1, "silu": 1,
         "hT_ps": 2, "q2_max": 2, "q2_clip": 1, "q2_rec": 1, "q2_s": 1, "q2_inv": 1, "q2b_ps": 1, "q2b_sb": 1,
         "q2_big": 1, "q2_int": 1, "f_ps": 1, "x2": 2, "x2res": 1,
         "g_ps": 1, "g_sb": 1, "p_ps": 4, "p_sb": 4, "u_slot": 1, "m_ps": 1, "m_sb": 1,
         "x3T_ps": 1, "x3T_sb": 1, "a_ps": 1, "x3": 1, "x4T_ps": 1, "x4T_sb": 1,
         "lg_ps": 1, "lg_th": 1, "gate": 22, "cT_ps": 1, "cT_sb": 1,
         "gu_ps": MC, "cb_ps": EC // 2, "g_th": MC, "m_a": MC, "m_b": MC, "m_c": EC, "y_ps": 1, "out_sb": 1}
for _p in ("l1", "l2", "l3", "l4"):
    COUNT.update({_p + "_st": T, _p + "_mv": T, _p + "_ve": 1, _p + "_rs": 1, _p + "_xn": T})


def layers_kernel(nc, a, out):
    ctx = ExitStack()
    with ctx:
        def sb(name, shape, dt=F32):
            return ctx.enter_context(nc.sbuf_tensor(name, shape, dt))

        def ps(name, shape, dt=F32):
            return ctx.enter_context(nc.psum_tensor(name, shape, dt))

        sem = {n: ctx.enter_context(nc.semaphore(n)) for n in COUNT}
        loaded = {n: ctx.enter_context(nc.semaphore("ld_" + n)) for n in ("l0", "ffn", "l1", "moe")}
        s_const = ctx.enter_context(nc.semaphore("s_const"))
        s_setv = ctx.enter_context(nc.semaphore("s_setv"))
        s_setp = ctx.enter_context(nc.semaphore("s_setp"))
        s_seta = ctx.enter_context(nc.semaphore("s_seta"))
        s_gate2 = ctx.enter_context(nc.semaphore("s_gate2"))
        s_rows = ctx.enter_context(nc.semaphore("s_rows"))

        def have(eng, name, b, k=None):
            n = COUNT[name]
            if isinstance(b, int):
                if b >= 0:
                    eng.wait_ge(sem[name], b * n + (n if k is None else k + 1))
            else:
                eng.wait_ge(sem[name], b * n + (n if k is None else k + 1))

        wq, wk, wv, wo = (sb(n, [P, P]) for n in ("wq_s", "wk_s", "wv_s", "wo_s"))
        bq, bk, bv = (sb(n, [P, 1]) for n in ("bq_s", "bk_s", "bv_s"))
        bqs = sb("bqs", [P, 1])
        bo, bo1 = sb("bo_s", [P, P]), sb("bo1_s", [P, P])
        w1, w2 = sb("w1_s", [P, HC * P]), sb("w2_s", [P, HC * P])
        w1q, w2q = sb("w1q", [P, HC * P], BF16), sb("w2q", [P, HC * P], BF16)
        wabs, wmean, wrec = sb("wabs", [P, 2]), sb("wmean", [P, 2]), sb("wrec", [P, 2])
        cw, cb = sb("cw_s", [P, HC, 3]), sb("cb_s", [P, HC])
        Wq, Wk, Wv, Wo = (sb(n, [P, C1, P]) for n in ("Wq_s", "Wk_s", "Wv_s", "Wo_s"))
        bq1, bk1, bv1 = (sb(n, [P, C1]) for n in ("bq1_s", "bk1_s", "bv1_s"))
        qsum, qshift = sb("qsum", [P, C1]), sb("qshift", [P, C1])
        bkd, bvd = sb("bkd", [P, C1, H1]), sb("bvd", [P, C1, H1])
        AT, BV = sb("AT", [P, H1, P]), sb("BV", [P, H1, P])
        csum = sb("csum", [P, B])
        uflat, pflat = sb("uflat", [B, H1 * P]), sb("pflat", [B, H1 * P])
        urow, prow = sb("urow", [H1, B, P]), sb("prow", [H1, B, P])
        arow, brow, brow_n = sb("arow", [H1, P]), sb("brow", [H1, P]), sb("brow_n", [H1, P])
        gk, gb = sb("gk_s", [P, E]), sb("gb_s", [P, E])
        mg, mu, md = (sb(n, [P, MC, P]) for n in ("mg_s", "mu_s", "md_s"))
        ident, identb, ones = sb("ident", [P, P]), sb("identb", [P, P], BF16), sb("ones", [P, P])
        mask_s = sb("mask_s", [P, T, KT], BF16)
        mask_t = sb("mask_t", [P, 2, WIN], BF16)
        denom = sb("denom", [P, HG, HG * D0])
        pick = sb("pick", [96, EC, 2, M1], BF16)
        mhalf = sb("mhalf", [P, T])
        repg, repe = sb("repg", [P, T, 8]), sb("repe", [P, T, 8])

        x_s = sb("x_s", [P, T, P])
        xres = sb("xres_s", [P, T, P])
        ctxT = sb("ctxT_s", [P, WIN + S])
        ctx_all = sb("ctx_all", [P, B, S])
        xn = {p: sb(p + "_xn_s", [P, T, P]) for p in ("l1", "l2", "l3", "l4")}
        lst = {p: sb(p + "_st_s", [P, T, 6]) for p in xn}
        lmv = {p: sb(p + "_mv_s", [P, T, 2]) for p in xn}
        lve = {p: sb(p + "_ve_s", [P, T]) for p in xn}
        lrs = {p: sb(p + "_rs_s", [P, T]) for p in xn}
        xnT = sb("xnT", [P, S])
        qk = sb("qk", [P, 2, S])
        rem = sb("rem", [P, 2, S])
        parts = sb("parts_s", [P, PARTS, 2, S], BF16)
        Q = sb("Q", [ROWS + 2, H0, S], BF16)
        K = sb("K", [ROWS + 2, H0, WIN + S], BF16)
        V = sb("V", [P, NB, H0 // HG, HG, HG * D0])
        mx = sb("mx", [P, H0, T])
        nhl = sb("nhl", [H0 * T, 2, P], BF16)
        PT = sb("PT", [P, 2, H0, WIN])
        rden = sb("rden_s", [P, S])
        oT = sb("oT", [P, S])
        x1 = sb("x1_s", [P, T, P])
        am1, cl1, rc1, s1, iv1 = (sb(n, [P, T]) for n in ("am1", "cl1", "rc1", "s1", "iv1"))
        big1 = sb("big1", [P, T, P])
        int1 = sb("int1", [P, T, P], BF16)
        q1T = sb("q1T", [P, S], BF16)
        q1b = sb("q1b", [P, S])
        hs = sb("hs", [P, HC, S + 2])
        hc = sb("hc", [P, HC, S])
        th = sb("th_s", [P, HC, S])
        am2, cl2, rc2, s2, iv2 = (sb(n, [P, T]) for n in ("am2", "cl2", "rc2", "s2", "iv2"))
        q2b = sb("q2b", [P, S])
        int2 = sb("int2", [P, HC, S], BF16)
        x2 = sb("x2_s", [P, T, P])
        x2res = sb("x2res_s", [P, T, P])
        ctxn = sb("ctxn", [P, T, P])
        G = sb("G", [P, P])
        PG = sb("PG", [P, H1, P])
        uslot = sb("uslot", [H1, P])
        M = sb("M", [P, P])
        x3T = sb("x3T", [P, S])
        x3 = sb("x3_s", [P, T, P])
        x4T = sb("x4T", [P, S])
        lth = sb("lth", [P, T, E])
        sg, sc = sb("sg", [P, T, E]), sb("sc", [P, T, E])
        pair_sum, pair_max = sb("pair_sum", [P, T * GROUPS, 2]), sb("pair_max", [P, T * GROUPS, 2])
        cross, same = sb("cross", [P, T * GROUPS]), sb("same", [P, T * GROUPS])
        gsum, gtop, gmark = sb("gsum", [P, T, 16]), sb("gtop", [P, T, 8]), sb("gmark", [P, T, 16])
        gsel = sb("gsel", [P, T, GROUPS])
        emask, etop, emark = sb("emask", [P, T, 32]), sb("etop", [P, T, 8]), sb("emark", [P, T, 32])
        tsum, trec, tnorm = sb("tsum", [P, T]), sb("trec", [P, T]), sb("tnorm", [P, T])
        wsel, comb, cr1, cr2 = (sb(n, [P, T, E]) for n in ("wsel", "comb", "cr1", "cr2"))
        cparts = sb("cparts", [P, T, PARTS, 32], BF16)
        cT = sb("cT", [96, S], BF16)
        gth = sb("gth", [P, 2, S])
        ga, gbuf = sb("ga", [P, 2, S]), sb("gbuf", [P, 2, S])
        inter = sb("inter", [P, MC, S])
        y = sb("y", [P, T, P])

        A = [ps(f"A{i}", [P, 512]) for i in range(2)]
        O = ps("O", [P, 2, S])
        F = [ps(f"F{i}", [P, 512]) for i in range(2)]
        MB = [ps(f"M{i}", [P, 512]) for i in range(3)]

        block = ctx.enter_context(nc.Block())

        L0_LOADS = [(wq, "wq"), (wk, "wk"), (bq, "bq"), (bk, "bk"), (wv, "wv"), (bv, "bv"), (wo, "wo")]
        FFN_LOADS = [(w1, "w1"), (w2, "w2"), (cw, "cw"), (cb, "cb")]
        L1_LOADS = [(Wq, "Wq"), (Wk, "Wk"), (bq1, "bq1"), (bk1, "bk1"), (Wv, "Wv"), (bv1, "bv1"), (Wo, "Wo")]
        MOE_LOADS = [(gk, "gk"), (mg, "mg"), (mu, "mu"), (md, "md")]
        N_L0 = 16 * (len(L0_LOADS) + 1)
        N_FFN = 16 * len(FFN_LOADS)
        N_L1 = 16 * (len(L1_LOADS) + 2)
        N_MOE = 16 * (len(MOE_LOADS) + 1)
        C_ALL = 36
        SV_WQ = 7 + C1
        SV_BD = SV_WQ + 5
        SV_ROWS = SV_BD + 17
        SV_END = SV_ROWS + 9

        @block.sync
        def _(sp):
            def load_x(b):
                have(sp, "xres", b - 1)
                have(sp, "l1_xn", b - 1)
                sp.dma_start(x_s[:, :, :], a["x"][b].rearrange("(t p) d -> p t d", p=P)).then_inc(sem["x_in"], 16)

            def load_ctxT(b):
                have(sp, "v_ps", b - 1)
                sp.dma_start(ctxT[:, WIN:], a["ctxT"][b]).then_inc(sem["ctxT_in"], 16)

            def load_ctx(b):
                have(sp, "g_ps", b - 1)
                sp.dma_start(ctxn[:, :, :], a["ctx"][b].rearrange("(t p) d -> p t d", p=P)).then_inc(sem["ctx_in"], 16)

            def spread_parts(b):
                have(sp, "parts", b)
                have(sp, "st_ps", b - 1)
                for c, (pq, pk) in enumerate(COMBOS):
                    sp.dma_start(Q[D0 * c:D0 * c + D0, :, :], parts[:, pq, 0, :]).then_inc(sem["qk_rows"], 16)
                    sp.dma_start(K[D0 * c:D0 * c + D0, :, WIN:], parts[:, pk, 1, :]).then_inc(sem["qk_rows"], 16)

            def spread_max(b):
                have(sp, "max_lo", b)
                for part in range(2):
                    sp.dma_start(Q[ROWS + part:ROWS + part + 1, :, :], nhl[:, part, :]).then_inc(sem["max_rows"], 16)

            def store(b):
                have(sp, "out_sb", b)
                sp.dma_start(out[b].rearrange("(t p) d -> p t d", p=P), y[:, :, :]).then_inc(sem["out_st"], 16)

            load_x(0)
            for t_, n in L0_LOADS:
                sp.dma_start(t_[tuple([slice(None)] * len(t_.shape))], a[n]).then_inc(loaded["l0"], 16)
            sp.dma_start(bo[:, :], a["bo"].partition_broadcast(P)).then_inc(loaded["l0"], 16)
            sp.wait_ge(s_const, 1)
            load_ctxT(0)
            load_ctx(0)
            for t_, n in FFN_LOADS:
                sp.dma_start(t_[tuple([slice(None)] * len(t_.shape))], a[n]).then_inc(loaded["ffn"], 16)
            for t_, n in L1_LOADS:
                sp.dma_start(t_[tuple([slice(None)] * len(t_.shape))], a[n]).then_inc(loaded["l1"], 16)
            sp.dma_start(bo1[:, :], a["bo1"].partition_broadcast(P)).then_inc(loaded["l1"], 16)
            sp.dma_start(ctx_all[:, :, :], a["ctxT"].rearrange("b p s -> p b s")).then_inc(loaded["l1"], 16)
            for t_, n in MOE_LOADS:
                sp.dma_start(t_[tuple([slice(None)] * len(t_.shape))], a[n]).then_inc(loaded["moe"], 16)
            sp.dma_start(gb[:, :], a["gb"].partition_broadcast(P)).then_inc(loaded["moe"], 16)
            sp.wait_ge(s_const, C_ALL)

            def regroup():
                sp.wait_ge(s_setv, SV_ROWS + 8)
                for src, dst in ((uflat, urow), (pflat, prow)):
                    for b_ in range(B):
                        sp.dma_start(dst[:, b_, :], src[b_:b_ + 1, :]).then_inc(s_rows, 16)

            def iteration(t, first, last):
                if not last:
                    spread_parts(t)
                    spread_max(t)
                if first:
                    regroup()
                if isinstance(t, int):
                    if t >= 2:
                        store(t - 2)
                    if t + 1 < B:
                        load_x(t + 1)
                        load_ctxT(t + 1)
                    if 1 <= t < B:
                        load_ctx(t)

            for t in range(B + 1):
                iteration(t, t == 0, t == B)
            store(B - 1)
            have(sp, "out_st", B - 1)

        @block.gpsimd
        def _(pool):
            done = [0]

            def step(ins):
                done[0] += 1
                ins.then_inc(s_const, 1)
                pool.wait_ge(s_const, done[0])

            step(pool.memset(ctxT[:, 0:WIN], 0.0))
            for m_ in (ident, identb):
                step(pool.memset(m_[:, :], 0.0))
                step(pool.affine_select(out=m_[:, :], in_=m_[:, :], compare_op=ALU.not_equal, fill=1.0, base=0,
                                        pattern=[[-1, P]], channel_multiplier=1))
            step(pool.memset(ones[:, :], 1.0))
            step(pool.memset(K[:, :, :], 0.0))
            step(pool.memset(K[32:ROWS + 2, :, :], 1.0))
            step(pool.memset(K[:, :, 0:WIN], 0.0))
            step(pool.memset(V[:, :, :, :, :], 0.0))
            step(pool.memset(denom[:, :, :], 0.0))
            own = denom[:, :, :].rearrange("p a b -> p (a b)")
            for h in range(HG):
                step(pool.memset(denom[:, h, D0 * h:D0 * h + D0], 1.0))
            step(pool.memset(mask_s[:, :, :], 0.0))
            step(pool.memset(mask_t[:, :, :], 0.0))
            for j in range(P // QT):
                m_ = mask_s[QT * j:QT * j + QT, :, :]
                step(pool.affine_select(out=m_, in_=m_, compare_op=ALU.is_ge, fill=MASKED, base=0,
                                        pattern=[[0, T], [1, KT]], channel_multiplier=-1))
                step(pool.affine_select(out=m_, in_=m_, compare_op=ALU.is_ge, fill=MASKED, base=WIN,
                                        pattern=[[0, T], [-1, KT]], channel_multiplier=1))
                if QT * j < WIN:
                    m_ = mask_s[QT * j:QT * j + QT, 0, :]
                    step(pool.affine_select(out=m_, in_=m_, compare_op=ALU.is_ge, fill=MASKED, base=QT * j - WIN,
                                            pattern=[[1, KT]], channel_multiplier=0))
            step(pool.affine_select(out=mask_t[:, :, :], in_=mask_t[:, :, :], compare_op=ALU.is_ge, fill=MASKED, base=0,
                                    pattern=[[0, 2], [-1, WIN]], channel_multiplier=1))
            step(pool.affine_select(out=mask_t[:, :, :], in_=mask_t[:, :, :], compare_op=ALU.is_ge, fill=MASKED,
                                    base=WIN, pattern=[[0, 2], [1, WIN]], channel_multiplier=-1))
            step(pool.affine_select(out=mask_t[:, 0, :], in_=mask_t[:, 0, :], compare_op=ALU.is_ge, fill=MASKED,
                                    base=-WIN, pattern=[[0, WIN]], channel_multiplier=1))
            step(pool.memset(pick[:, :, :, :], 1.0))
            for k in range(PARTS):
                m_ = pick[32 * k:32 * k + 32, :, :, :]
                step(pool.affine_select(out=m_, in_=m_, compare_op=ALU.is_equal, fill=0.0, base=0,
                                        pattern=[[-2, EC], [-1, 2], [0, M1]], channel_multiplier=1))
            step(pool.memset(mhalf[:, :], -0.5))
            step(pool.memset(cparts[:, :, :, :], 0.0))
            assert done[0] == C_ALL, done[0]

            def norm(p, b):
                have(pool, p + "_mv", b)
                pool.tensor_scalar(lve[p][:, :], lmv[p][:, :, 1], LN_EPS, None, ALU.add).then_inc(sem[p + "_ve"], 1)
                have(pool, p + "_ve", b)
                have(pool, p + "_xn", b - 1)
                pool.tensor_tensor(lrs[p][:, :], lve[p][:, :], mhalf[:, :], ALU.pow).then_inc(sem[p + "_rs"], 1)

            def residual(b):
                have(pool, "x_in", b)
                have(pool, "x1", b - 1)
                pool.tensor_tensor(xres[:, :, :], x_s[:, :, :], bo[:, None, :].broadcast_to([P, T, P]), ALU.add)\
                    .then_inc(sem["xres"], 1)

            def split(b):
                have(pool, "qk_sb", b)
                pool.tensor_tensor(rem[:, :, :], qk[:, :, :], parts[:, 0, :, :], ALU.subtract).then_inc(sem["split_r"], 1)
                have(pool, "split_r", b)
                have(pool, "qk_rows", b - 1)
                pool.tensor_copy(parts[:, 1, :, :], rem[:, :, :]).then_inc(sem["split_mid"], 1)
                have(pool, "split_mid", b)
                pool.tensor_tensor(parts[:, 2, :, :], rem[:, :, :], parts[:, 1, :, :], ALU.subtract)\
                    .then_inc(sem["parts"], 1)

            def residual2(b):
                have(pool, "x2", b)
                have(pool, "x3", b - 1)
                pool.tensor_tensor(x2res[:, :, :], x2[:, :, :], bo1[:, None, :].broadcast_to([P, T, P]), ALU.add)\
                    .then_inc(sem["x2res"], 1)

            pool.wait_ge(loaded["l0"], N_L0)
            for t in range(B + 1):
                if t < B:
                    norm("l1", t)
                    residual(t)
                    split(t)
                if t >= 1:
                    if t == 1:
                        pool.wait_ge(loaded["l1"], N_L1)
                    norm("l2", t - 1)
                    residual2(t - 1)
                    norm("l3", t - 1)
                    norm("l4", t - 1)

        @block.scalar
        def _(act):
            def evac(dst, src, after, name):
                return nc.scalar.activation(dst, src, ACT.Copy)

            def front(b):
                have(act, "xnT_ps", b)
                have(act, "qk_ps", b - 1)
                nc.scalar.activation(xnT[:, :], A[0][:, 0:S], ACT.Copy).then_inc(sem["xnT_sb"], 1)
                have(act, "qk_ps", b)
                have(act, "qk_rows", b - 1)
                for i, (bias, scale) in enumerate(((bqs, SCALE0), (bk, 1.0))):
                    nc.scalar.activation(qk[:, i, :], A[1][:, S * i:S * i + S], ACT.Identity, bias=bias[:, :],
                                         scale=scale).then_inc(sem["qk_sb"], 1)
                    nc.scalar.activation(parts[:, 0, i, :], A[1][:, S * i:S * i + S], ACT.Identity, bias=bias[:, :],
                                         scale=scale).then_inc(sem["qk_sb"], 1)

            def exps(b):
                for k in range(2 * NB):
                    n = k // 2
                    have(act, "st_ps", b, k)
                    have(act, "pv_ps", b, n - 2) if n >= 2 else have(act, "pv_ps", b - 1, n + 2)
                    nc.scalar.activation(PT[:, n % 2, 8 * (k % 2):8 * (k % 2) + 8, :].rearrange("p h q -> p (h q)"),
                                         A[k % 2][:, :], ACT.Exp).then_inc(sem["probs"], 1)

            def ffn_in(b):
                have(act, "q1T_ps", b)
                have(act, "h_ps", b - 1)
                nc.scalar.activation(q1T[:, :], F[0][:, 0:P].bitcast(BF16), ACT.Copy).then_inc(sem["q1T_sb"], 1)
                have(act, "q1b_ps", b)
                have(act, "h_sb", b - 1)
                nc.scalar.activation(q1b[:, :], F[1][:, 0:S], ACT.Copy).then_inc(sem["q1b_sb"], 1)

            def ffn_mid(b):
                for c in range(HC):
                    have(act, "h_sb", b, c // 2)
                    have(act, "hT_ps", b - 1)
                    have(act, "q2_big", b - 1)
                    nc.scalar.activation(hc[:, c, :], hs[:, c, 1:S + 1], ACT.Identity, bias=cb[:, c:c + 1],
                                         scale=cw[:, c, 1:2]).then_inc(sem["c_mid"], 1)
                have(act, "c_all", b)
                have(act, "q2_int", b - 1)
                nc.scalar.activation(th[:, :, :], hc[:, :, :], ACT.Tanh, scale=0.5).then_inc(sem["th"], 1)

            def ffn_out(b):
                have(act, "q2b_ps", b)
                have(act, "q2_big", b - 1)
                nc.scalar.activation(q2b[:, :], F[0][:, 0:S], ACT.Copy).then_inc(sem["q2b_sb"], 1)

            def gram(b):
                have(act, "g_ps", b)
                have(act, "p_ps", b - 1)
                nc.scalar.activation(G[:, :], MB[0][:, 0:P], ACT.Copy).then_inc(sem["g_sb"], 1)
                for k in range(4):
                    have(act, "p_ps", b, k)
                    have(act, "m_ps", b - 1)
                    nc.scalar.activation(PG[:, 4 * k:4 * k + 4, :].rearrange("p h j -> p (h j)"), MB[1 + k % 2][:, :],
                                         ACT.Copy).then_inc(sem["p_sb"], 1)

            def layer1(b):
                have(act, "x3T_ps", b)
                have(act, "a_ps", b - 1)
                nc.scalar.activation(x3T[:, :], MB[1][:, 0:S], ACT.Copy, bias=1.0).then_inc(sem["x3T_sb"], 1)
                have(act, "x4T_ps", b)
                have(act, "gu_ps", b - 1)
                nc.scalar.activation(x4T[:, :], MB[0][:, 0:S], ACT.Copy).then_inc(sem["x4T_sb"], 1)
                have(act, "lg_ps", b)
                have(act, "gate", b - 1)
                nc.scalar.activation(lth[:, :, :].rearrange("p t e -> p (t e)"), MB[1][:, 0:T * E], ACT.Tanh,
                                     scale=0.5).then_inc(sem["lg_th"], 1)
                have(act, "cT_ps", b)
                have(act, "cb_ps", b - 1)
                nc.scalar.activation(cT[:, :], MB[2][0:96, 0:P].bitcast(BF16), ACT.Copy).then_inc(sem["cT_sb"], 1)
                for c in range(MC):
                    have(act, "gu_ps", b, c)
                    have(act, "m_a", b, c - 2) if c >= 2 else have(act, "m_a", b - 1)
                    nc.scalar.activation(gth[:, c % 2, :], MB[c % 2][:, 0:S], ACT.Tanh, scale=0.5)\
                        .then_inc(sem["g_th"], 1)

            act.wait_ge(loaded["l0"], N_L0)
            nc.scalar.activation(bqs[:, :], bq[:, :], ACT.Copy, scale=SCALE0).then_inc(s_seta, 1)
            act.wait_ge(s_seta, 1)

            def setup():
                for k in range(8):
                    r, odd = k // 2, k % 2
                    act.wait_ge(s_setp, 2 + r)
                    dst = (AT if r < 2 else BV)[:, 8 * (r % 2) + odd:8 * (r % 2) + 8:2, :]
                    nc.scalar.activation(dst, MB[odd][:, :].rearrange("p (h j) -> p h j", j=P), ACT.Copy, scale=SCALE1 if k < 4 else 1.0)\
                        .then_inc(s_seta, 1)

            for t in range(B + 1):
                if t < B:
                    front(t)
                if t == 0:
                    setup()
                if t >= 1:
                    gram(t - 1)
                    ffn_in(t - 1)
                if t < B:
                    exps(t)
                if t >= 1:
                    ffn_mid(t - 1)
                    ffn_out(t - 1)
                    layer1(t - 1)

        @block.tensor
        def _(pe):
            def front(b):
                have(pe, "l1_xn", b)
                have(pe, "x1", b - 1)
                for t in range(T):
                    last = pe.transpose(A[0][:, P * t:P * t + P], xn["l1"][:, t, :], ident[:, :])
                last.then_inc(sem["xnT_ps"], 1)
                have(pe, "xnT_sb", b)
                have(pe, "ctxT_in", b)
                have(pe, "probs", b - 1)
                pe.matmul(A[1][:, 0:S], wq[:, :], xnT[:, :], start=True, stop=True)
                pe.matmul(A[1][:, S:2 * S], wk[:, :], ctxT[:, WIN:], start=True, stop=True).then_inc(sem["qk_ps"], 1)
                for n in range(NB):
                    last = pe.matmul(A[0][:, P * n:P * n + P], ctxT[:, WIN * n:WIN * n + KEYS], wv[:, :],
                                     start=True, stop=True)
                last.then_inc(sem["v_ps"], 1)

            def row_scores(b):
                have(pe, "qk_rows", b)
                for k in range(8):
                    t, hg = k // 4, k % 4
                    bank = A[(k + 1) % 2]
                    if k == 0:
                        have(pe, "qk_sb", b)
                    elif k == 1:
                        have(pe, "v_sb", b)
                    else:
                        have(pe, "rowmax", b, k - 2)
                    pe.matmul(bank[:, 0:HG * KT], identb[:, :], mask_s[:, t:t + 1, :].broadcast_to([P, HG, KT]),
                              start=True, stop=False, skip_group_check=True)
                    for h in range(HG):
                        for j in range(P // QT):
                            q0 = P * t + QT * j
                            last = pe.matmul(bank[QT * j:QT * j + QT, KT * h:KT * h + KT],
                                             Q[0:ROWS, HG * hg + h, q0:q0 + QT], K[0:ROWS, HG * hg + h, q0:q0 + KT],
                                             start=False, stop=(h == HG - 1), skip_group_check=True)
                    last.then_inc(sem["s_ps"], 1)

            def max_rows(b):
                have(pe, "rowmax", b)
                pe.transpose(A[1][0:H0 * T, 0:P], mx[:, :, :].rearrange("p h t -> p (h t)"), ident[:, :])\
                    .then_inc(sem["maxT_ps"], 1)

            def key_scores(b, k):
                n, half = k // 2, k % 2
                if k == 0:
                    have(pe, "max_rows", b)
                if k == 1:
                    have(pe, "max_lo", b)
                if k >= 2:
                    have(pe, "probs", b, k - 2)
                bank = A[k % 2]
                pe.matmul(bank[:, :], identb[:, :], mask_t[:, min(n, 1):min(n, 1) + 1, :].broadcast_to([P, 8, WIN]),
                          start=True, stop=False, skip_group_check=True)
                for h in range(8):
                    last = pe.matmul(bank[:, WIN * h:WIN * h + WIN], K[:, 8 * half + h, WIN * n:WIN * n + KEYS],
                                     Q[:, 8 * half + h, WIN * n:WIN * n + WIN], start=False, stop=(h == 7),
                                     skip_group_check=True)
                last.then_inc(sem["st_ps"], 1)

            def values(b, n):
                have(pe, "probs", b, 2 * n + 1)
                if n == 0:
                    have(pe, "v_sb", b)
                    have(pe, "o_div", b - 1)
                for what in range(2):
                    for h in range(HG):
                        for g in range(H0 // HG):
                            w = V[:, n, g, h, :] if what == 0 else denom[:, h, :]
                            last = pe.matmul(O[32 * g:32 * g + 32, what, WIN * n:WIN * n + WIN], w,
                                             PT[:, n % 2, HG * g + h, :], start=(h == 0), stop=(h == HG - 1),
                                             skip_group_check=True)
                last.then_inc(sem["pv_ps"], 1)

            def out_proj(b):
                have(pe, "o_sb", b)
                have(pe, "probs", b)
                for t in range(T):
                    last = pe.matmul(A[0][:, P * t:P * t + P], oT[:, P * t:P * t + P], wo[:, :], start=True, stop=True)
                last.then_inc(sem["op_ps"], 1)

            def ffn_in(b):
                have(pe, "q1_int", b)
                have(pe, "q2b_sb", b - 1)
                for t in range(T):
                    last = pe.transpose(F[0][:, 0:P].bitcast(BF16)[:, P * t:P * t + P], int1[:, t, :], identb[:, :])
                last.then_inc(sem["q1T_ps"], 1)
                have(pe, "q1_inv", b)
                have(pe, "x2", b - 1)
                for t in range(T):
                    last = pe.matmul(F[1][:, P * t:P * t + P], iv1[:, t:t + 1].broadcast_to([P, P]), ident[:, :],
                                     start=True, stop=True)
                last.then_inc(sem["q1b_ps"], 1)

            def ffn_up(b):
                have(pe, "q1T_sb", b)
                for f in range(2):
                    if f == 1:
                        have(pe, "q1b_sb", b)
                    for i in range(2):
                        c = 2 * f + i
                        last = pe.matmul(F[f][:, S * i:S * i + S], w1q[:, P * c:P * c + P], q1T[:, :],
                                         start=True, stop=True)
                    last.then_inc(sem["h_ps"], 1)

            def ffn_turn(b):
                have(pe, "silu", b)
                for t in range(T):
                    have(pe, "h_sb", b, t)
                    for c in range(HC):
                        last = pe.transpose(F[t][:, P * c:P * c + P], hc[:, c, P * t:P * t + P], ident[:, :])
                    last.then_inc(sem["hT_ps"], 1)

            def ffn_scale(b):
                have(pe, "q2_s", b)
                have(pe, "q2_max", b, 0)
                for t in range(T):
                    last = pe.matmul(F[0][:, P * t:P * t + P], s2[:, t:t + 1].broadcast_to([P, P]), ident[:, :],
                                     start=True, stop=True)
                last.then_inc(sem["q2b_ps"], 1)

            def ffn_down(b):
                have(pe, "q2_int", b)
                have(pe, "q2_max", b)
                for t in range(T):
                    for c in range(HC):
                        last = pe.matmul(F[1][:, P * t:P * t + P], int2[:, c, P * t:P * t + P], w2q[:, P * c:P * c + P],
                                         start=(c == 0), stop=(c == HC - 1), skip_group_check=True)
                last.then_inc(sem["f_ps"], 1)

            def gram(b):
                have(pe, "ctx_in", b)
                have(pe, "g_th", b - 1)
                have(pe, "out_sb", b - 1)
                have(pe, "m_b", b - 1)
                for t in range(T):
                    last = pe.matmul(MB[0][:, 0:P], ctxn[:, t, :], ctxn[:, t, :], start=(t == 0), stop=(t == T - 1))
                last.then_inc(sem["g_ps"], 1)
                have(pe, "g_sb", b)
                for k in range(4):
                    if k >= 2:
                        have(pe, "p_sb", b, k - 2)
                    else:
                        have(pe, "out_sb", b - 1)
                        have(pe, "m_c", b - 1)
                    pe.matmul(MB[1 + k % 2][:, :], G[:, :], BV[:, 4 * k:4 * k + 4, :], start=True, stop=True)\
                        .then_inc(sem["p_ps"], 1)

            def mix(b):
                have(pe, "p_sb", b)
                have(pe, "u_slot", b)
                for h in range(H1):
                    pe.matmul(MB[0][:, 0:P], AT[:, h, :], PG[:, h, :], start=(h == 0), stop=False)
                pe.matmul(MB[0][:, 0:P], uslot[:, :], brow[:, :], start=False, stop=False)
                pe.matmul(MB[0][:, 0:P], arow[:, :], prow[:, b, :], start=False, stop=True).then_inc(sem["m_ps"], 1)

            def attend(b):
                have(pe, "l3_xn", b)
                have(pe, "m_sb", b)
                for t in range(T):
                    last = pe.transpose(MB[1][:, P * t:P * t + P], xn["l3"][:, t, :], ident[:, :])
                last.then_inc(sem["x3T_ps"], 1)
                have(pe, "x3T_sb", b)
                for t in range(T):
                    last = pe.matmul(MB[2][:, P * t:P * t + P], x3T[:, P * t:P * t + P], M[:, :], start=True, stop=True)
                last.then_inc(sem["a_ps"], 1)

            def route(b):
                have(pe, "l4_xn", b)
                for t in range(T):
                    last = pe.transpose(MB[0][:, P * t:P * t + P], xn["l4"][:, t, :], ident[:, :])
                last.then_inc(sem["x4T_ps"], 1)
                have(pe, "x4T_sb", b)
                for t in range(T):
                    last = pe.matmul(MB[1][:, E * t:E * t + E], x4T[:, P * t:P * t + P], gk[:, :], start=True, stop=True)
                last.then_inc(sem["lg_ps"], 1)

            def gate_up(b, c):
                if c == 1:
                    have(pe, "lg_th", b)
                if c >= 2:
                    have(pe, "m_b", b, c - 2)
                pe.matmul(MB[c % 2][:, 0:S], mg[:, c, :], x4T[:, :], start=True, stop=True)
                pe.matmul(MB[c % 2][:, S:2 * S], mu[:, c, :], x4T[:, :], start=True, stop=True)\
                    .then_inc(sem["gu_ps"], 1)

            def combine(b, k):
                if k == 0:
                    have(pe, "gate", b)
                    for t in range(T):
                        last = pe.transpose(MB[2][0:96, 0:P].bitcast(BF16)[:, P * t:P * t + P],
                                            cparts[:, t, :, :].rearrange("p k e -> p (k e)"), identb[:, :])
                    last.then_inc(sem["cT_ps"], 1)
                    have(pe, "cT_sb", b)
                else:
                    have(pe, "m_c", b, 2 * k - 1)
                for i in range(2):
                    last = pe.matmul(MB[2][:, S * i:S * i + S], pick[:, 2 * k + i, :, :].rearrange("p a m -> p (a m)"),
                                     cT[:, :], start=True, stop=True)
                last.then_inc(sem["cb_ps"], 1)

            def down(b):
                have(pe, "m_c", b)
                for t in range(T):
                    for c in range(MC):
                        if t == 0:
                            if c == EC:
                                have(pe, "m_b", b)
                        last = pe.matmul(MB[1][:, P * t:P * t + P], inter[:, c, P * t:P * t + P], md[:, c, :],
                                         start=(c == 0), stop=(c == MC - 1))
                last.then_inc(sem["y_ps"], 1)

            pe.wait_ge(s_const, C_ALL)
            pe.wait_ge(loaded["l0"], N_L0)

            def setup():
                pe.wait_ge(s_setv, 2)
                pe.matmul(F[0][:, 0:2], ones[:, :], wabs[:, :], start=True, stop=True).then_inc(s_setp, 1)
                pe.wait_ge(loaded["l1"], N_L1)
                pe.wait_ge(s_setv, SV_WQ)
                for k in range(4):
                    lhs, rhs = (Wk, Wq) if k < 2 else (Wv, Wo)
                    if k >= 1:
                        pe.wait_ge(s_seta, 1 + 2 * k)
                    for i in range(4):
                        c = 4 * (k % 2) + i
                        for odd in range(2):
                            p0 = D1 * odd
                            last = pe.matmul(MB[odd][:, P * i:P * i + P], lhs[p0:p0 + D1, c, :], rhs[p0:p0 + D1, c, :],
                                             start=True, stop=True, skip_group_check=True)
                    last.then_inc(s_setp, 1)
                pe.wait_ge(s_setv, SV_BD)
                for i, (d_, w_) in enumerate(((bkd, Wq), (bvd, Wo))):
                    for c in range(C1):
                        last = pe.matmul(MB[2][0:H1, P * i:P * i + P], d_[:, c, :], w_[:, c, :], start=(c == 0),
                                         stop=(c == C1 - 1))
                last.then_inc(s_setp, 1)
                pe.wait_ge(s_seta, 9)
                for k in range(8):
                    src = AT if k < 4 else BV
                    bank = MB[k % 2]
                    if k >= 2:
                        pe.wait_ge(s_setv, SV_ROWS + k - 1)
                    pe.matmul(bank[0:B, :], csum[:, :], src[:, 4 * (k % 4):4 * (k % 4) + 4, :], start=True, stop=True)\
                        .then_inc(s_setp, 1)
                pe.wait_ge(s_setv, SV_ROWS + 8)

            for t in range(B + 1):
                if t < B:
                    front(t)
                if t == 0:
                    setup()
                if t < B:
                    row_scores(t)
                if t >= 1:
                    gram(t - 1)
                if t < B:
                    max_rows(t)
                if t >= 1:
                    mix(t - 1)
                    ffn_in(t - 1)
                    ffn_up(t - 1)
                if t < B:
                    for k in range(2):
                        key_scores(t, k)
                    for n in range(NB):
                        if n + 1 < NB:
                            key_scores(t, 2 * n + 2)
                            key_scores(t, 2 * n + 3)
                        values(t, n)
                if t >= 1:
                    ffn_turn(t - 1)
                if t < B:
                    out_proj(t)
                if t >= 1:
                    ffn_scale(t - 1)
                    ffn_down(t - 1)
                    attend(t - 1)
                    route(t - 1)
                    gate_up(t - 1, 0)
                    gate_up(t - 1, 1)
                    combine(t - 1, 0)
                    for c in range(2, MC):
                        gate_up(t - 1, c)
                        if c % 2 == 1 and c // 2 < EC // 2:
                            combine(t - 1, c // 2)
                    down(t - 1)

        @block.vector
        def _(dve):
            v = nc.vector
            setv = [0]

            def step(ins):
                setv[0] += 1
                ins.then_inc(s_setv, 1)

            def norm_stats(p, src, b):
                for t in range(T):
                    v.bn_stats(lst[p][:, t, :], src[:, t, :]).then_inc(sem[p + "_st"], 1)
                for t in range(T):
                    have(dve, p + "_st", b, t)
                    v.bn_aggr(lmv[p][:, t, :], lst[p][:, t, :]).then_inc(sem[p + "_mv"], 1)

            def norm_apply(p, src, b):
                have(dve, p + "_rs", b)
                for t in range(T):
                    v.tensor_scalar(xn[p][:, t, :], src[:, t, :], lmv[p][:, t, 0:1], lrs[p][:, t:t + 1],
                                    ALU.subtract, ALU.mult).then_inc(sem[p + "_xn"], 1)

            def front(b):
                have(dve, "x_in", b)
                norm_stats("l1", x_s, b)
                have(dve, "xnT_ps", b - 1)
                norm_apply("l1", x_s, b)

            def values_in(b):
                have(dve, "v_ps", b)
                have(dve, "pv_ps", b - 1)
                src = A[0][:, :].rearrange("p (w h d) -> p w h d", h=HG, d=D0)
                dst = V[:, :, :, :, :].rearrange("p n g h c -> p (n g) (h c)")
                for h in range(HG):
                    ins = v.tensor_copy(dst[:, :, (HG * D0 + D0) * h:(HG * D0 + D0) * h + D0], src[:, :, h, :])
                ins.then_inc(sem["v_sb"], 1)

            def row_max(b, k):
                t, hg = k // 4, k % 4
                have(dve, "s_ps", b, k)
                if k == 0:
                    have(dve, "maxT_ps", b - 1)
                v.tensor_reduce(mx[:, HG * hg:HG * hg + HG, t], A[(k + 1) % 2][:, 0:HG * KT]
                                .rearrange("p (h c) -> p h c", c=KT), AX.X, ALU.max).then_inc(sem["rowmax"], 1)

            def max_parts(b):
                have(dve, "maxT_ps", b)
                have(dve, "max_rows", b - 1)
                v.tensor_scalar(nhl[:, 0, :], A[1][0:H0 * T, 0:P], -1.0, None, ALU.mult).then_inc(sem["max_hi"], 1)
                have(dve, "max_hi", b)
                v.scalar_tensor_tensor(out=nhl[:, 1, :], in0=A[1][0:H0 * T, 0:P], scalar=-1.0, in1=nhl[:, 0, :],
                                       op0=ALU.mult, op1=ALU.subtract).then_inc(sem["max_lo"], 1)

            def attn_out(b):
                have(dve, "pv_ps", b)
                v.reciprocal(rden[:, :], O[:, 1, :]).then_inc(sem["rden"], 1)
                have(dve, "rden", b)
                have(dve, "op_ps", b - 1)
                v.tensor_tensor(oT[:, :], O[:, 0, :], rden[:, :], ALU.mult).then_inc(sem["o_div"], 1)
                have(dve, "o_div", b)
                v.tensor_scalar(oT[:, :], oT[:, :], bv[:, 0:1], None, ALU.add).then_inc(sem["o_sb"], 1)

            def add1(b):
                have(dve, "op_ps", b)
                have(dve, "xres", b)
                have(dve, "x2", b - 1)
                v.tensor_tensor(x1[:, :, :], A[0][:, 0:S].rearrange("p (t d) -> p t d", t=T), xres[:, :, :], ALU.add)\
                    .then_inc(sem["x1"], 1)

            def ffn_quant(b):
                have(dve, "x1", b)
                norm_stats("l2", x1, b)
                norm_apply("l2", x1, b)
                have(dve, "l2_xn", b)
                v.tensor_reduce(am1[:, :], xn["l2"][:, :, :], AX.X, ALU.max, apply_absolute_value=True)\
                    .then_inc(sem["q1_max"], 1)
                have(dve, "q1_max", b)
                v.tensor_scalar(cl1[:, :], am1[:, :], Q_EPS, None, ALU.max).then_inc(sem["q1_clip"], 1)
                have(dve, "q1_clip", b)
                v.reciprocal(rc1[:, :], cl1[:, :]).then_inc(sem["q1_rec"], 1)
                have(dve, "q1b_ps", b - 1)
                v.tensor_scalar(iv1[:, :], cl1[:, :], 1.0 / 127, wmean[:, 0:1], ALU.mult, ALU.mult)\
                    .then_inc(sem["q1_inv"], 1)
                have(dve, "q1_rec", b)
                v.tensor_scalar(s1[:, :], rc1[:, :], 127.0, None, ALU.mult).then_inc(sem["q1_s"], 1)
                have(dve, "q1_s", b)
                for t in range(T):
                    v.tensor_scalar(big1[:, t, :], xn["l2"][:, t, :], s1[:, t:t + 1], MAGIC, ALU.mult, ALU.add)\
                        .then_inc(sem["q1_big"], 1)
                have(dve, "q1_big", b)
                have(dve, "q1T_ps", b - 1)
                v.tensor_scalar(int1[:, :, :], big1[:, :, :], MAGIC, 127.0, ALU.subtract, ALU.min)\
                    .then_inc(sem["q1_int"], 1)

            def ffn_conv(b):
                have(dve, "q1b_sb", b)
                have(dve, "c_all", b - 1)
                for f in range(2):
                    have(dve, "h_ps", b, f)
                    v.tensor_tensor(hs[:, 2 * f:2 * f + 2, 1:S + 1], F[f][:, :].rearrange("p (c s) -> p c s", c=2),
                                    q1b[:, None, :].broadcast_to([P, 2, S]), ALU.mult).then_inc(sem["h_sb"], 1)
                for c in range(HC):
                    have(dve, "c_mid", b, c)
                    v.scalar_tensor_tensor(out=hc[:, c, :], in0=hs[:, c, 0:S], scalar=cw[:, c, 0:1], in1=hc[:, c, :],
                                           op0=ALU.mult, op1=ALU.add).then_inc(sem["c_left"], 1)
                for c in range(HC):
                    have(dve, "c_left", b, c)
                    v.scalar_tensor_tensor(out=hc[:, c, :], in0=hs[:, c, 2:S + 2], scalar=cw[:, c, 2:3],
                                           in1=hc[:, c, :], op0=ALU.mult, op1=ALU.add).then_inc(sem["c_all"], 1)

            def ffn_silu(b):
                have(dve, "th", b)
                v.scalar_tensor_tensor(out=hc[:, :, :], in0=th[:, :, :], scalar=1.0, in1=hc[:, :, :], op0=ALU.add,
                                       op1=ALU.mult).then_inc(sem["silu"], 1)

            def ffn_quant2(b):
                for t in range(T):
                    have(dve, "hT_ps", b, t)
                    v.tensor_reduce(am2[:, t:t + 1], F[t][:, :], AX.X, ALU.max, apply_absolute_value=True)\
                        .then_inc(sem["q2_max"], 1)
                have(dve, "q2_max", b)
                v.tensor_scalar(cl2[:, :], am2[:, :], 2 * Q_EPS, None, ALU.max).then_inc(sem["q2_clip"], 1)
                have(dve, "q2_clip", b)
                v.reciprocal(rc2[:, :], cl2[:, :]).then_inc(sem["q2_rec"], 1)
                v.tensor_scalar(iv2[:, :], cl2[:, :], 0.5 / 127, wmean[:, 1:2], ALU.mult, ALU.mult)\
                    .then_inc(sem["q2_inv"], 1)
                have(dve, "q2_rec", b)
                have(dve, "q2b_ps", b - 1)
                v.tensor_scalar(s2[:, :], rc2[:, :], 127.0, None, ALU.mult).then_inc(sem["q2_s"], 1)

            def ffn_round2(b):
                have(dve, "q2b_sb", b)
                v.tensor_tensor(th[:, :, :], hc[:, :, :], q2b[:, None, :].broadcast_to([P, HC, S]), ALU.mult)\
                    .then_inc(sem["q2_big"], 1)
                have(dve, "q2_big", b)
                have(dve, "f_ps", b - 1)
                v.tensor_scalar(int2[:, :, :], th[:, :, :], MAGIC, MAGIC, ALU.add, ALU.subtract)\
                    .then_inc(sem["q2_int"], 1)

            def add2(b):
                have(dve, "f_ps", b)
                have(dve, "q2_inv", b)
                have(dve, "x2res", b - 1)
                for t in range(T):
                    v.scalar_tensor_tensor(out=x2[:, t, :], in0=F[1][:, P * t:P * t + P], scalar=iv2[:, t:t + 1],
                                           in1=x1[:, t, :], op0=ALU.mult, op1=ALU.add).then_inc(sem["x2"], 1)

            def mix_in(b):
                have(dve, "m_ps", b - 1)
                v.tensor_copy(uslot[:, :], urow[:, b, :]).then_inc(sem["u_slot"], 1)

            def mix_out(b):
                have(dve, "m_ps", b)
                have(dve, "a_ps", b - 1)
                v.tensor_copy(M[:, :], MB[0][:, 0:P]).then_inc(sem["m_sb"], 1)

            def attend(b):
                have(dve, "x2", b)
                norm_stats("l3", x2, b)
                norm_apply("l3", x2, b)
                have(dve, "a_ps", b)
                have(dve, "x2res", b)
                v.tensor_tensor(x3[:, :, :], MB[2][:, 0:S].rearrange("p (t d) -> p t d", t=T), x2res[:, :, :], ALU.add)\
                    .then_inc(sem["x3"], 1)
                have(dve, "x3", b)
                norm_stats("l4", x3, b)
                norm_apply("l4", x3, b)

            def route(b):
                n = [0]

                def link(ins, wait=True):
                    ins.then_inc(sem["gate"], 1)
                    n[0] += 1
                    if wait and n[0] < COUNT["gate"]:
                        have(dve, "gate", b, n[0] - 1)

                have(dve, "lg_th", b)
                link(v.tensor_scalar(sg[:, :, :], lth[:, :, :], 0.5, 0.5, ALU.mult, ALU.add))
                link(v.tensor_tensor(sc[:, :, :], sg[:, :, :], gb[:, None, :].broadcast_to([P, T, E]), ALU.add))
                pairs = sc[:, :, :].rearrange("p t (g a b) -> p (t g) a b", g=GROUPS, b=2)
                link(v.tensor_tensor(pair_sum[:, :, :], pairs[:, :, :, 0], pairs[:, :, :, 1], ALU.add), False)
                link(v.tensor_tensor(pair_max[:, :, :], pairs[:, :, :, 0], pairs[:, :, :, 1], ALU.max))
                link(v.tensor_tensor(cross[:, :], pair_max[:, :, 0], pair_max[:, :, 1], ALU.add), False)
                link(v.tensor_tensor(same[:, :], pair_sum[:, :, 0], pair_sum[:, :, 1], ALU.max))
                link(v.tensor_tensor(gsum[:, :, 0:GROUPS], cross[:, :].rearrange("p (t g) -> p t g", t=T),
                                     same[:, :].rearrange("p (t g) -> p t g", t=T), ALU.max))
                for t in range(T):
                    ins = v.max(gtop[:, t, :], gsum[:, t, :])
                link(ins)
                link(v.tensor_copy(repg[:, :, 0:TOPG], gtop[:, :, 0:TOPG]))
                for t in range(T):
                    ins = v.match_replace(gmark[:, t, :], repg[:, t, :], gsum[:, t, :], PICKED)
                link(ins)
                link(v.tensor_scalar(gsel[:, :, :], gmark[:, :, 0:GROUPS], PICKED, None, ALU.is_equal))
                for t in range(T):
                    ins = v.tensor_tensor(emask[:, t, 0:E].rearrange("p (g e) -> p g e", g=GROUPS),
                                          sc[:, t, :].rearrange("p (g e) -> p g e", g=GROUPS),
                                          gsel[:, t, :, None].broadcast_to([P, GROUPS, EG]), ALU.mult)
                link(ins)
                for t in range(T):
                    ins = v.max(etop[:, t, :], emask[:, t, :])
                link(ins)
                link(v.tensor_copy(repe[:, :, 0:TOPK], etop[:, :, 0:TOPK]), False)
                link(v.tensor_reduce(tsum[:, :], etop[:, :, 0:TOPK], AX.X, ALU.add))
                link(v.tensor_scalar(trec[:, :], tsum[:, :], 1e-20, None, ALU.add), False)
                for t in range(T):
                    ins = v.match_replace(emark[:, t, :], repe[:, t, :], emask[:, t, :], PICKED)
                link(ins)
                link(v.reciprocal(tnorm[:, :], trec[:, :]), False)
                link(v.scalar_tensor_tensor(out=wsel[:, :, :], in0=emark[:, :, 0:E], scalar=PICKED, in1=emask[:, :, 0:E],
                                            op0=ALU.is_equal, op1=ALU.mult))
                for t in range(T):
                    ins = v.tensor_scalar(comb[:, t, :], wsel[:, t, :], tnorm[:, t:t + 1], 0.5 * GSCALE,
                                          ALU.mult, ALU.mult)
                link(ins)
                have(dve, "cT_ps", b - 1)
                link(v.tensor_copy(cparts[:, :, 0, 0:E], comb[:, :, :]))
                v.tensor_tensor(cr1[:, :, :], comb[:, :, :], cparts[:, :, 0, 0:E], ALU.subtract).then_inc(s_gate2, 1)
                dve.wait_ge(s_gate2, 3 * b + 1)
                v.tensor_copy(cparts[:, :, 1, 0:E], cr1[:, :, :]).then_inc(s_gate2, 1)
                dve.wait_ge(s_gate2, 3 * b + 2)
                v.tensor_tensor(cr2[:, :, :], cr1[:, :, :], cparts[:, :, 1, 0:E], ALU.subtract).then_inc(s_gate2, 1)
                dve.wait_ge(s_gate2, 3 * b + 3)
                link(v.tensor_copy(cparts[:, :, 2, 0:E], cr2[:, :, :]))
                assert n[0] == COUNT["gate"], n[0]

            def experts(b):
                have(dve, "y_ps", b - 1)
                for c in range(MC):
                    i = c % 2
                    have(dve, "g_th", b, c)
                    v.scalar_tensor_tensor(out=ga[:, i, :], in0=gth[:, i, :], scalar=1.0, in1=MB[i][:, 0:S],
                                           op0=ALU.add, op1=ALU.mult).then_inc(sem["m_a"], 1)
                    have(dve, "m_a", b, c)
                    if c < EC:
                        v.tensor_tensor(gbuf[:, i, :], ga[:, i, :], MB[i][:, S:2 * S], ALU.mult).then_inc(sem["m_b"], 1)
                        have(dve, "m_b", b, c)
                        have(dve, "cb_ps", b, c // 2)
                        v.tensor_tensor(inter[:, c, :], gbuf[:, i, :], MB[2][:, S * i:S * i + S], ALU.mult)\
                            .then_inc(sem["m_c"], 1)
                    else:
                        v.scalar_tensor_tensor(out=inter[:, c, :], in0=ga[:, i, :], scalar=0.5, in1=MB[i][:, S:2 * S],
                                               op0=ALU.mult, op1=ALU.mult).then_inc(sem["m_b"], 1)

            def finish(b):
                have(dve, "y_ps", b)
                have(dve, "out_st", b - 1)
                v.tensor_tensor(y[:, :, :], MB[1][:, 0:S].rearrange("p (t d) -> p t d", t=T), x3[:, :, :], ALU.add)\
                    .then_inc(sem["out_sb"], 1)

            def setup_ffn():
                dve.wait_ge(loaded["ffn"], N_FFN)
                for i, w_ in enumerate((w1, w2)):
                    step(v.tensor_reduce(wabs[:, i:i + 1], w_[:, :], AX.X, ALU.add, apply_absolute_value=True))

            def setup_l1():
                dve.wait_ge(loaded["l1"], N_L1)
                step(v.tensor_reduce(qsum[:, :], Wq[:, :, :], AX.X, ALU.add))
                step(v.memset(bkd[:, :, :], 0.0))
                step(v.memset(bvd[:, :, :], 0.0))
                dve.wait_ge(s_setv, 5)
                step(v.tensor_tensor(qshift[:, :], bq1[:, :], qsum[:, :], ALU.subtract))
                dve.wait_ge(s_setv, 6)
                step(v.tensor_scalar(qsum[:, :], qshift[:, :], 1.0 / P, None, ALU.mult))
                dve.wait_ge(s_setv, 7)
                for c in range(C1):
                    step(v.tensor_scalar(Wq[:, c, :], Wq[:, c, :], qsum[:, c:c + 1], None, ALU.add))
                assert setv[0] == SV_WQ
                for d_, b_ in ((bkd, bk1), (bvd, bv1)):
                    flat = d_[:, :, :].rearrange("p c h -> p (c h)")
                    for half in range(2):
                        rows = slice(D1 * half, D1 * half + D1)
                        step(v.tensor_copy(flat[rows, half:half + (H1 + 2) * (C1 - 1) + 1:H1 + 2], b_[rows, :]))
                step(v.tensor_reduce(csum[:, :], ctx_all[:, :, :], AX.X, ALU.add))
                assert setv[0] == SV_BD
                dve.wait_ge(s_setp, 1)
                step(v.tensor_scalar(wmean[:, :], F[0][:, 0:2], 1.0 / (HC * P * P), Q_EPS, ALU.mult, ALU.max))
                dve.wait_ge(s_setv, setv[0])
                step(v.reciprocal(wrec[:, :], wmean[:, :]))
                dve.wait_ge(s_setv, setv[0])
                for i, w_ in enumerate((w1, w2)):
                    step(v.tensor_scalar(w_[:, :], w_[:, :], wrec[:, i:i + 1], MAGIC, ALU.mult, ALU.add))
                dve.wait_ge(s_setv, setv[0])
                for w_ in (w1, w2):
                    step(v.tensor_scalar(w_[:, :], w_[:, :], MAGIC, 1.0, ALU.subtract, ALU.min))
                dve.wait_ge(s_setv, setv[0])
                for w_, q_ in ((w1, w1q), (w2, w2q)):
                    step(v.tensor_scalar(q_[:, :], w_[:, :], -1.0, None, ALU.max))
                step(v.memset(hs[:, :, 0:1], 0.0))
                step(v.memset(hs[:, :, S + 1:S + 2], 0.0))
                for r_ in (gsum, emask, repg, repe):
                    step(v.memset(r_[:, :, :], GONE))
                dve.wait_ge(s_setp, 6)
                step(v.tensor_scalar(arow[:, :], MB[2][0:H1, 0:P], SCALE1, None, ALU.mult))
                step(v.tensor_copy(brow[:, :], MB[2][0:H1, P:2 * P]))
                step(v.tensor_scalar(brow_n[:, :], MB[2][0:H1, P:2 * P], float(S), None, ALU.mult))
                assert setv[0] == SV_ROWS, setv[0]
                for k in range(8):
                    dve.wait_ge(s_setp, 7 + k)
                    step(v.tensor_copy((uflat if k < 4 else pflat)[:, 4 * P * (k % 4):4 * P * (k % 4) + 4 * P],
                                       MB[k % 2][0:B, :]))

            def setup_rows():
                dve.wait_ge(s_rows, 16 * 2 * B)
                dve.wait_ge(s_setv, setv[0])
                step(v.tensor_tensor(prow[:, :, :], prow[:, :, :], brow_n[:, None, :].broadcast_to([H1, B, P]), ALU.add))
                dve.wait_ge(s_setv, setv[0])
                assert setv[0] == SV_END

            for t in range(B + 1):
                if t < B:
                    front(t)
                    values_in(t)
                if t == 0:
                    setup_ffn()
                    setup_l1()
                    dve.wait_ge(s_const, C_ALL)
                if t == 1:
                    setup_rows()
                if t >= 1:
                    mix_in(t - 1)
                if t < B:
                    for k in range(8):
                        row_max(t, k)
                    max_parts(t)
                if t >= 1:
                    ffn_quant(t - 1)
                    mix_out(t - 1)
                    ffn_conv(t - 1)
                    ffn_silu(t - 1)
                if t < B:
                    attn_out(t)
                    if t == 0:
                        add1(t)
                if t >= 1:
                    ffn_quant2(t - 1)
                    ffn_round2(t - 1)
                    add2(t - 1)
                    if t < B:
                        add1(t)
                    attend(t - 1)
                    if t == 1:
                        dve.wait_ge(loaded["moe"], N_MOE)
                    route(t - 1)
                    experts(t - 1)
                    finish(t - 1)


def _layout(inp):
    f = {k: np.asarray(v) for k, v in inp.items()}

    def tr(w):
        return w.reshape(H0, D0, -1).transpose(1, 0, 2).reshape(P, -1)

    def chunks(w):
        return w.reshape(-1, P, w.shape[-1]).transpose(1, 0, 2)

    def wide(e, sh):
        return np.concatenate([e.transpose(1, 0, 2).reshape(P, E * M1), sh], axis=1).reshape(P, MC, P)

    return {
        "x": f["x"], "ctx": f["ctx_1024"], "ctxT": f["ctx_1024"].transpose(0, 2, 1),
        "wq": tr(f["L0_xattn_wq"]).T, "bq": tr(f["L0_xattn_bq"][:, None]),
        "wk": tr(f["L0_xattn_wk"]).T, "bk": tr(f["L0_xattn_bk"][:, None]),
        "wv": f["L0_xattn_wv"].T, "bv": f["L0_xattn_bv"][:, None], "wo": f["L0_xattn_wo"].T, "bo": f["L0_xattn_bo"],
        "w1": f["L0_ffn_w1"].T, "cw": chunks(f["L0_ffn_conv_w"][:, 0, :]),
        "cb": chunks(f["L0_ffn_conv_b"][:, None])[:, :, 0],
        "w2": chunks(f["L0_ffn_w2"].T).reshape(P, HC * P),
        "Wq": chunks(f["L1_xattn_Wq"].T), "bq1": f["L1_xattn_bq"].reshape(C1, P).T,
        "Wk": chunks(f["L1_xattn_Wk"].T), "bk1": f["L1_xattn_bk"].reshape(C1, P).T,
        "Wv": chunks(f["L1_xattn_Wv"].T), "bv1": f["L1_xattn_bv"].reshape(C1, P).T,
        "Wo": chunks(f["L1_xattn_Wo"]), "bo1": f["L1_xattn_bo"],
        "gk": f["L1_ffn_gate_kernel"], "gb": f["L1_ffn_gate_bias"],
        "mg": wide(f["L1_ffn_w_gate"], f["L1_ffn_sw_gate"]), "mu": wide(f["L1_ffn_w_up"], f["L1_ffn_sw_up"]),
        "md": chunks(np.concatenate([f["L1_ffn_w_down"].reshape(E * M1, P), f["L1_ffn_sw_down"]])),
    }


def kernel(**inputs):
    import concourse.bacc as bacc
    from concourse.bass_utils import run_bass_kernel_spmd

    nc = bacc.Bacc("TRN2", target_bir_lowering=False, num_devices=1)
    laid = _layout(inputs)
    arrays, a = {}, {}
    for name in INPUTS:
        arr = np.ascontiguousarray(laid[name])
        arrays["in_" + name] = arr
        a[name] = nc.dram_tensor("in_" + name, arr.shape, mybir.dt.from_np(arr.dtype), kind="ExternalInput").ap()
    out = nc.dram_tensor("out", (B, S, P), F32, kind="ExternalOutput").ap()
    layers_kernel(nc, a, out)
    r = run_bass_kernel_spmd(nc, [arrays], core_ids=[0])
    return r.results[0]["out"]
```

```python
from contextlib import ExitStack

import numpy as np
import concourse.bass as bass
from concourse import mybir

F32 = mybir.dt.float32
BF16 = mybir.dt.bfloat16
ALU = mybir.AluOpType
ACT = mybir.ActivationFunctionType
AX = mybir.AxisListType

P = 128
B, S = 8, 256
T = S // P
H0, D0 = 16, 8
WIN = 64
NB = S // WIN
KEYS = 2 * WIN
QT = 32
KT = WIN + QT
HG = 4
PARTS = 3
COMBOS = [(0, 0), (0, 1), (1, 0), (0, 2), (2, 0), (1, 1)]
ROWS = len(COMBOS) * D0
HC = 4
H1, D1 = 16, 64
C1 = H1 * D1 // P
E, M1 = 16, 64
EC = E * M1 // P
MC = EC + 1
RING = 3
AHEAD = 5
TOPK, GROUPS, TOPG, GSCALE = 4, 4, 2, 2.5
EG = E // GROUPS
LN_EPS, Q_EPS = 1e-5, 1e-5
MAGIC = 1.5 * 2.0 ** 23
MASKED = -1e30
GONE = -1e30
PICKED = -2e30
SCALE0 = float(D0) ** -0.5
SCALE1 = float(D1) ** -0.5

INPUTS = ["x", "ctx", "ctxT", "wq", "bq", "wk", "bk", "wv", "bv", "wo", "bo",
          "w1", "cw", "cb", "w2", "Wq", "bq1", "Wk", "bk1", "Wv", "bv1", "Wo", "bo1",
          "gk", "gb", "mg", "mu", "md"]

COUNT = {"x_in": 16, "ctxT_in": 16, "ctx_in": 16, "qk_rows": 16 * 2 * len(COMBOS), "max_rows": 32, "out_st": 16,
         "xres": 1, "xnT_ps": 1, "xnT_sb": 1, "qk_ps": 1, "qk_sb": 4, "split_r": 1, "split_mid": 1, "parts": 1,
         "v_ps": 1, "v_sb": 1, "s_ps": 8, "rowmax": 8, "maxT_ps": 1, "max_hi": 1, "max_lo": 1,
         "st_ps": 8, "probs": 8, "pv_ps": NB, "rden": 2, "o_div": 2, "op_ps": 1, "x1": 1, "x1_kept": 1,
         "q1_max": 1, "q1_clip": 1, "q1_rec": 1, "q1_s": 1, "q1_inv": 1, "q1_big": 2, "q1_int": 1, "q1T_ps": 1, "q1b_ps": 1,
         "q1T_sb": 1, "q1b_sb": 1, "h_ps": 2, "h_sb": 2, "c_mid": HC, "c_left": HC, "c_all": HC, "th": 1, "silu": 1,
         "hT_ps": 2, "q2_max": 2, "q2_clip": 1, "q2_rec": 1, "q2_s": 1, "q2_inv": 1, "q2b_ps": 1, "q2b_sb": 1,
         "q2_big": 1, "q2_int": 1, "f_ps": 1, "x2": 2, "x2res": 1,
         "g_ps": 1, "g_sb": 1, "p_ps": 4, "p_sb": 4, "u_slot": 1, "m_ps": 1, "m_sb": 1,
         "x3T_ps": 1, "x3T_sb": 1, "a_ps": 1, "x3": 1, "x4T_ps": 1, "x4T_sb": 1,
         "lg_ps": 1, "lg_th": 1, "gate": 21, "cT_ps": 1, "cT_sb": 1,
         "gu_ps": MC, "cb_ps": EC // 2, "cb_sb": EC // 2, "g_th": MC, "m_a": MC, "m_b": MC, "m_c": EC, "y_ps": 1, "out_sb": 1}
for _p in ("l1", "l2", "l3", "l4"):
    COUNT.update({_p + "_st": T, _p + "_mv": T, _p + "_ve": 1, _p + "_rs": 1, _p + "_xn": T})


def layers_kernel(nc, a, out):
    ctx = ExitStack()
    with ctx:
        def sb(name, shape, dt=F32):
            return ctx.enter_context(nc.sbuf_tensor(name, shape, dt))

        def ps(name, shape, dt=F32):
            return ctx.enter_context(nc.psum_tensor(name, shape, dt))

        sem = {n: ctx.enter_context(nc.semaphore(n)) for n in COUNT}
        loaded = {n: ctx.enter_context(nc.semaphore("ld_" + n)) for n in ("l0", "ffn", "l1", "moe")}
        s_const = ctx.enter_context(nc.semaphore("s_const"))
        s_setv = ctx.enter_context(nc.semaphore("s_setv"))
        s_setp = ctx.enter_context(nc.semaphore("s_setp"))
        s_seta = ctx.enter_context(nc.semaphore("s_seta"))
        s_gate2 = ctx.enter_context(nc.semaphore("s_gate2"))
        s_bias = ctx.enter_context(nc.semaphore("s_bias"))
        s_rows = ctx.enter_context(nc.semaphore("s_rows"))

        def have(eng, name, b, k=None):
            n = COUNT[name]
            if isinstance(b, int):
                if b >= 0:
                    eng.wait_ge(sem[name], b * n + (n if k is None else k + 1))
            else:
                eng.wait_ge(sem[name], b * n + (n if k is None else k + 1))

        wq, wk, wv, wo = (sb(n, [P, P]) for n in ("wq_s", "wk_s", "wv_s", "wo_s"))
        bq, bk, bv = (sb(n, [P, 1]) for n in ("bq_s", "bk_s", "bv_s"))
        bqs = sb("bqs", [P, 1])
        bo, bo1 = sb("bo_s", [P, P]), sb("bo1_s", [P, P])
        w1, w2 = sb("w1_s", [P, HC * P]), sb("w2_s", [P, HC * P])
        w1q, w2q = sb("w1q", [P, HC * P], BF16), sb("w2q", [P, HC * P], BF16)
        wabs, wmean, wrec = sb("wabs", [P, 2]), sb("wmean", [P, 2]), sb("wrec", [P, 2])
        cw, cb = sb("cw_s", [P, HC, 3]), sb("cb_s", [P, HC])
        Wq, Wk, Wv, Wo = (sb(n, [P, C1, P]) for n in ("Wq_s", "Wk_s", "Wv_s", "Wo_s"))
        bq1, bk1, bv1 = (sb(n, [P, C1]) for n in ("bq1_s", "bk1_s", "bv1_s"))
        qsum, qshift = sb("qsum", [P, C1]), sb("qshift", [P, C1])
        bkd, bvd = sb("bkd", [P, C1, H1]), sb("bvd", [P, C1, H1])
        AT, BV = sb("AT", [P, H1, P]), sb("BV", [P, H1, P])
        csum = sb("csum", [P, B])
        uflat, pflat = sb("uflat", [B, H1 * P]), sb("pflat", [B, H1 * P])
        urow, prow = sb("urow", [H1, B, P]), sb("prow", [H1, B, P])
        arow, brow, brow_n = sb("arow", [H1, P]), sb("brow", [H1, P]), sb("brow_n", [H1, P])
        gk, gb, gbh = sb("gk_s", [P, E]), sb("gb_s", [P, E]), sb("gbh", [P, E])
        mg, mu, md = (sb(n, [P, MC, P]) for n in ("mg_s", "mu_s", "md_s"))
        ident, identb, ones = sb("ident", [P, P]), sb("identb", [P, P], BF16), sb("ones", [P, P])
        mask_s = sb("mask_s", [P, T, KT], BF16)
        mask_t = sb("mask_t", [P, 2, WIN], BF16)
        denom = sb("denom", [P, HG, HG * D0])
        pick = sb("pick", [96, EC, 2, M1], BF16)
        mhalf, eps = sb("mhalf", [P, T]), sb("eps", [P, T])
        repg, repe = sb("repg", [P, T, 8]), sb("repe", [P, T, 8])

        x_s = sb("x_s", [P, T, P])
        xres = sb("xres_s", [P, T, P])
        ctxT = sb("ctxT_s", [P, WIN + S])
        ctx_all = sb("ctx_all", [P, B, S])
        xn = {p: sb(p + "_xn_s", [P, T, P]) for p in ("l1", "l2", "l3", "l4")}
        lst = {p: sb(p + "_st_s", [P, T, 6]) for p in xn}
        lmv = {p: sb(p + "_mv_s", [P, T, 2]) for p in xn}
        lve = {p: sb(p + "_ve_s", [P, T]) for p in xn}
        lrs = {p: sb(p + "_rs_s", [P, T]) for p in xn}
        xnT = sb("xnT", [P, S])
        qk = sb("qk", [P, 2, S])
        rem = sb("rem", [P, 2, S])
        parts = sb("parts_s", [P, PARTS, 2, S], BF16)
        Q = sb("Q", [ROWS + 2, H0, S], BF16)
        K = sb("K", [ROWS + 2, H0, WIN + S], BF16)
        V = sb("V", [P, NB, H0 // HG, HG, HG * D0])
        mx = sb("mx", [P, H0, T])
        nhl = sb("nhl", [H0 * T, 2, P], BF16)
        PT = sb("PT", [P, 2, H0, WIN])
        rden = sb("rden_s", [P, S])
        oT = sb("oT", [P, S])
        x1, x1k = sb("x1_s", [P, T, P]), sb("x1k_s", [P, T, P])
        am1, cl1, rc1, s1, iv1 = (sb(n, [P, T]) for n in ("am1", "cl1", "rc1", "s1", "iv1"))
        big1 = sb("big1", [P, T, P])
        int1 = sb("int1", [P, T, P], BF16)
        q1T = sb("q1T", [P, S], BF16)
        q1b = sb("q1b", [P, S])
        hs = sb("hs", [P, HC, S + 2])
        hc = sb("hc", [P, HC, S])
        th = sb("th_s", [P, HC, S])
        am2, cl2, rc2, s2, iv2 = (sb(n, [P, T]) for n in ("am2", "cl2", "rc2", "s2", "iv2"))
        q2b = sb("q2b", [P, S])
        int2 = sb("int2", [P, HC, S], BF16)
        x2 = sb("x2_s", [P, T, P])
        x2res = sb("x2res_s", [P, T, P])
        ctxn = sb("ctxn", [P, T, P])
        G = sb("G", [P, P])
        PG = sb("PG", [P, H1, P])
        uslot = sb("uslot", [H1, P])
        M = sb("M", [P, P])
        x3T = sb("x3T", [P, S])
        x3 = sb("x3_s", [P, T, P])
        x4T = sb("x4T", [P, S])
        lth = sb("lth", [P, T, E])
        sc = sb("sc", [P, T, E])
        pair_sum, pair_max = sb("pair_sum", [P, T * GROUPS, 2]), sb("pair_max", [P, T * GROUPS, 2])
        cross, same = sb("cross", [P, T * GROUPS]), sb("same", [P, T * GROUPS])
        gsum, gtop, gmark = sb("gsum", [P, T, 16]), sb("gtop", [P, T, 8]), sb("gmark", [P, T, 16])
        gsel = sb("gsel", [P, T, GROUPS])
        emask, etop, emark = sb("emask", [P, T, 32]), sb("etop", [P, T, 8]), sb("emark", [P, T, 32])
        tsum, trec, tnorm = sb("tsum", [P, T]), sb("trec", [P, T]), sb("tnorm", [P, T])
        wsel, comb, cr1, cr2 = (sb(n, [P, T, E]) for n in ("wsel", "comb", "cr1", "cr2"))
        cparts = sb("cparts", [P, T, PARTS, 32], BF16)
        cT = sb("cT", [96, S], BF16)
        gth = sb("gth", [P, RING, S])
        ga = sb("ga", [P, RING, S])
        cbs = sb("cbs", [P, 4, S])
        inter = sb("inter", [P, MC, S])
        y = sb("y", [P, T, P])

        A = [ps(f"A{i}", [P, 512]) for i in range(2)]
        O = ps("O", [P, 2, S])
        F = [ps(f"F{i}", [P, 512]) for i in range(2)]
        MB = [ps(f"M{i}", [P, 512]) for i in range(3)]

        R = [MB[0], MB[1], F[0]]
        CB = [MB[2][:, :], O[:, :, :].rearrange("p a s -> p (a s)")]
        Y = F[1]
        OV = [O[:, 0, :], MB[2][:, 0:S]]

        block = ctx.enter_context(nc.Block())

        L0_LOADS = [(wq, "wq"), (wk, "wk"), (bq, "bq"), (bk, "bk"), (wv, "wv"), (bv, "bv"), (wo, "wo")]
        FFN_LOADS = [(w1, "w1"), (w2, "w2"), (cw, "cw"), (cb, "cb")]
        L1_LOADS = [(Wq, "Wq"), (Wk, "Wk"), (bq1, "bq1"), (bk1, "bk1"), (Wv, "Wv"), (bv1, "bv1"), (Wo, "Wo")]
        MOE_LOADS = [(gk, "gk"), (mg, "mg"), (mu, "mu"), (md, "md")]
        N_L0 = 16 * (len(L0_LOADS) + 1)
        N_FFN = 16 * len(FFN_LOADS)
        N_L1 = 16 * (len(L1_LOADS) + 2)
        N_MOE = 16 * (len(MOE_LOADS) + 1)
        C_ALL = 37
        SV_WQ = 7 + C1
        SV_BD = SV_WQ + 5
        SV_ROWS = SV_BD + 17
        SV_END = SV_ROWS + 9

        @block.sync
        def _(sp):
            def load_x(b):
                have(sp, "xres", b - 1)
                have(sp, "l1_xn", b - 1)
                sp.dma_start(x_s[:, :, :], a["x"][b].rearrange("(t p) d -> p t d", p=P)).then_inc(sem["x_in"], 16)

            def load_ctxT(b):
                have(sp, "v_ps", b - 1)
                sp.dma_start(ctxT[:, WIN:], a["ctxT"][b]).then_inc(sem["ctxT_in"], 16)

            def load_ctx(b):
                have(sp, "g_ps", b - 1)
                sp.dma_start(ctxn[:, :, :], a["ctx"][b].rearrange("(t p) d -> p t d", p=P)).then_inc(sem["ctx_in"], 16)

            def spread_parts(b):
                have(sp, "st_ps", b - 1)
                for part, made in enumerate(("qk_sb", "split_mid", "parts")):
                    have(sp, made, b)
                    for c, (pq, pk) in enumerate(COMBOS):
                        if pq == part:
                            sp.dma_start(Q[D0 * c:D0 * c + D0, :, :], parts[:, pq, 0, :]).then_inc(sem["qk_rows"], 16)
                        if pk == part:
                            sp.dma_start(K[D0 * c:D0 * c + D0, :, WIN:], parts[:, pk, 1, :])\
                                .then_inc(sem["qk_rows"], 16)

            def spread_max(b):
                have(sp, "max_lo", b)
                for part in range(2):
                    sp.dma_start(Q[ROWS + part:ROWS + part + 1, :, :], nhl[:, part, :]).then_inc(sem["max_rows"], 16)

            def store(b):
                have(sp, "out_sb", b)
                sp.dma_start(out[b].rearrange("(t p) d -> p t d", p=P), y[:, :, :]).then_inc(sem["out_st"], 16)

            load_x(0)
            for t_, n in L0_LOADS:
                sp.dma_start(t_[tuple([slice(None)] * len(t_.shape))], a[n]).then_inc(loaded["l0"], 16)
            sp.dma_start(bo[:, :], a["bo"].partition_broadcast(P)).then_inc(loaded["l0"], 16)
            sp.wait_ge(s_const, 1)
            load_ctxT(0)
            load_ctx(0)
            for t_, n in FFN_LOADS:
                sp.dma_start(t_[tuple([slice(None)] * len(t_.shape))], a[n]).then_inc(loaded["ffn"], 16)
            for t_, n in L1_LOADS:
                sp.dma_start(t_[tuple([slice(None)] * len(t_.shape))], a[n]).then_inc(loaded["l1"], 16)
            sp.dma_start(bo1[:, :], a["bo1"].partition_broadcast(P)).then_inc(loaded["l1"], 16)
            sp.dma_start(ctx_all[:, :, :], a["ctxT"].rearrange("b p s -> p b s")).then_inc(loaded["l1"], 16)
            for t_, n in MOE_LOADS:
                sp.dma_start(t_[tuple([slice(None)] * len(t_.shape))], a[n]).then_inc(loaded["moe"], 16)
            sp.dma_start(gb[:, :], a["gb"].partition_broadcast(P)).then_inc(loaded["moe"], 16)
            sp.wait_ge(s_const, C_ALL)

            def regroup():
                sp.wait_ge(s_setv, SV_ROWS + 8)
                for src, dst in ((uflat, urow), (pflat, prow)):
                    for b_ in range(B):
                        sp.dma_start(dst[:, b_, :], src[b_:b_ + 1, :]).then_inc(s_rows, 16)

            def iteration(t, nxt=True, nxt2=True, stage2=True):
                if nxt:
                    spread_parts(t + 1)
                if nxt2:
                    load_x(t + 2)
                    load_ctxT(t + 2)
                if nxt:
                    load_ctx(t + 1)
                if stage2:
                    store(t - 1)
                if nxt:
                    spread_max(t + 1)

            spread_parts(0)
            load_x(1)
            load_ctxT(1)
            spread_max(0)
            regroup()
            iteration(0, stage2=False)
            iteration(1)
            with sp.Fori(2, B - 2) as t:
                iteration(t)
            iteration(B - 2, nxt2=False)
            iteration(B - 1, nxt=False, nxt2=False)
            store(B - 1)
            have(sp, "out_st", B - 1)

        @block.gpsimd
        def _(pool):
            done = [0]

            def step(ins):
                done[0] += 1
                ins.then_inc(s_const, 1)
                pool.wait_ge(s_const, done[0])

            step(pool.memset(ctxT[:, 0:WIN], 0.0))
            for m_ in (ident, identb):
                step(pool.memset(m_[:, :], 0.0))
                step(pool.affine_select(out=m_[:, :], in_=m_[:, :], compare_op=ALU.not_equal, fill=1.0, base=0,
                                        pattern=[[-1, P]], channel_multiplier=1))
            step(pool.memset(ones[:, :], 1.0))
            step(pool.memset(K[:, :, :], 0.0))
            step(pool.memset(K[32:ROWS + 2, :, :], 1.0))
            step(pool.memset(K[:, :, 0:WIN], 0.0))
            step(pool.memset(V[:, :, :, :, :], 0.0))
            step(pool.memset(denom[:, :, :], 0.0))
            own = denom[:, :, :].rearrange("p a b -> p (a b)")
            for h in range(HG):
                step(pool.memset(denom[:, h, D0 * h:D0 * h + D0], 1.0))
            step(pool.memset(mask_s[:, :, :], 0.0))
            step(pool.memset(mask_t[:, :, :], 0.0))
            for j in range(P // QT):
                m_ = mask_s[QT * j:QT * j + QT, :, :]
                step(pool.affine_select(out=m_, in_=m_, compare_op=ALU.is_ge, fill=MASKED, base=0,
                                        pattern=[[0, T], [1, KT]], channel_multiplier=-1))
                step(pool.affine_select(out=m_, in_=m_, compare_op=ALU.is_ge, fill=MASKED, base=WIN,
                                        pattern=[[0, T], [-1, KT]], channel_multiplier=1))
                if QT * j < WIN:
                    m_ = mask_s[QT * j:QT * j + QT, 0, :]
                    step(pool.affine_select(out=m_, in_=m_, compare_op=ALU.is_ge, fill=MASKED, base=QT * j - WIN,
                                            pattern=[[1, KT]], channel_multiplier=0))
            step(pool.affine_select(out=mask_t[:, :, :], in_=mask_t[:, :, :], compare_op=ALU.is_ge, fill=MASKED, base=0,
                                    pattern=[[0, 2], [-1, WIN]], channel_multiplier=1))
            step(pool.affine_select(out=mask_t[:, :, :], in_=mask_t[:, :, :], compare_op=ALU.is_ge, fill=MASKED,
                                    base=WIN, pattern=[[0, 2], [1, WIN]], channel_multiplier=-1))
            step(pool.affine_select(out=mask_t[:, 0, :], in_=mask_t[:, 0, :], compare_op=ALU.is_ge, fill=MASKED,
                                    base=-WIN, pattern=[[0, WIN]], channel_multiplier=1))
            step(pool.memset(pick[:, :, :, :], 1.0))
            for k in range(PARTS):
                m_ = pick[32 * k:32 * k + 32, :, :, :]
                step(pool.affine_select(out=m_, in_=m_, compare_op=ALU.is_equal, fill=0.0, base=0,
                                        pattern=[[-2, EC], [-1, 2], [0, M1]], channel_multiplier=1))
            step(pool.memset(mhalf[:, :], -0.5))
            step(pool.memset(eps[:, :], LN_EPS))
            step(pool.memset(cparts[:, :, :, :], 0.0))
            assert done[0] == C_ALL, done[0]

            def norm(p, b):
                have(pool, p + "_mv", b)
                pool.tensor_tensor(lve[p][:, :], lmv[p][:, :, 1], eps[:, :], ALU.add).then_inc(sem[p + "_ve"], 1)
                have(pool, p + "_ve", b)
                have(pool, p + "_xn", b - 1)
                pool.tensor_tensor(lrs[p][:, :], lve[p][:, :], mhalf[:, :], ALU.pow).then_inc(sem[p + "_rs"], 1)

            def residual(b):
                have(pool, "x_in", b)
                have(pool, "x1", b - 1)
                pool.tensor_tensor(xres[:, :, :], x_s[:, :, :], bo[:, None, :].broadcast_to([P, T, P]), ALU.add)\
                    .then_inc(sem["xres"], 1)

            def split_rem(b):
                have(pool, "qk_sb", b)
                pool.tensor_tensor(rem[:, :, :], qk[:, :, :], parts[:, 0, :, :], ALU.subtract).then_inc(sem["split_r"], 1)

            def split_low(b):
                have(pool, "split_mid", b)
                pool.tensor_tensor(parts[:, 2, :, :], rem[:, :, :], parts[:, 1, :, :], ALU.subtract)\
                    .then_inc(sem["parts"], 1)

            def residual2(b):
                have(pool, "x2", b)
                have(pool, "x3", b - 1)
                pool.tensor_tensor(x2res[:, :, :], x2[:, :, :], bo1[:, None, :].broadcast_to([P, T, P]), ALU.add)\
                    .then_inc(sem["x2res"], 1)

            pool.wait_ge(loaded["l0"], N_L0)

            def weigh(b):
                for c in range(EC):
                    have(pool, "m_b", b, c)
                    have(pool, "cb_sb", b, c // 2)
                    pool.tensor_tensor(inter[:, c, :], inter[:, c, :], cbs[:, c % 4, :], ALU.mult)\
                        .then_inc(sem["m_c"], 1)

            def iteration(t, stage1=True, stage2=True, nxt=True):
                if nxt:
                    norm("l1", t + 1)
                if stage2:
                    norm("l3", t - 1)
                if nxt:
                    split_rem(t + 1)
                if stage2:
                    residual2(t - 1)
                if nxt:
                    split_low(t + 1)
                if stage1:
                    norm("l2", t)
                if stage2:
                    norm("l4", t - 1)
                if nxt:
                    residual(t + 1)
                if stage2:
                    weigh(t - 1)

            norm("l1", 0)
            split_rem(0)
            split_low(0)
            pool.wait_ge(s_bias, 2)
            residual(0)
            iteration(0, stage2=False)
            pool.wait_ge(loaded["l1"], N_L1)
            iteration(1)
            with pool.Fori(2, B - 1) as t:
                iteration(t)
            iteration(B - 1, nxt=False)
            iteration(B, stage1=False, nxt=False)

        @block.scalar
        def _(act):
            def front(b):
                have(act, "xnT_ps", b)
                have(act, "qk_ps", b - 1)
                nc.scalar.activation(xnT[:, :], A[1][:, 0:S], ACT.Copy).then_inc(sem["xnT_sb"], 1)
                have(act, "qk_ps", b)
                have(act, "qk_rows", b - 1)
                for i, (bias, scale) in enumerate(((bqs, SCALE0), (bk, 1.0))):
                    nc.scalar.activation(qk[:, i, :], A[1][:, S * i:S * i + S], ACT.Identity, bias=bias[:, :],
                                         scale=scale).then_inc(sem["qk_sb"], 1)
                    nc.scalar.activation(parts[:, 0, i, :], A[1][:, S * i:S * i + S], ACT.Identity, bias=bias[:, :],
                                         scale=scale).then_inc(sem["qk_sb"], 1)

            def split_mid(b):
                have(act, "split_r", b)
                nc.scalar.activation(parts[:, 1, :, :], rem[:, :, :], ACT.Copy).then_inc(sem["split_mid"], 1)

            def exps(b, first, last):
                for k in range(first, last):
                    n = k // 2
                    have(act, "st_ps", b, k)
                    have(act, "pv_ps", b, n - 2) if n >= 2 else have(act, "pv_ps", b - 1, n + 2)
                    nc.scalar.activation(PT[:, n % 2, 8 * (k % 2):8 * (k % 2) + 8, :].rearrange("p h q -> p (h q)"),
                                         A[k % 2][:, :], ACT.Exp).then_inc(sem["probs"], 1)

            def ffn_in(b):
                have(act, "x1", b)
                have(act, "x2", b - 1)
                nc.scalar.activation(x1k[:, :, :], x1[:, :, :], ACT.Copy).then_inc(sem["x1_kept"], 1)
                have(act, "q1T_ps", b)
                have(act, "h_ps", b - 1)
                nc.scalar.activation(q1T[:, :], F[0][:, 0:P].bitcast(BF16), ACT.Copy).then_inc(sem["q1T_sb"], 1)
                have(act, "q1b_ps", b)
                have(act, "h_sb", b - 1)
                nc.scalar.activation(q1b[:, :], MB[1][:, 0:S], ACT.Copy).then_inc(sem["q1b_sb"], 1)

            def ffn_mid(b):
                for c in range(HC):
                    have(act, "h_sb", b, c // 2)
                    have(act, "hT_ps", b - 1)
                    have(act, "q2_big", b - 1)
                    nc.scalar.activation(hc[:, c, :], hs[:, c, 1:S + 1], ACT.Identity, bias=cb[:, c:c + 1],
                                         scale=cw[:, c, 1:2]).then_inc(sem["c_mid"], 1)

            def ffn_tanh(b):
                have(act, "c_all", b)
                have(act, "q2_int", b - 1)
                nc.scalar.activation(th[:, :, :], hc[:, :, :], ACT.Tanh, scale=0.5).then_inc(sem["th"], 1)

            def ffn_out(b):
                have(act, "q2b_ps", b)
                have(act, "q2_big", b - 1)
                nc.scalar.activation(q2b[:, :], F[0][:, 0:S], ACT.Copy).then_inc(sem["q2b_sb"], 1)

            def gram(b):
                have(act, "g_ps", b)
                have(act, "p_ps", b - 1)
                nc.scalar.activation(G[:, :], F[0][:, 0:P], ACT.Copy).then_inc(sem["g_sb"], 1)

            def gram_values(b, k):
                have(act, "p_ps", b, k)
                have(act, "m_ps", b - 1)
                nc.scalar.activation(PG[:, 4 * k:4 * k + 4, :].rearrange("p h j -> p (h j)"), F[1 - k % 2][:, :],
                                     ACT.Copy).then_inc(sem["p_sb"], 1)

            def attend(b):
                have(act, "x3T_ps", b)
                have(act, "a_ps", b - 1)
                nc.scalar.activation(x3T[:, :], MB[1][:, 0:S], ACT.Copy, bias=1.0).then_inc(sem["x3T_sb"], 1)

            def tokens4(b):
                have(act, "x4T_ps", b)
                have(act, "gu_ps", b - 1)
                nc.scalar.activation(x4T[:, :], MB[0][:, 0:S], ACT.Copy).then_inc(sem["x4T_sb"], 1)

            def logits(b):
                have(act, "lg_ps", b)
                have(act, "gate", b - 1)
                nc.scalar.activation(lth[:, :, :].rearrange("p t e -> p (t e)"), MB[1][:, 0:T * E], ACT.Tanh,
                                     scale=0.5).then_inc(sem["lg_th"], 1)

            def experts(b, c):
                have(act, "gu_ps", b, c)
                have(act, "m_a", b, c - RING) if c >= RING else have(act, "m_a", b - 1)
                nc.scalar.activation(gth[:, c % RING, :], R[c % RING][:, 0:S], ACT.Tanh, scale=0.5)\
                    .then_inc(sem["g_th"], 1)

            def weights(b, k):
                have(act, "cb_ps", b, k)
                have(act, "m_c", b, 2 * k - 3) if k >= 2 else have(act, "m_c", b - 1)
                nc.scalar.activation(cbs[:, 2 * (k % 2):2 * (k % 2) + 2, :].rearrange("p c s -> p (c s)"), CB[k % 2], ACT.Copy)\
                    .then_inc(sem["cb_sb"], 1)

            def moe(b):
                for c in range(2, AHEAD):
                    experts(b, c)
                have(act, "cT_ps", b)
                have(act, "cb_ps", b - 1)
                nc.scalar.activation(cT[:, :], MB[2][0:96, 0:P].bitcast(BF16), ACT.Copy).then_inc(sem["cT_sb"], 1)
                weights(b, 0)
                weights(b, 1)
                for c in range(AHEAD, MC):
                    experts(b, c)
                    if c in (AHEAD, AHEAD + 2):
                        weights(b, (c - AHEAD) // 2 + 2)

            act.wait_ge(loaded["l0"], N_L0)
            nc.scalar.activation(bqs[:, :], bq[:, :], ACT.Copy, scale=SCALE0).then_inc(s_seta, 1)
            act.wait_ge(s_seta, 1)

            def setup():
                for k in range(8):
                    r, odd = k // 2, k % 2
                    act.wait_ge(s_setp, 2 + r)
                    dst = (AT if r < 2 else BV)[:, 8 * (r % 2) + odd:8 * (r % 2) + 8:2, :]
                    nc.scalar.activation(dst, MB[odd][:, :].rearrange("p (h j) -> p h j", j=P), ACT.Copy, scale=SCALE1 if k < 4 else 1.0)\
                        .then_inc(s_seta, 1)

            def iteration(t, stage1=True, stage2=True, nxt=True):
                if stage2:
                    ffn_in(t - 1)
                    ffn_mid(t - 1)
                if stage1:
                    exps(t, 0, 4)
                if stage2:
                    ffn_tanh(t - 1)
                if stage1:
                    exps(t, 4, 2 * NB)
                if stage2:
                    ffn_out(t - 1)
                if nxt:
                    front(t + 1)
                if stage1:
                    gram(t)
                    gram_values(t, 0)
                if nxt:
                    split_mid(t + 1)
                if stage2:
                    attend(t - 1)
                if stage1:
                    gram_values(t, 1)
                    gram_values(t, 2)
                if stage2:
                    tokens4(t - 1)
                if stage2:
                    logits(t - 1)
                    experts(t - 1, 0)
                    experts(t - 1, 1)
                if stage1:
                    gram_values(t, 3)
                if stage2:
                    moe(t - 1)

            front(0)
            split_mid(0)
            setup()
            iteration(0, stage2=False)
            iteration(1)
            with act.Fori(2, B - 1) as t:
                iteration(t)
            iteration(B - 1, nxt=False)
            iteration(B, stage1=False, nxt=False)

        @block.tensor
        def _(pe):
            def front(b):
                have(pe, "l1_xn", b)
                have(pe, "probs", b - 1)
                for t in range(T):
                    last = pe.transpose(A[1][:, P * t:P * t + P], xn["l1"][:, t, :], ident[:, :])
                last.then_inc(sem["xnT_ps"], 1)

            def values_proj(b):
                have(pe, "ctxT_in", b)
                have(pe, "probs", b - 1)
                for n in range(NB):
                    last = pe.matmul(A[0][:, P * n:P * n + P], ctxT[:, WIN * n:WIN * n + KEYS], wv[:, :],
                                     start=True, stop=True)
                last.then_inc(sem["v_ps"], 1)

            def qk_proj(b):
                have(pe, "xnT_sb", b)
                pe.matmul(A[1][:, 0:S], wq[:, :], xnT[:, :], start=True, stop=True)
                pe.matmul(A[1][:, S:2 * S], wk[:, :], ctxT[:, WIN:], start=True, stop=True).then_inc(sem["qk_ps"], 1)

            def row_scores(b, first, last):
                if first == 0:
                    have(pe, "qk_rows", b)
                for k in range(first, last):
                    t, hg = k // 4, k % 4
                    bank = A[(k + 1) % 2]
                    if k == 0:
                        have(pe, "qk_sb", b)
                    elif k == 1:
                        have(pe, "v_sb", b)
                    else:
                        have(pe, "rowmax", b, k - 2)
                    pe.matmul(bank[:, 0:HG * KT], identb[:, :], mask_s[:, t:t + 1, :].broadcast_to([P, HG, KT]),
                              start=True, stop=False, skip_group_check=True)
                    for h in range(HG):
                        for j in range(P // QT):
                            q0 = P * t + QT * j
                            tile = pe.matmul(bank[QT * j:QT * j + QT, KT * h:KT * h + KT],
                                             Q[0:ROWS, HG * hg + h, q0:q0 + QT], K[0:ROWS, HG * hg + h, q0:q0 + KT],
                                             start=False, stop=(h == HG - 1), skip_group_check=True)
                    tile.then_inc(sem["s_ps"], 1)

            def max_rows(b):
                have(pe, "rowmax", b)
                pe.transpose(A[1][0:H0 * T, 0:P], mx[:, :, :].rearrange("p h t -> p (h t)"), ident[:, :])\
                    .then_inc(sem["maxT_ps"], 1)

            def key_scores(b, k):
                n, half = k // 2, k % 2
                if k == 0:
                    have(pe, "max_rows", b)
                if k == 1:
                    have(pe, "max_lo", b)
                if k >= 2:
                    have(pe, "probs", b, k - 2)
                bank = A[k % 2]
                pe.matmul(bank[:, :], identb[:, :], mask_t[:, min(n, 1):min(n, 1) + 1, :].broadcast_to([P, 8, WIN]),
                          start=True, stop=False, skip_group_check=True)
                for h in range(8):
                    last = pe.matmul(bank[:, WIN * h:WIN * h + WIN], K[:, 8 * half + h, WIN * n:WIN * n + KEYS],
                                     Q[:, 8 * half + h, WIN * n:WIN * n + WIN], start=False, stop=(h == 7),
                                     skip_group_check=True)
                last.then_inc(sem["st_ps"], 1)

            def values(b, n):
                have(pe, "probs", b, 2 * n + 1)
                if n == 0:
                    have(pe, "v_sb", b)
                    have(pe, "cb_sb", b - 2) if not isinstance(b, int) or b >= 2 else None
                    have(pe, "x1", b - 1)
                if n == 2:
                    have(pe, "cb_sb", b - 2) if not isinstance(b, int) or b >= 2 else None
                for what in range(2):
                    for h in range(HG):
                        for g in range(H0 // HG):
                            w = V[:, n, g, h, :] if what == 0 else denom[:, h, :]
                            c = 2 * WIN * what + WIN * (n % 2)
                            last = pe.matmul(OV[n // 2][32 * g:32 * g + 32, c:c + WIN], w,
                                             PT[:, n % 2, HG * g + h, :], start=(h == 0), stop=(h == HG - 1),
                                             skip_group_check=True)
                last.then_inc(sem["pv_ps"], 1)

            def out_proj(b):
                have(pe, "o_div", b)
                for t in range(T):
                    last = pe.matmul(O[:, 0, P * t:P * t + P], oT[:, P * t:P * t + P], wo[:, :], start=True, stop=True)
                last.then_inc(sem["op_ps"], 1)

            def ffn_in(b):
                have(pe, "q1_int", b)
                have(pe, "m_b", b - 1)
                have(pe, "p_sb", b)
                for t in range(T):
                    last = pe.transpose(F[0][:, 0:P].bitcast(BF16)[:, P * t:P * t + P], int1[:, t, :], identb[:, :])
                last.then_inc(sem["q1T_ps"], 1)
                have(pe, "q1_inv", b)
                for t in range(T):
                    last = pe.matmul(MB[1][:, P * t:P * t + P], iv1[:, t:t + 1].broadcast_to([P, P]), ident[:, :],
                                     start=True, stop=True)
                last.then_inc(sem["q1b_ps"], 1)

            def ffn_up(b):
                have(pe, "q1T_sb", b)
                for f in range(2):
                    if f == 1:
                        have(pe, "out_sb", b - 1)
                    for i in range(2):
                        c = 2 * f + i
                        last = pe.matmul(F[f][:, S * i:S * i + S], w1q[:, P * c:P * c + P], q1T[:, :],
                                         start=True, stop=True)
                    last.then_inc(sem["h_ps"], 1)

            def ffn_turn(b):
                have(pe, "silu", b)
                for t in range(T):
                    have(pe, "h_sb", b, t)
                    for c in range(HC):
                        last = pe.transpose(F[t][:, P * c:P * c + P], hc[:, c, P * t:P * t + P], ident[:, :])
                    last.then_inc(sem["hT_ps"], 1)

            def ffn_scale(b):
                have(pe, "q2_s", b)
                have(pe, "q2_max", b, 0)
                for t in range(T):
                    last = pe.matmul(F[0][:, P * t:P * t + P], s2[:, t:t + 1].broadcast_to([P, P]), ident[:, :],
                                     start=True, stop=True)
                last.then_inc(sem["q2b_ps"], 1)

            def ffn_down(b):
                have(pe, "q2_int", b)
                have(pe, "q2_max", b)
                for t in range(T):
                    for c in range(HC):
                        last = pe.matmul(F[1][:, P * t:P * t + P], int2[:, c, P * t:P * t + P], w2q[:, P * c:P * c + P],
                                         start=(c == 0), stop=(c == HC - 1), skip_group_check=True)
                last.then_inc(sem["f_ps"], 1)

            def gram(b):
                have(pe, "ctx_in", b)
                have(pe, "q2b_sb", b - 1)
                have(pe, "m_b", b - 2) if not isinstance(b, int) or b >= 2 else None
                for t in range(T):
                    last = pe.matmul(F[0][:, 0:P], ctxn[:, t, :], ctxn[:, t, :], start=(t == 0), stop=(t == T - 1))
                last.then_inc(sem["g_ps"], 1)

            def gram_values(b, k):
                if k == 0:
                    have(pe, "g_sb", b)
                    have(pe, "x2", b - 1)
                if k >= 2:
                    have(pe, "p_sb", b, k - 2)
                pe.matmul(F[1 - k % 2][:, :], G[:, :], BV[:, 4 * k:4 * k + 4, :], start=True, stop=True)\
                    .then_inc(sem["p_ps"], 1)

            def mix(b, first, last):
                if first == 0:
                    have(pe, "p_sb", b)
                    have(pe, "m_b", b - 1)
                for h in range(first, last):
                    pe.matmul(MB[0][:, 0:P], AT[:, h, :], PG[:, h, :], start=(h == 0), stop=False)
                if last == H1:
                    have(pe, "u_slot", b)
                    pe.matmul(MB[0][:, 0:P], uslot[:, :], brow[:, :], start=False, stop=False)
                    pe.matmul(MB[0][:, 0:P], arow[:, :], prow[:, b, :], start=False, stop=True).then_inc(sem["m_ps"], 1)

            def attend(b):
                have(pe, "l3_xn", b)
                have(pe, "q1b_sb", b)
                have(pe, "m_sb", b)
                for t in range(T):
                    last = pe.transpose(MB[1][:, P * t:P * t + P], xn["l3"][:, t, :], ident[:, :])
                last.then_inc(sem["x3T_ps"], 1)
                have(pe, "x3T_sb", b)
                have(pe, "o_div", b + 1) if not isinstance(b, int) or b < B - 1 else None
                for t in range(T):
                    last = pe.matmul(MB[2][:, P * t:P * t + P], x3T[:, P * t:P * t + P], M[:, :], start=True, stop=True)
                last.then_inc(sem["a_ps"], 1)

            def route(b):
                have(pe, "l4_xn", b)
                for t in range(T):
                    last = pe.transpose(MB[0][:, P * t:P * t + P], xn["l4"][:, t, :], ident[:, :])
                last.then_inc(sem["x4T_ps"], 1)

            def logits(b):
                have(pe, "x4T_sb", b)
                for t in range(T):
                    last = pe.matmul(MB[1][:, E * t:E * t + E], x4T[:, P * t:P * t + P], gk[:, :], start=True, stop=True)
                last.then_inc(sem["lg_ps"], 1)

            def gate_up(b, c):
                if c == 1:
                    have(pe, "lg_th", b)
                if c >= RING:
                    have(pe, "m_b", b, c - RING)
                elif c == 2:
                    have(pe, "p_sb", b + 1) if not isinstance(b, int) or b < B - 1 else None
                bank = R[c % RING]
                pe.matmul(bank[:, 0:S], mg[:, c, :], x4T[:, :], start=True, stop=True)
                pe.matmul(bank[:, S:2 * S], mu[:, c, :], x4T[:, :], start=True, stop=True)\
                    .then_inc(sem["gu_ps"], 1)

            def turn_weights(b):
                have(pe, "gate", b)
                for t in range(T):
                    last = pe.transpose(MB[2][0:96, 0:P].bitcast(BF16)[:, P * t:P * t + P],
                                        cparts[:, t, :, :].rearrange("p k e -> p (k e)"), identb[:, :])
                last.then_inc(sem["cT_ps"], 1)

            def combine(b, k):
                if k == 0:
                    have(pe, "cT_sb", b)
                elif k == 1:
                    have(pe, "x1", b + 1) if not isinstance(b, int) or b < B - 1 else None
                else:
                    have(pe, "cb_sb", b, k - 2)
                for i in range(2):
                    last = pe.matmul(CB[k % 2][:, S * i:S * i + S], pick[:, 2 * k + i, :, :].rearrange("p a m -> p (a m)"),
                                     cT[:, :], start=True, stop=True)
                last.then_inc(sem["cb_ps"], 1)

            def down(b, c):
                if c < EC:
                    have(pe, "m_c", b, c)
                else:
                    have(pe, "m_b", b)
                for t in range(T):
                    last = pe.matmul(Y[:, P * t:P * t + P], inter[:, c, P * t:P * t + P], md[:, c, :],
                                     start=(c == 0 and t == 0), stop=(c == MC - 1), skip_group_check=True)
                if c == MC - 1:
                    last.then_inc(sem["y_ps"], 1)

            def experts(b, rows):
                def scores(k):
                    if rows is not None:
                        row_scores(rows, k, k + 1)

                scores(0)
                gate_up(b, 2)
                scores(1)
                gate_up(b, 3)
                scores(2)
                gate_up(b, 4)
                scores(3)
                turn_weights(b)
                gate_up(b, 5)
                combine(b, 0)
                combine(b, 1)
                scores(4)
                down(b, 0)
                gate_up(b, 6)
                combine(b, 2)
                down(b, 1)
                scores(5)
                down(b, 2)
                gate_up(b, 7)
                combine(b, 3)
                down(b, 3)
                scores(6)
                gate_up(b, 8)
                down(b, 4)
                scores(7)
                for c in range(AHEAD, MC):
                    down(b, c)

            pe.wait_ge(s_const, C_ALL)
            pe.wait_ge(loaded["l0"], N_L0)

            def setup_bo():
                pe.matmul(O[:, 0, 0:P], bv[:, 0:1].broadcast_to([P, P]), wo[:, :], start=True, stop=True).then_inc(s_bias, 1)

            def setup():
                pe.wait_ge(s_setv, 2)
                pe.matmul(F[0][:, 0:2], ones[:, :], wabs[:, :], start=True, stop=True).then_inc(s_setp, 1)
                pe.wait_ge(loaded["l1"], N_L1)
                pe.wait_ge(s_setv, SV_WQ)
                for k in range(4):
                    lhs, rhs = (Wk, Wq) if k < 2 else (Wv, Wo)
                    if k >= 1:
                        pe.wait_ge(s_seta, 1 + 2 * k)
                    for i in range(4):
                        c = 4 * (k % 2) + i
                        for odd in range(2):
                            p0 = D1 * odd
                            last = pe.matmul(MB[odd][:, P * i:P * i + P], lhs[p0:p0 + D1, c, :], rhs[p0:p0 + D1, c, :],
                                             start=True, stop=True, skip_group_check=True)
                    last.then_inc(s_setp, 1)
                pe.wait_ge(s_setv, SV_BD)
                for i, (d_, w_) in enumerate(((bkd, Wq), (bvd, Wo))):
                    for c in range(C1):
                        last = pe.matmul(MB[2][0:H1, P * i:P * i + P], d_[:, c, :], w_[:, c, :], start=(c == 0),
                                         stop=(c == C1 - 1))
                last.then_inc(s_setp, 1)
                pe.wait_ge(s_seta, 9)
                for k in range(8):
                    src = AT if k < 4 else BV
                    bank = MB[k % 2]
                    if k >= 2:
                        pe.wait_ge(s_setv, SV_ROWS + k - 1)
                    pe.matmul(bank[0:B, :], csum[:, :], src[:, 4 * (k % 4):4 * (k % 4) + 4, :], start=True, stop=True)\
                        .then_inc(s_setp, 1)
                pe.wait_ge(s_setv, SV_ROWS + 8)

            def iteration(t, stage1=True, stage2=True, nxt=True):
                if stage2:
                    ffn_in(t - 1)
                    mix(t - 1, 0, 4)
                    ffn_up(t - 1)
                    mix(t - 1, 4, 12)
                if stage1:
                    key_scores(t, 0)
                    key_scores(t, 1)
                    for n in range(NB - 1):
                        key_scores(t, 2 * n + 2)
                        key_scores(t, 2 * n + 3)
                        values(t, n)
                if stage2:
                    ffn_turn(t - 1)
                if stage1:
                    values(t, NB - 1)
                if nxt:
                    front(t + 1)
                if stage2:
                    ffn_scale(t - 1)
                if nxt:
                    values_proj(t + 1)
                    qk_proj(t + 1)
                if stage2:
                    ffn_down(t - 1)
                    mix(t - 1, 12, H1)
                if stage1:
                    out_proj(t)
                if stage1:
                    gram(t)
                    gram_values(t, 0)
                if stage2:
                    attend(t - 1)
                if stage1:
                    gram_values(t, 1)
                    gram_values(t, 2)
                if stage2:
                    route(t - 1)
                if stage2:
                    logits(t - 1)
                    gate_up(t - 1, 0)
                    gate_up(t - 1, 1)
                if stage1:
                    gram_values(t, 3)
                if stage2:
                    experts(t - 1, t + 1 if nxt else None)
                elif nxt:
                    row_scores(t + 1, 0, 8)
                if nxt:
                    max_rows(t + 1)

            front(0)
            values_proj(0)
            qk_proj(0)
            setup_bo()
            row_scores(0, 0, 8)
            max_rows(0)
            setup()
            iteration(0, stage2=False)
            iteration(1)
            with pe.Fori(2, B - 1) as t:
                iteration(t)
            iteration(B - 1, nxt=False)
            iteration(B, stage1=False, nxt=False)

        @block.vector
        def _(dve):
            v = nc.vector
            setv = [0]

            def step(ins):
                setv[0] += 1
                ins.then_inc(s_setv, 1)

            def norm_stats(p, src, b):
                for t in range(T):
                    v.bn_stats(lst[p][:, t, :], src[:, t, :]).then_inc(sem[p + "_st"], 1)
                dve.drain()
                for t in range(T):
                    v.bn_aggr(lmv[p][:, t, :], lst[p][:, t, :]).then_inc(sem[p + "_mv"], 1)

            def norm_apply(p, src, b):
                have(dve, p + "_rs", b)
                for t in range(T):
                    v.tensor_scalar(xn[p][:, t, :], src[:, t, :], lmv[p][:, t, 0:1], lrs[p][:, t:t + 1],
                                    ALU.subtract, ALU.mult).then_inc(sem[p + "_xn"], 1)

            def front(b):
                have(dve, "x_in", b)
                norm_stats("l1", x_s, b)

            def front_apply(b):
                have(dve, "xnT_ps", b - 1)
                norm_apply("l1", x_s, b)

            def values_in(b):
                have(dve, "v_ps", b)
                have(dve, "pv_ps", b - 1)
                src = A[0][:, :].rearrange("p (w h d) -> p w h d", h=HG, d=D0)
                dst = V[:, :, :, :, :].rearrange("p n g h c -> p (n g) (h c)")
                for h in range(HG):
                    ins = v.tensor_copy(dst[:, :, (HG * D0 + D0) * h:(HG * D0 + D0) * h + D0], src[:, :, h, :])
                ins.then_inc(sem["v_sb"], 1)

            def row_max(b, k):
                t, hg = k // 4, k % 4
                have(dve, "s_ps", b, k)
                if k == 0:
                    have(dve, "maxT_ps", b - 1)
                v.tensor_reduce(mx[:, HG * hg:HG * hg + HG, t], A[(k + 1) % 2][:, 0:HG * KT]
                                .rearrange("p (h c) -> p h c", c=KT), AX.X, ALU.max).then_inc(sem["rowmax"], 1)

            def max_parts(b):
                have(dve, "maxT_ps", b)
                have(dve, "max_rows", b - 1)
                v.tensor_scalar(nhl[:, 0, :], A[1][0:H0 * T, 0:P], -1.0, None, ALU.mult).then_inc(sem["max_hi"], 1)
                have(dve, "max_hi", b)
                v.scalar_tensor_tensor(out=nhl[:, 1, :], in0=A[1][0:H0 * T, 0:P], scalar=-1.0, in1=nhl[:, 0, :],
                                       op0=ALU.mult, op1=ALU.subtract).then_inc(sem["max_lo"], 1)

            def attn_out(b, half):
                have(dve, "pv_ps", b, 2 * half + 1)
                cols = slice(2 * WIN * half, 2 * WIN * half + 2 * WIN)
                v.reciprocal(rden[:, cols], OV[half][:, 2 * WIN:4 * WIN]).then_inc(sem["rden"], 1)
                have(dve, "rden", b, half)
                if half == 0:
                    have(dve, "op_ps", b - 1)
                v.tensor_tensor(oT[:, cols], OV[half][:, 0:2 * WIN], rden[:, cols], ALU.mult).then_inc(sem["o_div"], 1)

            def add1(b):
                have(dve, "op_ps", b)
                have(dve, "xres", b)
                have(dve, "x1_kept", b - 1)
                v.tensor_tensor(x1[:, :, :], O[:, 0, :].rearrange("p (t d) -> p t d", t=T), xres[:, :, :], ALU.add)\
                    .then_inc(sem["x1"], 1)

            def ffn_norm(b):
                have(dve, "x1", b)
                norm_stats("l2", x1, b)

            def ffn_quant_a(b):
                norm_apply("l2", x1, b)
                have(dve, "l2_xn", b)
                v.tensor_reduce(am1[:, :], xn["l2"][:, :, :], AX.X, ALU.max, apply_absolute_value=True)\
                    .then_inc(sem["q1_max"], 1)

            def ffn_quant_b(b):
                have(dve, "q1_max", b)
                v.tensor_scalar(cl1[:, :], am1[:, :], Q_EPS, None, ALU.max).then_inc(sem["q1_clip"], 1)
                have(dve, "q1_clip", b)
                v.reciprocal(rc1[:, :], cl1[:, :]).then_inc(sem["q1_rec"], 1)
                have(dve, "q1b_ps", b - 1)
                v.tensor_scalar(iv1[:, :], cl1[:, :], 1.0 / 127, wmean[:, 0:1], ALU.mult, ALU.mult)\
                    .then_inc(sem["q1_inv"], 1)
                have(dve, "q1_rec", b)
                v.tensor_scalar(s1[:, :], rc1[:, :], 127.0, None, ALU.mult).then_inc(sem["q1_s"], 1)
                have(dve, "q1_s", b)
                for t in range(T):
                    v.tensor_scalar(big1[:, t, :], xn["l2"][:, t, :], s1[:, t:t + 1], MAGIC, ALU.mult, ALU.add)\
                        .then_inc(sem["q1_big"], 1)
                have(dve, "q1_big", b)
                have(dve, "q1T_ps", b - 1)
                v.tensor_scalar(int1[:, :, :], big1[:, :, :], MAGIC, 127.0, ALU.subtract, ALU.min)\
                    .then_inc(sem["q1_int"], 1)

            def ffn_take(b):
                have(dve, "q1b_sb", b)
                have(dve, "c_all", b - 1)
                for f in range(2):
                    have(dve, "h_ps", b, f)
                    v.tensor_tensor(hs[:, 2 * f:2 * f + 2, 1:S + 1], F[f][:, :].rearrange("p (c s) -> p c s", c=2),
                                    q1b[:, None, :].broadcast_to([P, 2, S]), ALU.mult).then_inc(sem["h_sb"], 1)

            def ffn_conv(b):
                for c in range(HC):
                    have(dve, "c_mid", b, c)
                    v.scalar_tensor_tensor(out=hc[:, c, :], in0=hs[:, c, 0:S], scalar=cw[:, c, 0:1], in1=hc[:, c, :],
                                           op0=ALU.mult, op1=ALU.add).then_inc(sem["c_left"], 1)
                for c in range(HC):
                    have(dve, "c_left", b, c)
                    v.scalar_tensor_tensor(out=hc[:, c, :], in0=hs[:, c, 2:S + 2], scalar=cw[:, c, 2:3],
                                           in1=hc[:, c, :], op0=ALU.mult, op1=ALU.add).then_inc(sem["c_all"], 1)

            def ffn_silu(b):
                have(dve, "th", b)
                v.scalar_tensor_tensor(out=hc[:, :, :], in0=th[:, :, :], scalar=1.0, in1=hc[:, :, :], op0=ALU.add,
                                       op1=ALU.mult).then_inc(sem["silu"], 1)

            def ffn_quant2(b):
                for t in range(T):
                    have(dve, "hT_ps", b, t)
                    v.tensor_reduce(am2[:, t:t + 1], F[t][:, :], AX.X, ALU.max, apply_absolute_value=True)\
                        .then_inc(sem["q2_max"], 1)
                have(dve, "q2_max", b)
                v.tensor_scalar(cl2[:, :], am2[:, :], 2 * Q_EPS, None, ALU.max).then_inc(sem["q2_clip"], 1)
                have(dve, "q2_clip", b)
                v.reciprocal(rc2[:, :], cl2[:, :]).then_inc(sem["q2_rec"], 1)
                v.tensor_scalar(iv2[:, :], cl2[:, :], 0.5 / 127, wmean[:, 1:2], ALU.mult, ALU.mult)\
                    .then_inc(sem["q2_inv"], 1)
                have(dve, "q2_rec", b)
                have(dve, "q2b_ps", b - 1)
                v.tensor_scalar(s2[:, :], rc2[:, :], 127.0, None, ALU.mult).then_inc(sem["q2_s"], 1)

            def ffn_round2(b):
                have(dve, "q2b_sb", b)
                v.tensor_tensor(th[:, :, :], hc[:, :, :], q2b[:, None, :].broadcast_to([P, HC, S]), ALU.mult)\
                    .then_inc(sem["q2_big"], 1)
                have(dve, "q2_big", b)
                have(dve, "f_ps", b - 1)
                v.tensor_scalar(int2[:, :, :], th[:, :, :], MAGIC, MAGIC, ALU.add, ALU.subtract)\
                    .then_inc(sem["q2_int"], 1)

            def add2(b):
                have(dve, "f_ps", b)
                have(dve, "q2_inv", b)
                have(dve, "x1_kept", b)
                have(dve, "x2res", b - 1)
                for t in range(T):
                    v.scalar_tensor_tensor(out=x2[:, t, :], in0=F[1][:, P * t:P * t + P], scalar=iv2[:, t:t + 1],
                                           in1=x1k[:, t, :], op0=ALU.mult, op1=ALU.add).then_inc(sem["x2"], 1)

            def mix_in(b):
                have(dve, "m_ps", b - 1)
                v.tensor_copy(uslot[:, :], urow[:, b, :]).then_inc(sem["u_slot"], 1)

            def mix_out(b):
                have(dve, "m_ps", b)
                have(dve, "a_ps", b - 1)
                v.tensor_copy(M[:, :], MB[0][:, 0:P]).then_inc(sem["m_sb"], 1)

            def norm3(b):
                have(dve, "x2", b)
                norm_stats("l3", x2, b)

            def attend(b):
                have(dve, "a_ps", b)
                have(dve, "x2res", b)
                v.tensor_tensor(x3[:, :, :], MB[2][:, 0:S].rearrange("p (t d) -> p t d", t=T), x2res[:, :, :], ALU.add)\
                    .then_inc(sem["x3"], 1)
                have(dve, "x3", b)
                norm_stats("l4", x3, b)

            def route(b, rows):
                n = [0]
                between = {5: lambda: gate(b, 0), 7: lambda: gate_by_up(b, 0), 9: lambda: gate(b, 1),
                           10: lambda: gate_by_up(b, 1), 13: lambda: rows is None or row_max(rows, 0),
                           16: lambda: gate(b, 2), 17: lambda: rows is None or row_max(rows, 1),
                           18: lambda: gate_by_up(b, 2)}

                def link(ins, wait=True):
                    ins.then_inc(sem["gate"], 1)
                    n[0] += 1
                    if n[0] in between:
                        between[n[0]]()
                    if wait and n[0] < COUNT["gate"]:
                        if n[0] in (6, 8, 11, 14):
                            dve.drain()
                        else:
                            have(dve, "gate", b, n[0] - 1)

                have(dve, "lg_th", b)
                link(v.scalar_tensor_tensor(out=sc[:, :, :], in0=lth[:, :, :], scalar=0.5,
                                            in1=gbh[:, None, :].broadcast_to([P, T, E]), op0=ALU.mult, op1=ALU.add))
                pairs = sc[:, :, :].rearrange("p t (g a b) -> p (t g) a b", g=GROUPS, b=2)
                link(v.tensor_tensor(pair_sum[:, :, :], pairs[:, :, :, 0], pairs[:, :, :, 1], ALU.add), False)
                link(v.tensor_tensor(pair_max[:, :, :], pairs[:, :, :, 0], pairs[:, :, :, 1], ALU.max))
                link(v.tensor_tensor(cross[:, :], pair_max[:, :, 0], pair_max[:, :, 1], ALU.add), False)
                link(v.tensor_tensor(same[:, :], pair_sum[:, :, 0], pair_sum[:, :, 1], ALU.max))
                link(v.tensor_tensor(gsum[:, :, 0:GROUPS], cross[:, :].rearrange("p (t g) -> p t g", t=T),
                                     same[:, :].rearrange("p (t g) -> p t g", t=T), ALU.max))
                for t in range(T):
                    ins = v.max(gtop[:, t, :], gsum[:, t, :])
                link(ins)
                link(v.tensor_copy(repg[:, :, 0:TOPG], gtop[:, :, 0:TOPG]))
                for t in range(T):
                    ins = v.match_replace(gmark[:, t, :], repg[:, t, :], gsum[:, t, :], PICKED)
                link(ins)
                link(v.tensor_scalar(gsel[:, :, :], gmark[:, :, 0:GROUPS], PICKED, None, ALU.is_equal))
                for t in range(T):
                    ins = v.tensor_tensor(emask[:, t, 0:E].rearrange("p (g e) -> p g e", g=GROUPS),
                                          sc[:, t, :].rearrange("p (g e) -> p g e", g=GROUPS),
                                          gsel[:, t, :, None].broadcast_to([P, GROUPS, EG]), ALU.mult)
                link(ins)
                for t in range(T):
                    ins = v.max(etop[:, t, :], emask[:, t, :])
                link(ins)
                link(v.tensor_copy(repe[:, :, 0:TOPK], etop[:, :, 0:TOPK]), False)
                link(v.tensor_reduce(tsum[:, :], etop[:, :, 0:TOPK], AX.X, ALU.add))
                link(v.tensor_scalar(trec[:, :], tsum[:, :], 1e-20, None, ALU.add), False)
                for t in range(T):
                    ins = v.match_replace(emark[:, t, :], repe[:, t, :], emask[:, t, :], PICKED)
                link(ins)
                link(v.reciprocal(tnorm[:, :], trec[:, :]), False)
                link(v.scalar_tensor_tensor(out=wsel[:, :, :], in0=emark[:, :, 0:E], scalar=PICKED, in1=emask[:, :, 0:E],
                                            op0=ALU.is_equal, op1=ALU.mult))
                for t in range(T):
                    ins = v.tensor_scalar(comb[:, t, :], wsel[:, t, :], tnorm[:, t:t + 1], 0.5 * GSCALE,
                                          ALU.mult, ALU.mult)
                link(ins)
                have(dve, "cT_ps", b - 1)
                link(v.tensor_copy(cparts[:, :, 0, 0:E], comb[:, :, :]))
                v.tensor_tensor(cr1[:, :, :], comb[:, :, :], cparts[:, :, 0, 0:E], ALU.subtract).then_inc(s_gate2, 1)
                dve.wait_ge(s_gate2, 3 * b + 1)
                v.tensor_copy(cparts[:, :, 1, 0:E], cr1[:, :, :]).then_inc(s_gate2, 1)
                dve.wait_ge(s_gate2, 3 * b + 2)
                v.tensor_tensor(cr2[:, :, :], cr1[:, :, :], cparts[:, :, 1, 0:E], ALU.subtract).then_inc(s_gate2, 1)
                dve.wait_ge(s_gate2, 3 * b + 3)
                link(v.tensor_copy(cparts[:, :, 2, 0:E], cr2[:, :, :]))
                assert n[0] == COUNT["gate"], n[0]

            def gate(b, c):
                have(dve, "g_th", b, c)
                if c == 0:
                    have(dve, "y_ps", b - 1)
                v.scalar_tensor_tensor(out=ga[:, c % RING, :], in0=gth[:, c % RING, :], scalar=1.0,
                                       in1=R[c % RING][:, 0:S], op0=ALU.add, op1=ALU.mult).then_inc(sem["m_a"], 1)

            def gate_by_up(b, c):
                have(dve, "m_a", b, c)
                if c < EC:
                    v.tensor_tensor(inter[:, c, :], ga[:, c % RING, :], R[c % RING][:, S:2 * S], ALU.mult)\
                        .then_inc(sem["m_b"], 1)
                else:
                    v.scalar_tensor_tensor(out=inter[:, c, :], in0=ga[:, c % RING, :], scalar=0.5,
                                           in1=R[c % RING][:, S:2 * S], op0=ALU.mult, op1=ALU.mult).then_inc(sem["m_b"], 1)

            def finish(b):
                have(dve, "y_ps", b)
                have(dve, "out_st", b - 1)
                v.tensor_tensor(y[:, :, :], Y[:, 0:S].rearrange("p (t d) -> p t d", t=T), x3[:, :, :], ALU.add)\
                    .then_inc(sem["out_sb"], 1)

            def setup_ffn():
                dve.wait_ge(loaded["ffn"], N_FFN)
                for i, w_ in enumerate((w1, w2)):
                    step(v.tensor_reduce(wabs[:, i:i + 1], w_[:, :], AX.X, ALU.add, apply_absolute_value=True))

            def setup_bo():
                dve.wait_ge(s_bias, 1)
                v.tensor_tensor(bo[:, :], bo[:, :], O[:, 0, 0:P], ALU.add).then_inc(s_bias, 1)

            def setup_l1():
                dve.wait_ge(loaded["l1"], N_L1)
                step(v.tensor_reduce(qsum[:, :], Wq[:, :, :], AX.X, ALU.add))
                step(v.memset(bkd[:, :, :], 0.0))
                step(v.memset(bvd[:, :, :], 0.0))
                dve.wait_ge(s_setv, 5)
                step(v.tensor_tensor(qshift[:, :], bq1[:, :], qsum[:, :], ALU.subtract))
                dve.wait_ge(s_setv, 6)
                step(v.tensor_scalar(qsum[:, :], qshift[:, :], 1.0 / P, None, ALU.mult))
                dve.wait_ge(s_setv, 7)
                for c in range(C1):
                    step(v.tensor_scalar(Wq[:, c, :], Wq[:, c, :], qsum[:, c:c + 1], None, ALU.add))
                assert setv[0] == SV_WQ
                for d_, b_ in ((bkd, bk1), (bvd, bv1)):
                    flat = d_[:, :, :].rearrange("p c h -> p (c h)")
                    for half in range(2):
                        rows = slice(D1 * half, D1 * half + D1)
                        step(v.tensor_copy(flat[rows, half:half + (H1 + 2) * (C1 - 1) + 1:H1 + 2], b_[rows, :]))
                step(v.tensor_reduce(csum[:, :], ctx_all[:, :, :], AX.X, ALU.add))
                assert setv[0] == SV_BD
                dve.wait_ge(s_setp, 1)
                step(v.tensor_scalar(wmean[:, :], F[0][:, 0:2], 1.0 / (HC * P * P), Q_EPS, ALU.mult, ALU.max))
                dve.wait_ge(s_setv, setv[0])
                step(v.reciprocal(wrec[:, :], wmean[:, :]))
                dve.wait_ge(s_setv, setv[0])
                for i, w_ in enumerate((w1, w2)):
                    step(v.tensor_scalar(w_[:, :], w_[:, :], wrec[:, i:i + 1], MAGIC, ALU.mult, ALU.add))
                dve.wait_ge(s_setv, setv[0])
                for w_ in (w1, w2):
                    step(v.tensor_scalar(w_[:, :], w_[:, :], MAGIC, 1.0, ALU.subtract, ALU.min))
                dve.wait_ge(s_setv, setv[0])
                for w_, q_ in ((w1, w1q), (w2, w2q)):
                    step(v.tensor_scalar(q_[:, :], w_[:, :], -1.0, None, ALU.max))
                step(v.memset(hs[:, :, 0:1], 0.0))
                step(v.memset(hs[:, :, S + 1:S + 2], 0.0))
                for r_ in (gsum, emask, repg, repe):
                    step(v.memset(r_[:, :, :], GONE))
                dve.wait_ge(s_setp, 6)
                step(v.tensor_scalar(arow[:, :], MB[2][0:H1, 0:P], SCALE1, None, ALU.mult))
                step(v.tensor_copy(brow[:, :], MB[2][0:H1, P:2 * P]))
                step(v.tensor_scalar(brow_n[:, :], MB[2][0:H1, P:2 * P], float(S), None, ALU.mult))
                assert setv[0] == SV_ROWS, setv[0]
                for k in range(8):
                    dve.wait_ge(s_setp, 7 + k)
                    step(v.tensor_copy((uflat if k < 4 else pflat)[:, 4 * P * (k % 4):4 * P * (k % 4) + 4 * P],
                                       MB[k % 2][0:B, :]))

            def setup_rows():
                dve.wait_ge(s_rows, 16 * 2 * B)
                dve.wait_ge(s_setv, setv[0])
                step(v.tensor_tensor(prow[:, :, :], prow[:, :, :], brow_n[:, None, :].broadcast_to([H1, B, P]), ALU.add))
                dve.wait_ge(s_setv, setv[0])
                assert setv[0] == SV_END

            def iteration(t, stage1=True, stage2=True, nxt=True, second=False):
                if stage2:
                    ffn_take(t - 1)
                if second:
                    setup_rows()
                    dve.wait_ge(loaded["moe"], N_MOE)
                    step(v.tensor_scalar(gbh[:, :], gb[:, :], 0.5, None, ALU.add))
                    dve.wait_ge(s_setv, setv[0])
                if nxt:
                    front(t + 1)
                if stage2:
                    mix_in(t - 1)
                    ffn_conv(t - 1)
                if nxt:
                    front_apply(t + 1)
                if stage2:
                    ffn_silu(t - 1)
                    ffn_quant2(t - 1)
                if stage1:
                    attn_out(t, 0)
                if stage2:
                    ffn_round2(t - 1)
                if stage1:
                    attn_out(t, 1)
                if stage2:
                    add2(t - 1)
                    norm3(t - 1)
                if nxt:
                    values_in(t + 1)
                if stage2:
                    norm_apply("l3", x2, t - 1)
                    mix_out(t - 1)
                if stage1:
                    add1(t)
                if stage1:
                    ffn_norm(t)
                if stage2:
                    attend(t - 1)
                if stage1:
                    ffn_quant_a(t)
                if stage2:
                    norm_apply("l4", x3, t - 1)
                if stage1:
                    ffn_quant_b(t)
                if stage2:
                    route(t - 1, t + 1 if nxt else None)
                    gate(t - 1, RING)
                    for c in range(RING, MC):
                        if c + 1 < MC:
                            gate(t - 1, c + 1)
                        gate_by_up(t - 1, c)
                        if nxt and c < MC - 1:
                            row_max(t + 1, c - RING + 2)
                    if nxt:
                        row_max(t + 1, 7)
                elif nxt:
                    for k in range(8):
                        row_max(t + 1, k)
                if stage2:
                    finish(t - 1)
                if nxt:
                    max_parts(t + 1)

            front(0)
            front_apply(0)
            values_in(0)
            setup_bo()
            for k in range(8):
                row_max(0, k)
            max_parts(0)
            setup_ffn()
            setup_l1()
            dve.wait_ge(s_const, C_ALL)
            iteration(0, stage2=False)
            iteration(1, second=True)
            with dve.Fori(2, B - 1) as t:
                iteration(t)
            iteration(B - 1, nxt=False)
            iteration(B, stage1=False, nxt=False)


def _layout(inp):
    f = {k: np.asarray(v) for k, v in inp.items()}

    def tr(w):
        return w.reshape(H0, D0, -1).transpose(1, 0, 2).reshape(P, -1)

    def chunks(w):
        return w.reshape(-1, P, w.shape[-1]).transpose(1, 0, 2)

    def wide(e, sh):
        return np.concatenate([e.transpose(1, 0, 2).reshape(P, E * M1), sh], axis=1).reshape(P, MC, P)

    return {
        "x": f["x"], "ctx": f["ctx_1024"], "ctxT": f["ctx_1024"].transpose(0, 2, 1),
        "wq": tr(f["L0_xattn_wq"]).T, "bq": tr(f["L0_xattn_bq"][:, None]),
        "wk": tr(f["L0_xattn_wk"]).T, "bk": tr(f["L0_xattn_bk"][:, None]),
        "wv": f["L0_xattn_wv"].T, "bv": f["L0_xattn_bv"][:, None], "wo": f["L0_xattn_wo"].T, "bo": f["L0_xattn_bo"],
        "w1": f["L0_ffn_w1"].T, "cw": chunks(f["L0_ffn_conv_w"][:, 0, :]),
        "cb": chunks(f["L0_ffn_conv_b"][:, None])[:, :, 0],
        "w2": chunks(f["L0_ffn_w2"].T).reshape(P, HC * P),
        "Wq": chunks(f["L1_xattn_Wq"].T), "bq1": f["L1_xattn_bq"].reshape(C1, P).T,
        "Wk": chunks(f["L1_xattn_Wk"].T), "bk1": f["L1_xattn_bk"].reshape(C1, P).T,
        "Wv": chunks(f["L1_xattn_Wv"].T), "bv1": f["L1_xattn_bv"].reshape(C1, P).T,
        "Wo": chunks(f["L1_xattn_Wo"]), "bo1": f["L1_xattn_bo"],
        "gk": f["L1_ffn_gate_kernel"], "gb": f["L1_ffn_gate_bias"],
        "mg": wide(f["L1_ffn_w_gate"], f["L1_ffn_sw_gate"]), "mu": wide(f["L1_ffn_w_up"], f["L1_ffn_sw_up"]),
        "md": chunks(np.concatenate([f["L1_ffn_w_down"].reshape(E * M1, P), f["L1_ffn_sw_down"]])),
    }


def kernel(**inputs):
    import concourse.bacc as bacc
    from concourse.bass_utils import run_bass_kernel_spmd

    nc = bacc.Bacc("TRN2", target_bir_lowering=False, num_devices=1)
    laid = _layout(inputs)
    arrays, a = {}, {}
    for name in INPUTS:
        arr = np.ascontiguousarray(laid[name])
        arrays["in_" + name] = arr
        a[name] = nc.dram_tensor("in_" + name, arr.shape, mybir.dt.from_np(arr.dtype), kind="ExternalInput").ap()
    out = nc.dram_tensor("out", (B, S, P), F32, kind="ExternalOutput").ap()
    layers_kernel(nc, a, out)
    r = run_bass_kernel_spmd(nc, [arrays], core_ids=[0])
    return r.results[0]["out"]
```

```python
from contextlib import ExitStack

import numpy as np
import concourse.bass as bass
from concourse import mybir

F32 = mybir.dt.float32
BF16 = mybir.dt.bfloat16
ALU = mybir.AluOpType
ACT = mybir.ActivationFunctionType
AX = mybir.AxisListType

P = 128
B, S = 8, 256
T = S // P
H0, D0 = 16, 8
WIN = 64
NB = S // WIN
KEYS = 2 * WIN
QT = 32
KT = WIN + QT
HG = 4
PARTS = 3
COMBOS = [(0, 0), (0, 1), (1, 0), (0, 2), (2, 0), (1, 1)]
ROWS = len(COMBOS) * D0
HC = 4
H1, D1 = 16, 64
C1 = H1 * D1 // P
E, M1 = 16, 64
EC = E * M1 // P
MC = EC + 1
RING = 3
AHEAD = 5
TOPK, GROUPS, TOPG, GSCALE = 4, 4, 2, 2.5
EG = E // GROUPS
LN_EPS, Q_EPS = 1e-5, 1e-5
MAGIC = 1.5 * 2.0 ** 23
MASKED = -1e30
GONE = -1e30
PICKED = -2e30
SCALE0 = float(D0) ** -0.5
SCALE1 = float(D1) ** -0.5

INPUTS = ["x", "ctx", "ctxT", "w0", "columns", "bo", "w1", "w2", "Wq", "Wk", "Wv", "Wo", "bo1",
          "gk", "gb", "mg", "mu", "md"]

COUNT = {"x_in": 16, "ctxT_in": 16, "ctx_in": 16, "qk_rows": 16 * 2 * len(COMBOS), "max_rows": 32, "out_st": 16,
         "xres": 1, "xnT_ps": 1, "xnT_sb": 1, "qk_ps": 1, "qk_sb": 4, "split_r": 1, "split_mid": 1, "parts": 1,
         "v_ps": 1, "v_sb": 1, "s_ps": 8, "rowmax": 8, "maxT_ps": 1, "max_hi": 1, "max_lo": 1,
         "st_ps": 8, "probs": 8, "pv_ps": NB, "rden": 2, "o_div": 2, "op_ps": 1, "x1": 1, "x1_kept": 1,
         "q1_max": 1, "q1_clip": 1, "q1_rec": 1, "q1_s": 1, "q1_inv": 1, "q1_big": 2, "q1_int": 1, "q1T_ps": 1, "q1b_ps": 1,
         "q1T_sb": 1, "q1b_sb": 1, "h_ps": 2, "h_sb": 2, "c_mid": HC, "c_left": HC, "c_all": HC, "th": 2, "silu": 2,
         "hT_ps": 2, "q2_max": 2, "q2_clip": 1, "q2_rec": 1, "q2_s": 1, "q2_inv": 1, "q2b_ps": 1, "q2b_sb": 1,
         "q2_big": T, "q2_int": T, "f_ps": T, "x2": T, "x2res": 1,
         "g_ps": 1, "g_sb": 1, "p_ps": 4, "p_sb": 4, "u_slot": 1, "m_ps": 1, "m_sb": 1,
         "x3T_ps": 1, "x3T_sb": 1, "a_ps": 1, "x3": T, "x4T_ps": 1, "x4T_sb": 1,
         "lg_ps": 1, "lg_th": 1, "gate": 21, "cT_ps": 1, "cT_sb": 1,
         "gu_ps": MC, "cb_ps": EC // 2, "cb_sb": EC // 2, "g_th": MC, "m_a": MC, "m_b": MC, "m_c": EC, "y_ps": 1, "out_sb": 1}
for _p in ("l1", "l2", "l3", "l4"):
    COUNT.update({_p + "_st": T, _p + "_mv": T, _p + "_ve": 1, _p + "_rs": 1, _p + "_xn": T})


def layers_kernel(nc, a, out):
    ctx = ExitStack()
    with ctx:
        def sb(name, shape, dt=F32):
            return ctx.enter_context(nc.sbuf_tensor(name, shape, dt))

        def ps(name, shape, dt=F32):
            return ctx.enter_context(nc.psum_tensor(name, shape, dt))

        sem = {n: ctx.enter_context(nc.semaphore(n)) for n in COUNT}
        loaded = {n: ctx.enter_context(nc.semaphore("ld_" + n)) for n in ("l0", "queries", "keys", "ffn", "l1", "sums", "moe")}
        s_fill = ctx.enter_context(nc.semaphore("s_fill"))
        s_const = ctx.enter_context(nc.semaphore("s_const"))
        s_setv = ctx.enter_context(nc.semaphore("s_setv"))
        s_setp = ctx.enter_context(nc.semaphore("s_setp"))
        s_seta = ctx.enter_context(nc.semaphore("s_seta"))
        s_gate2 = ctx.enter_context(nc.semaphore("s_gate2"))
        s_bias = ctx.enter_context(nc.semaphore("s_bias"))
        s_rows = ctx.enter_context(nc.semaphore("s_rows"))

        def have(eng, name, b, k=None):
            n = COUNT[name]
            if isinstance(b, int):
                if b >= 0:
                    eng.wait_ge(sem[name], b * n + (n if k is None else k + 1))
            else:
                eng.wait_ge(sem[name], b * n + (n if k is None else k + 1))

        w0 = sb("w0_s", [P, 4, P])
        wq, wk, wv, wo = (w0[:, i, :] for i in range(4))
        columns = sb("columns_s", [P, 3 + 4 * HC + 3 * C1])
        bq, bk, bv = (columns[:, i:i + 1] for i in range(3))
        cw = columns[:, 3:3 + 3 * HC].rearrange("p (c k) -> p c k", k=3)
        cb = columns[:, 3 + 3 * HC:3 + 4 * HC]
        bq1, bk1, bv1 = (columns[:, 3 + 4 * HC + C1 * i:3 + 4 * HC + C1 * i + C1] for i in range(3))
        bqs = sb("bqs", [P, 1])
        bo, bo1 = sb("bo_s", [P, P]), sb("bo1_s", [P, P])
        w1, w2 = sb("w1_s", [P, HC * P]), sb("w2_s", [P, HC * P])
        w1q, w2q = sb("w1q", [P, HC * P], BF16), sb("w2q", [P, HC * P], BF16)
        wabs, wmean, wrec = sb("wabs", [P, 2]), sb("wmean", [P, 2]), sb("wrec", [P, 2])
        Wq, Wk, Wv, Wo = (sb(n, [P, C1, P]) for n in ("Wq_s", "Wk_s", "Wv_s", "Wo_s"))
        qsum, qshift = sb("qsum", [P, C1]), sb("qshift", [P, C1])
        bkd, bvd = sb("bkd", [P, C1, H1]), sb("bvd", [P, C1, H1])
        AT, BV = sb("AT", [P, H1, P]), sb("BV", [P, H1, P])
        csum = sb("csum", [P, B])
        uflat, pflat = sb("uflat", [B, H1 * P]), sb("pflat", [B, H1 * P])
        urow, prow = sb("urow", [H1, B, P]), sb("prow", [H1, B, P])
        arow, brow, brow_n = sb("arow", [H1, P]), sb("brow", [H1, P]), sb("brow_n", [H1, P])
        gk, gb, gbh = sb("gk_s", [P, E]), sb("gb_s", [P, E]), sb("gbh", [P, E])
        mg, mu, md = (sb(n, [P, MC, P]) for n in ("mg_s", "mu_s", "md_s"))
        ident, identb, ones = sb("ident", [P, P]), sb("identb", [P, P], BF16), sb("ones", [P, P])
        mask_s = sb("mask_s", [P, T, KT], BF16)
        mask_t = sb("mask_t", [P, 2, WIN], BF16)
        denom = sb("denom", [P, HG, HG * D0])
        pick = sb("pick", [96, EC, 2, M1], BF16)
        mhalf, eps = sb("mhalf", [P, T]), sb("eps", [P, T])
        repg, repe = sb("repg", [P, T, 8]), sb("repe", [P, T, 8])

        x_s = sb("x_s", [P, T, P])
        xres = sb("xres_s", [P, T, P])
        ctxT = sb("ctxT_s", [P, WIN + S])
        ctx_all = sb("ctx_all", [P, B, S])
        xn = {p: sb(p + "_xn_s", [P, T, P]) for p in ("l1", "l2", "l3", "l4")}
        lst = {p: sb(p + "_st_s", [P, T, 6]) for p in xn}
        lmv = {p: sb(p + "_mv_s", [P, T, 2]) for p in xn}
        lve = {p: sb(p + "_ve_s", [P, T]) for p in xn}
        lrs = {p: sb(p + "_rs_s", [P, T]) for p in xn}
        xnT = sb("xnT", [P, S])
        qk = sb("qk", [P, 2, S])
        rem = sb("rem", [P, 2, S])
        parts = sb("parts_s", [P, PARTS, 2, S], BF16)
        Q = sb("Q", [ROWS + 2, H0, S], BF16)
        K = sb("K", [ROWS + 2, H0, WIN + S], BF16)
        V = sb("V", [P, NB, H0 // HG, HG, HG * D0])
        mx = sb("mx", [P, H0, T])
        nhl = sb("nhl", [H0 * T, 2, P], BF16)
        PT = sb("PT", [P, 2, H0, WIN])
        rden = sb("rden_s", [P, S])
        oT = sb("oT", [P, S])
        x1, x1k = sb("x1_s", [P, T, P]), sb("x1k_s", [P, T, P])
        am1, cl1, rc1, s1, iv1 = (sb(n, [P, T]) for n in ("am1", "cl1", "rc1", "s1", "iv1"))
        big1 = sb("big1", [P, T, P])
        int1 = sb("int1", [P, T, P], BF16)
        q1T = sb("q1T", [P, S], BF16)
        q1b = sb("q1b", [P, S])
        hs = sb("hs", [P, HC, S + 2])
        hc = sb("hc", [P, HC, S])
        th = sb("th_s", [P, HC, S])
        am2, cl2, rc2, s2, iv2 = (sb(n, [P, T]) for n in ("am2", "cl2", "rc2", "s2", "iv2"))
        q2b = sb("q2b", [P, S])
        int2 = sb("int2", [P, HC, S], BF16)
        x2 = sb("x2_s", [P, T, P])
        x2res = sb("x2res_s", [P, T, P])
        ctxn = sb("ctxn", [P, T, P])
        G = sb("G", [P, P])
        PG = sb("PG", [P, H1, P])
        uslot = sb("uslot", [H1, P])
        M = sb("M", [P, P])
        x3T = sb("x3T", [P, S])
        x3 = sb("x3_s", [P, T, P])
        x4T = sb("x4T", [P, S])
        lth = sb("lth", [P, T, E])
        sc = sb("sc", [P, T, E])
        pair_sum, pair_max = sb("pair_sum", [P, T * GROUPS, 2]), sb("pair_max", [P, T * GROUPS, 2])
        cross, same = sb("cross", [P, T * GROUPS]), sb("same", [P, T * GROUPS])
        gsum, gtop, gmark = sb("gsum", [P, T, 16]), sb("gtop", [P, T, 8]), sb("gmark", [P, T, 16])
        gsel = sb("gsel", [P, T, GROUPS])
        emask, etop, emark = sb("emask", [P, T, 32]), sb("etop", [P, T, 8]), sb("emark", [P, T, 32])
        tsum, trec, tnorm = sb("tsum", [P, T]), sb("trec", [P, T]), sb("tnorm", [P, T])
        wsel, comb, cr1, cr2 = (sb(n, [P, T, E]) for n in ("wsel", "comb", "cr1", "cr2"))
        cparts = sb("cparts", [P, T, PARTS, 32], BF16)
        cT = sb("cT", [96, S], BF16)
        gth = sb("gth", [P, RING, S])
        ga = sb("ga", [P, RING, S])
        cbs = sb("cbs", [P, 4, S])
        inter = sb("inter", [P, MC, S])
        y = sb("y", [P, T, P])

        A = [ps(f"A{i}", [P, 512]) for i in range(2)]
        O = ps("O", [P, 2, S])
        F = [ps(f"F{i}", [P, 512]) for i in range(2)]
        MB = [ps(f"M{i}", [P, 512]) for i in range(3)]

        R = [MB[0], MB[1], F[0]]
        CB = [MB[2][:, :], O[:, :, :].rearrange("p a s -> p (a s)")]
        Y = F[1]
        OV = [O[:, 0, :], MB[2][:, 0:S]]

        block = ctx.enter_context(nc.Block())

        FFN_LOADS = [(w1, "w1"), (w2, "w2")]
        L1_LOADS = [(Wv, "Wv"), (Wo, "Wo")]
        MOE_LOADS = [(gk, "gk"), (mg, "mg"), (mu, "mu"), (md, "md")]
        N_L0 = 16 * 3
        N_FFN = 16 * len(FFN_LOADS)
        N_L1 = 16 * len(L1_LOADS)
        N_SUMS = 16 * 2
        N_MOE = 16 * (len(MOE_LOADS) + 1)
        FILLS = ["mhalf", "eps", "pad", "ident", "identb", "K_empty", "mask_s", "mask_t", "K", "V", "denom", "ones",
                 "pick", "cparts"] + ["denom_own"] * HG
        CONSTS = ["ident", "identb"] + ["mask_s"] * 10 + ["mask_t"] * 3 + ["pick"] * PARTS

        def load(eng, group, tensors):
            for t_, n in tensors:
                eng.dma_start(t_[tuple([slice(None)] * len(t_.shape))], a[n]).then_inc(loaded[group], 16)

        def wait_made(eng, sem_, steps, name):
            eng.wait_ge(sem_, len(steps) - steps[::-1].index(name))

        SV_WQ = 3 + C1
        SV_ABS = SV_WQ + 2
        SV_SCALES = SV_ABS + 2
        SV_BD = SV_SCALES + 12 + 7
        SV_ROWS = SV_BD + 3
        SV_END = SV_ROWS + 9

        @block.sync
        def _(sp):
            def load_x(b):
                have(sp, "xres", b - 1)
                have(sp, "l1_xn", b - 1)
                sp.dma_start(x_s[:, :, :], a["x"][b].rearrange("(t p) d -> p t d", p=P)).then_inc(sem["x_in"], 16)

            def load_ctxT(b):
                have(sp, "v_ps", b - 1)
                sp.dma_start(ctxT[:, WIN:], a["ctxT"][b]).then_inc(sem["ctxT_in"], 16)

            def load_ctx(b):
                have(sp, "g_ps", b - 1)
                sp.dma_start(ctxn[:, :, :], a["ctx"][b].rearrange("(t p) d -> p t d", p=P)).then_inc(sem["ctx_in"], 16)

            def spread_parts(b):
                have(sp, "st_ps", b - 1)
                for part, made in enumerate(("qk_sb", "split_mid", "parts")):
                    have(sp, made, b, 0)
                    for c, (pq, _) in enumerate(COMBOS[:-1]):
                        if pq == part:
                            sp.dma_start(Q[D0 * c:D0 * c + D0, :, :], parts[:, pq, 0, :]).then_inc(sem["qk_rows"], 16)
                    if part == 0:
                        have(sp, "qk_sb", b, 1)
                    for c, (_, pk) in enumerate(COMBOS[:-1]):
                        if pk == part:
                            sp.dma_start(K[D0 * c:D0 * c + D0, :, WIN:], parts[:, pk, 1, :])\
                                .then_inc(sem["qk_rows"], 16)

            def spread_max(b):
                have(sp, "max_lo", b)
                for part in range(2):
                    sp.dma_start(Q[ROWS + part:ROWS + part + 1, :, :], nhl[:, part, :]).then_inc(sem["max_rows"], 16)

            def store(b):
                have(sp, "out_sb", b)
                sp.dma_start(out[b].rearrange("(t p) d -> p t d", p=P), y[:, :, :]).then_inc(sem["out_st"], 16)

            load_x(0)
            load(sp, "l0", [(w0, "w0"), (columns, "columns")])
            sp.dma_start(bo[:, :], a["bo"].partition_broadcast(P)).then_inc(loaded["l0"], 16)
            wait_made(sp, s_fill, FILLS, "pad")
            load_ctxT(0)
            wait_made(sp, s_fill, FILLS, "K")

            def regroup():
                sp.wait_ge(s_setv, SV_ROWS + 8)
                for src, dst in ((uflat, urow), (pflat, prow)):
                    for b_ in range(B):
                        sp.dma_start(dst[:, b_, :], src[b_:b_ + 1, :]).then_inc(s_rows, 16)

            def iteration(t, nxt=True, nxt2=True, stage2=True):
                if nxt:
                    spread_parts(t + 1)
                if nxt2:
                    load_x(t + 2)
                    load_ctxT(t + 2)
                if nxt:
                    load_ctx(t + 1)
                if nxt:
                    spread_max(t + 1)
                if stage2:
                    store(t - 1)

            spread_parts(0)
            sp.dma_start(bo1[:, :], a["bo1"].partition_broadcast(P)).then_inc(loaded["sums"], 16)
            sp.dma_start(ctx_all[:, :, :], a["ctxT"].rearrange("b p s -> p b s")).then_inc(loaded["sums"], 16)
            load_x(1)
            load_ctxT(1)
            load_ctx(0)
            spread_max(0)
            spread_parts(1)
            load_x(2)
            load_ctxT(2)
            load_ctx(1)
            load(sp, "moe", MOE_LOADS)
            sp.dma_start(gb[:, :], a["gb"].partition_broadcast(P)).then_inc(loaded["moe"], 16)
            regroup()
            spread_max(1)
            iteration(1)
            with sp.Fori(2, B - 2) as t:
                iteration(t)
            iteration(B - 2, nxt2=False)
            iteration(B - 1, nxt=False, nxt2=False)
            store(B - 1)
            have(sp, "out_st", B - 1)

        @block.gpsimd
        def _(pool):
            done = [0]

            def step(ins):
                assert done[0] < len(CONSTS)
                done[0] += 1
                ins.then_inc(s_const, 1)
                pool.wait_ge(s_const, done[0])

            def make_idents():
                for m_, name in ((ident, "ident"), (identb, "identb")):
                    wait_made(pool, s_fill, FILLS, name)
                    step(pool.affine_select(out=m_[:, :], in_=m_[:, :], compare_op=ALU.not_equal, fill=1.0, base=0,
                                            pattern=[[-1, P]], channel_multiplier=1))

            def make_masks():
                wait_made(pool, s_fill, FILLS, "mask_s")
                for j in range(P // QT):
                    m_ = mask_s[QT * j:QT * j + QT, :, :]
                    step(pool.affine_select(out=m_, in_=m_, compare_op=ALU.is_ge, fill=MASKED, base=0,
                                            pattern=[[0, T], [1, KT]], channel_multiplier=-1))
                    step(pool.affine_select(out=m_, in_=m_, compare_op=ALU.is_ge, fill=MASKED, base=WIN,
                                            pattern=[[0, T], [-1, KT]], channel_multiplier=1))
                    if QT * j < WIN:
                        m_ = mask_s[QT * j:QT * j + QT, 0, :]
                        step(pool.affine_select(out=m_, in_=m_, compare_op=ALU.is_ge, fill=MASKED, base=QT * j - WIN,
                                                pattern=[[1, KT]], channel_multiplier=0))
                wait_made(pool, s_fill, FILLS, "mask_t")
                step(pool.affine_select(out=mask_t[:, :, :], in_=mask_t[:, :, :], compare_op=ALU.is_ge, fill=MASKED,
                                        base=0, pattern=[[0, 2], [-1, WIN]], channel_multiplier=1))
                step(pool.affine_select(out=mask_t[:, :, :], in_=mask_t[:, :, :], compare_op=ALU.is_ge, fill=MASKED,
                                        base=WIN, pattern=[[0, 2], [1, WIN]], channel_multiplier=-1))
                step(pool.affine_select(out=mask_t[:, 0, :], in_=mask_t[:, 0, :], compare_op=ALU.is_ge, fill=MASKED,
                                        base=-WIN, pattern=[[0, WIN]], channel_multiplier=1))

            def make_pick():
                wait_made(pool, s_fill, FILLS, "pick")
                for k in range(PARTS):
                    m_ = pick[32 * k:32 * k + 32, :, :, :]
                    step(pool.affine_select(out=m_, in_=m_, compare_op=ALU.is_equal, fill=0.0, base=0,
                                            pattern=[[-2, EC], [-1, 2], [0, M1]], channel_multiplier=1))
                assert done[0] == len(CONSTS), done[0]

            def norm(p, b):
                have(pool, p + "_mv", b)
                pool.tensor_tensor(lve[p][:, :], lmv[p][:, :, 1], eps[:, :], ALU.add).then_inc(sem[p + "_ve"], 1)
                have(pool, p + "_ve", b)
                have(pool, p + "_xn", b - 1)
                pool.tensor_tensor(lrs[p][:, :], lve[p][:, :], mhalf[:, :], ALU.pow).then_inc(sem[p + "_rs"], 1)

            def residual(b):
                have(pool, "x_in", b)
                have(pool, "x1", b - 1)
                pool.tensor_tensor(xres[:, :, :], x_s[:, :, :], bo[:, None, :].broadcast_to([P, T, P]), ALU.add)\
                    .then_inc(sem["xres"], 1)

            def split_rem(b):
                have(pool, "qk_sb", b)
                pool.tensor_tensor(rem[:, :, :], qk[:, :, :], parts[:, 0, :, :], ALU.subtract).then_inc(sem["split_r"], 1)

            def split_low(b):
                have(pool, "split_mid", b)
                pool.tensor_tensor(parts[:, 2, :, :], rem[:, :, :], parts[:, 1, :, :], ALU.subtract)\
                    .then_inc(sem["parts"], 1)

            def residual2(b):
                have(pool, "x2", b)
                have(pool, "x3", b - 1)
                pool.tensor_tensor(x2res[:, :, :], x2[:, :, :], bo1[:, None, :].broadcast_to([P, T, P]), ALU.add)\
                    .then_inc(sem["x2res"], 1)

            def weigh(b):
                for c in range(EC):
                    have(pool, "m_b", b, c)
                    have(pool, "cb_sb", b, c // 2)
                    pool.tensor_tensor(inter[:, c, :], inter[:, c, :], cbs[:, c % 4, :], ALU.mult)\
                        .then_inc(sem["m_c"], 1)

            def iteration(t, stage1=True, stage2=True, nxt=True):
                if nxt:
                    norm("l1", t + 1)
                if stage2:
                    norm("l3", t - 1)
                    residual2(t - 1)
                if nxt:
                    split_rem(t + 1)
                    split_low(t + 1)
                if stage2:
                    norm("l4", t - 1)
                if stage1:
                    norm("l2", t)
                if nxt:
                    residual(t + 1)
                if stage2:
                    weigh(t - 1)

            make_idents()
            norm("l1", 0)
            make_masks()
            split_rem(0)
            split_low(0)
            make_pick()
            pool.wait_ge(s_bias, 2)
            residual(0)
            iteration(0, stage2=False)
            pool.wait_ge(loaded["sums"], N_SUMS)
            iteration(1)
            with pool.Fori(2, B - 1) as t:
                iteration(t)
            iteration(B - 1, nxt=False)
            iteration(B, stage1=False, nxt=False)

        @block.scalar
        def _(act):
            def front(b):
                have(act, "xnT_ps", b)
                have(act, "qk_ps", b - 1)
                nc.scalar.activation(xnT[:, :], A[1][:, 0:S], ACT.Copy).then_inc(sem["xnT_sb"], 1)
                have(act, "qk_ps", b)
                have(act, "qk_rows", b - 1)
                for high in (True, False):
                    for i, (bias, scale) in enumerate(((bqs[:, :], SCALE0), (bk, 1.0))):
                        nc.scalar.activation(parts[:, 0, i, :] if high else qk[:, i, :], A[1][:, S * i:S * i + S],
                                             ACT.Identity, bias=bias, scale=scale).then_inc(sem["qk_sb"], 1)

            def split_mid(b):
                have(act, "split_r", b)
                nc.scalar.activation(parts[:, 1, :, :], rem[:, :, :], ACT.Copy).then_inc(sem["split_mid"], 1)

            def spread_mid(b, i):
                have(act, "split_mid", b)
                have(act, "st_ps", b - 1)
                c = len(COMBOS) - 1
                dst = Q[D0 * c:D0 * c + D0, :, :] if i == 0 else K[D0 * c:D0 * c + D0, :, WIN:]
                act.dma_start(dst, parts[:, 1, i, :]).then_inc(sem["qk_rows"], 16)

            def exps(b, first, last):
                for k in range(first, last):
                    n = k // 2
                    have(act, "st_ps", b, k)
                    have(act, "pv_ps", b, n - 2) if n >= 2 else have(act, "pv_ps", b - 1, n + 2)
                    nc.scalar.activation(PT[:, n % 2, 8 * (k % 2):8 * (k % 2) + 8, :].rearrange("p h q -> p (h q)"),
                                         A[k % 2][:, :], ACT.Exp).then_inc(sem["probs"], 1)

            def ffn_in(b):
                have(act, "x1", b)
                have(act, "x2", b - 1)
                nc.scalar.activation(x1k[:, :, :], x1[:, :, :], ACT.Copy).then_inc(sem["x1_kept"], 1)
                have(act, "q1T_ps", b)
                have(act, "h_ps", b - 1)
                nc.scalar.activation(q1T[:, :], F[0][:, 0:P].bitcast(BF16), ACT.Copy).then_inc(sem["q1T_sb"], 1)
                have(act, "q1b_ps", b)
                have(act, "h_sb", b - 1)
                nc.scalar.activation(q1b[:, :], MB[1][:, 0:S], ACT.Copy).then_inc(sem["q1b_sb"], 1)

            def ffn_mid(b):
                for c in range(HC):
                    have(act, "h_sb", b, c // 2)
                    have(act, "hT_ps", b - 1)
                    have(act, "q2_big", b - 1)
                    nc.scalar.activation(hc[:, c, :], hs[:, c, 1:S + 1], ACT.Identity, bias=cb[:, c:c + 1],
                                         scale=cw[:, c, 1:2]).then_inc(sem["c_mid"], 1)

            def ffn_tanh(b, half):
                have(act, "c_all", b, 2 * half + 1)
                if half == 0:
                    have(act, "q2_int", b - 1)
                nc.scalar.activation(th[:, 2 * half:2 * half + 2, :], hc[:, 2 * half:2 * half + 2, :], ACT.Tanh, scale=0.5)\
                    .then_inc(sem["th"], 1)

            def ffn_out(b):
                have(act, "q2b_ps", b)
                have(act, "q2_big", b - 1)
                nc.scalar.activation(q2b[:, :], F[0][:, 0:S], ACT.Copy).then_inc(sem["q2b_sb"], 1)

            def gram(b):
                have(act, "g_ps", b)
                have(act, "p_ps", b - 1)
                nc.scalar.activation(G[:, :], F[0][:, 0:P], ACT.Copy).then_inc(sem["g_sb"], 1)

            def gram_values(b, k):
                have(act, "p_ps", b, k)
                have(act, "m_ps", b - 1)
                nc.scalar.activation(PG[:, 4 * k:4 * k + 4, :].rearrange("p h j -> p (h j)"), F[1 - k % 2][:, :],
                                     ACT.Copy).then_inc(sem["p_sb"], 1)

            def attend(b):
                have(act, "x3T_ps", b)
                have(act, "a_ps", b - 1)
                nc.scalar.activation(x3T[:, :], MB[1][:, 0:S], ACT.Copy, bias=1.0).then_inc(sem["x3T_sb"], 1)

            def tokens4(b):
                have(act, "x4T_ps", b)
                have(act, "gu_ps", b - 1)
                nc.scalar.activation(x4T[:, :], MB[0][:, 0:S], ACT.Copy).then_inc(sem["x4T_sb"], 1)

            def logits(b):
                have(act, "lg_ps", b)
                have(act, "gate", b - 1)
                nc.scalar.activation(lth[:, :, :].rearrange("p t e -> p (t e)"), MB[1][:, 0:T * E], ACT.Tanh,
                                     scale=0.5).then_inc(sem["lg_th"], 1)

            def experts(b, c):
                have(act, "gu_ps", b, c)
                have(act, "m_a", b, c - RING) if c >= RING else have(act, "m_a", b - 1)
                nc.scalar.activation(gth[:, c % RING, :], R[c % RING][:, 0:S], ACT.Tanh, scale=0.5)\
                    .then_inc(sem["g_th"], 1)

            def weights(b, k):
                have(act, "cb_ps", b, k)
                have(act, "m_c", b, 2 * k - 3) if k >= 2 else have(act, "m_c", b - 1)
                nc.scalar.activation(cbs[:, 2 * (k % 2):2 * (k % 2) + 2, :].rearrange("p c s -> p (c s)"), CB[k % 2], ACT.Copy)\
                    .then_inc(sem["cb_sb"], 1)

            def moe(b):
                for c in range(2, AHEAD):
                    experts(b, c)
                have(act, "cT_ps", b)
                have(act, "cb_ps", b - 1)
                nc.scalar.activation(cT[:, :], MB[2][0:96, 0:P].bitcast(BF16), ACT.Copy).then_inc(sem["cT_sb"], 1)
                weights(b, 0)
                weights(b, 1)
                for c in range(AHEAD, MC):
                    experts(b, c)
                    if c in (AHEAD, AHEAD + 2):
                        weights(b, (c - AHEAD) // 2 + 2)

            load(act, "queries", [(Wq, "Wq")])
            load(act, "keys", [(Wk, "Wk")])
            act.wait_ge(loaded["l0"], N_L0)
            nc.scalar.activation(bqs[:, :], bq, ACT.Copy, scale=SCALE0).then_inc(s_seta, 1)
            act.wait_ge(s_seta, 1)

            def setup():
                for k in range(8):
                    r, odd = k // 2, k % 2
                    act.wait_ge(s_setp, (1, 2, 4, 5)[r])
                    dst = (AT if r < 2 else BV)[:, 8 * (r % 2) + odd:8 * (r % 2) + 8:2, :]
                    nc.scalar.activation(dst, (MB if r % 2 == 0 else F)[odd][:, :].rearrange("p (h j) -> p h j", j=P), ACT.Copy, scale=SCALE1 if k < 4 else 1.0)\
                        .then_inc(s_seta, 1)

            def iteration(t, stage1=True, stage2=True, nxt=True):
                if stage2:
                    ffn_in(t - 1)
                    ffn_mid(t - 1)
                if stage1:
                    exps(t, 0, 2)
                if stage2:
                    ffn_tanh(t - 1, 0)
                if stage1:
                    exps(t, 2, 4)
                if stage2:
                    ffn_tanh(t - 1, 1)
                if stage1:
                    exps(t, 4, 2 * NB)
                if stage2:
                    ffn_out(t - 1)
                if nxt:
                    front(t + 1)
                if stage1:
                    gram(t)
                if stage2:
                    attend(t - 1)
                if nxt:
                    split_mid(t + 1)
                    spread_mid(t + 1, 0)
                if stage1:
                    gram_values(t, 0)
                    gram_values(t, 1)
                if nxt:
                    spread_mid(t + 1, 1)
                if stage1:
                    gram_values(t, 2)
                if stage2:
                    tokens4(t - 1)
                if stage1:
                    gram_values(t, 3)
                if stage2:
                    logits(t - 1)
                    experts(t - 1, 0)
                    experts(t - 1, 1)
                if stage2:
                    moe(t - 1)

            front(0)
            load(act, "ffn", FFN_LOADS)
            load(act, "l1", L1_LOADS)
            split_mid(0)
            wait_made(act, s_fill, FILLS, "K")
            spread_mid(0, 0)
            spread_mid(0, 1)
            setup()
            iteration(0, stage2=False)
            iteration(1)
            with act.Fori(2, B - 1) as t:
                iteration(t)
            iteration(B - 1, nxt=False)
            iteration(B, stage1=False, nxt=False)

        @block.tensor
        def _(pe):
            def front(b):
                have(pe, "l1_xn", b)
                have(pe, "probs", b - 1)
                for t in range(T):
                    last = pe.transpose(A[1][:, P * t:P * t + P], xn["l1"][:, t, :], ident[:, :])
                last.then_inc(sem["xnT_ps"], 1)

            def values_proj(b):
                have(pe, "ctxT_in", b)
                have(pe, "probs", b - 1)
                for n in range(NB):
                    last = pe.matmul(A[0][:, P * n:P * n + P], ctxT[:, WIN * n:WIN * n + KEYS], wv,
                                     start=True, stop=True)
                last.then_inc(sem["v_ps"], 1)

            def qk_proj(b):
                have(pe, "xnT_sb", b)
                pe.matmul(A[1][:, 0:S], wq, xnT[:, :], start=True, stop=True)
                pe.matmul(A[1][:, S:2 * S], wk, ctxT[:, WIN:], start=True, stop=True).then_inc(sem["qk_ps"], 1)

            def row_scores(b, first, last):
                if first == 0:
                    have(pe, "qk_rows", b)
                for k in range(first, last):
                    t, hg = k // 4, k % 4
                    bank = A[(k + 1) % 2]
                    if k == 0:
                        have(pe, "qk_sb", b)
                    elif k == 1:
                        have(pe, "v_sb", b)
                    else:
                        have(pe, "rowmax", b, k - 2)
                    pe.matmul(bank[:, 0:HG * KT], identb[:, :], mask_s[:, t:t + 1, :].broadcast_to([P, HG, KT]),
                              start=True, stop=False, skip_group_check=True)
                    for h in range(HG):
                        for j in range(P // QT):
                            q0 = P * t + QT * j
                            tile = pe.matmul(bank[QT * j:QT * j + QT, KT * h:KT * h + KT],
                                             Q[0:ROWS, HG * hg + h, q0:q0 + QT], K[0:ROWS, HG * hg + h, q0:q0 + KT],
                                             start=False, stop=(h == HG - 1), skip_group_check=True)
                    tile.then_inc(sem["s_ps"], 1)

            def max_rows(b):
                have(pe, "rowmax", b)
                pe.transpose(A[1][0:H0 * T, 0:P], mx[:, :, :].rearrange("p h t -> p (h t)"), ident[:, :])\
                    .then_inc(sem["maxT_ps"], 1)

            def key_scores(b, k):
                n, half = k // 2, k % 2
                if k == 0:
                    have(pe, "max_rows", b)
                if k == 1:
                    have(pe, "max_lo", b)
                if k >= 2:
                    have(pe, "probs", b, k - 2)
                bank = A[k % 2]
                pe.matmul(bank[:, :], identb[:, :], mask_t[:, min(n, 1):min(n, 1) + 1, :].broadcast_to([P, 8, WIN]),
                          start=True, stop=False, skip_group_check=True)
                for h in range(8):
                    last = pe.matmul(bank[:, WIN * h:WIN * h + WIN], K[:, 8 * half + h, WIN * n:WIN * n + KEYS],
                                     Q[:, 8 * half + h, WIN * n:WIN * n + WIN], start=False, stop=(h == 7),
                                     skip_group_check=True)
                last.then_inc(sem["st_ps"], 1)

            def values(b, n, first=0, last=2):
                have(pe, "probs", b, 2 * n + 1)
                if n == 0:
                    have(pe, "v_sb", b)
                    have(pe, "cb_sb", b - 2) if not isinstance(b, int) or b >= 2 else None
                    have(pe, "x1", b - 1)
                if n == 2:
                    have(pe, "cb_sb", b - 2) if not isinstance(b, int) or b >= 2 else None
                for what in range(first, last):
                    for h in range(HG):
                        for g in range(H0 // HG):
                            w = V[:, n, g, h, :] if what == 0 else denom[:, h, :]
                            c = 2 * WIN * what + WIN * (n % 2)
                            tile = pe.matmul(OV[n // 2][32 * g:32 * g + 32, c:c + WIN], w,
                                             PT[:, n % 2, HG * g + h, :], start=(h == 0), stop=(h == HG - 1),
                                             skip_group_check=True)
                if last == 2:
                    tile.then_inc(sem["pv_ps"], 1)

            def out_proj(b):
                have(pe, "o_div", b)
                for t in range(T):
                    last = pe.matmul(O[:, 0, P * t:P * t + P], oT[:, P * t:P * t + P], wo, start=True, stop=True)
                last.then_inc(sem["op_ps"], 1)

            def ffn_in(b):
                have(pe, "q1_int", b)
                have(pe, "m_b", b - 1)
                have(pe, "p_sb", b)
                for t in range(T):
                    last = pe.transpose(F[0][:, 0:P].bitcast(BF16)[:, P * t:P * t + P], int1[:, t, :], identb[:, :])
                last.then_inc(sem["q1T_ps"], 1)
                have(pe, "q1_inv", b)
                for t in range(T):
                    last = pe.matmul(MB[1][:, P * t:P * t + P], iv1[:, t:t + 1].broadcast_to([P, P]), ident[:, :],
                                     start=True, stop=True)
                last.then_inc(sem["q1b_ps"], 1)

            def ffn_up(b):
                have(pe, "q1T_sb", b)
                for f in range(2):
                    if f == 1:
                        have(pe, "out_sb", b - 1)
                    for i in range(2):
                        c = 2 * f + i
                        last = pe.matmul(F[f][:, S * i:S * i + S], w1q[:, P * c:P * c + P], q1T[:, :],
                                         start=True, stop=True)
                    last.then_inc(sem["h_ps"], 1)

            def ffn_turn(b):
                have(pe, "silu", b)
                for t in range(T):
                    have(pe, "h_sb", b, t)
                    for c in range(HC):
                        last = pe.transpose(F[t][:, P * c:P * c + P], hc[:, c, P * t:P * t + P], ident[:, :])
                    last.then_inc(sem["hT_ps"], 1)

            def ffn_scale(b):
                have(pe, "q2_s", b)
                have(pe, "q2_max", b, 0)
                for t in range(T):
                    last = pe.matmul(F[0][:, P * t:P * t + P], s2[:, t:t + 1].broadcast_to([P, P]), ident[:, :],
                                     start=True, stop=True)
                last.then_inc(sem["q2b_ps"], 1)

            def ffn_down(b):
                have(pe, "q2_max", b)
                for t in range(T):
                    have(pe, "q2_int", b, t)
                    for c in range(HC):
                        last = pe.matmul(F[1][:, P * t:P * t + P], int2[:, c, P * t:P * t + P], w2q[:, P * c:P * c + P],
                                         start=(c == 0), stop=(c == HC - 1), skip_group_check=True)
                    last.then_inc(sem["f_ps"], 1)

            def gram(b):
                have(pe, "ctx_in", b)
                have(pe, "q2b_sb", b - 1)
                have(pe, "m_b", b - 2) if not isinstance(b, int) or b >= 2 else None
                for t in range(T):
                    last = pe.matmul(F[0][:, 0:P], ctxn[:, t, :], ctxn[:, t, :], start=(t == 0), stop=(t == T - 1))
                last.then_inc(sem["g_ps"], 1)

            def gram_values(b, k):
                if k == 0:
                    have(pe, "g_sb", b)
                    have(pe, "x2", b - 1)
                if k >= 2:
                    have(pe, "p_sb", b, k - 2)
                pe.matmul(F[1 - k % 2][:, :], G[:, :], BV[:, 4 * k:4 * k + 4, :], start=True, stop=True)\
                    .then_inc(sem["p_ps"], 1)

            def mix(b, first, last):
                if first == 0:
                    have(pe, "p_sb", b)
                    have(pe, "m_b", b - 1)
                for h in range(first, last):
                    pe.matmul(MB[0][:, 0:P], AT[:, h, :], PG[:, h, :], start=(h == 0), stop=False)
                if last == H1:
                    have(pe, "u_slot", b)
                    pe.matmul(MB[0][:, 0:P], uslot[:, :], brow[:, :], start=False, stop=False)
                    pe.matmul(MB[0][:, 0:P], arow[:, :], prow[:, b, :], start=False, stop=True).then_inc(sem["m_ps"], 1)

            def turn3(b):
                have(pe, "l3_xn", b)
                have(pe, "q1b_sb", b)
                for t in range(T):
                    last = pe.transpose(MB[1][:, P * t:P * t + P], xn["l3"][:, t, :], ident[:, :])
                last.then_inc(sem["x3T_ps"], 1)

            def attend(b):
                have(pe, "x3T_sb", b)
                have(pe, "m_sb", b)
                have(pe, "o_div", b + 1) if not isinstance(b, int) or b < B - 1 else None
                for t in range(T):
                    last = pe.matmul(MB[2][:, P * t:P * t + P], x3T[:, P * t:P * t + P], M[:, :], start=True, stop=True)
                last.then_inc(sem["a_ps"], 1)

            def route(b):
                have(pe, "l4_xn", b)
                for t in range(T):
                    last = pe.transpose(MB[0][:, P * t:P * t + P], xn["l4"][:, t, :], ident[:, :])
                last.then_inc(sem["x4T_ps"], 1)

            def logits(b):
                have(pe, "x4T_sb", b)
                for t in range(T):
                    last = pe.matmul(MB[1][:, E * t:E * t + E], x4T[:, P * t:P * t + P], gk[:, :], start=True, stop=True)
                last.then_inc(sem["lg_ps"], 1)

            def gate_up(b, c):
                if c == 1:
                    have(pe, "lg_th", b)
                if c >= RING:
                    have(pe, "m_b", b, c - RING)
                elif c == 2:
                    have(pe, "p_sb", b + 1) if not isinstance(b, int) or b < B - 1 else None
                bank = R[c % RING]
                pe.matmul(bank[:, 0:S], mg[:, c, :], x4T[:, :], start=True, stop=True)
                pe.matmul(bank[:, S:2 * S], mu[:, c, :], x4T[:, :], start=True, stop=True)\
                    .then_inc(sem["gu_ps"], 1)

            def turn_weights(b):
                have(pe, "gate", b)
                for t in range(T):
                    last = pe.transpose(MB[2][0:96, 0:P].bitcast(BF16)[:, P * t:P * t + P],
                                        cparts[:, t, :, :].rearrange("p k e -> p (k e)"), identb[:, :])
                last.then_inc(sem["cT_ps"], 1)

            def combine(b, k):
                if k == 0:
                    have(pe, "cT_sb", b)
                elif k == 1:
                    have(pe, "x1", b + 1) if not isinstance(b, int) or b < B - 1 else None
                else:
                    have(pe, "cb_sb", b, k - 2)
                for i in range(2):
                    last = pe.matmul(CB[k % 2][:, S * i:S * i + S], pick[:, 2 * k + i, :, :].rearrange("p a m -> p (a m)"),
                                     cT[:, :], start=True, stop=True)
                last.then_inc(sem["cb_ps"], 1)

            def down(b, c):
                if c < EC:
                    have(pe, "m_c", b, c)
                else:
                    have(pe, "m_b", b)
                for t in range(T):
                    last = pe.matmul(Y[:, P * t:P * t + P], inter[:, c, P * t:P * t + P], md[:, c, :],
                                     start=(c == 0 and t == 0), stop=(c == MC - 1), skip_group_check=True)
                if c == MC - 1:
                    last.then_inc(sem["y_ps"], 1)

            def experts(b, rows):
                def scores(k):
                    if rows is not None:
                        row_scores(rows, k, k + 1)

                scores(0)
                gate_up(b, 2)
                scores(1)
                gate_up(b, 3)
                scores(2)
                gate_up(b, 4)
                scores(3)
                turn_weights(b)
                gate_up(b, 5)
                combine(b, 0)
                combine(b, 1)
                scores(4)
                gate_up(b, 6)
                down(b, 0)
                combine(b, 2)
                scores(5)
                down(b, 1)
                gate_up(b, 7)
                down(b, 2)
                combine(b, 3)
                down(b, 3)
                scores(6)
                gate_up(b, 8)
                down(b, 4)
                scores(7)
                down(b, 5)
                down(b, 6)
                if rows is not None:
                    max_rows(rows)
                down(b, 7)
                down(b, 8)

            def setup_bo():
                pe.matmul(O[:, 0, 0:P], bv.broadcast_to([P, P]), wo, start=True, stop=True).then_inc(s_bias, 1)

            def setup_products(first, last):
                pe.wait_ge(loaded["keys"], 16) if first == 0 else pe.wait_ge(loaded["l1"], N_L1)
                pe.wait_ge(s_setv, SV_WQ)
                for k in range(first, last):
                    lhs, rhs = (Wk, Wq) if k < 2 else (Wv, Wo)
                    pair = MB if k % 2 == 0 else F
                    if k >= 2:
                        pe.wait_ge(s_seta, 2 * k - 1)
                    for i in range(4):
                        c = 4 * (k % 2) + i
                        for odd in range(2):
                            p0 = D1 * odd
                            last = pe.matmul(pair[odd][:, P * i:P * i + P], lhs[p0:p0 + D1, c, :], rhs[p0:p0 + D1, c, :],
                                             start=True, stop=True, skip_group_check=True)
                    last.then_inc(s_setp, 1)

            def setup_scales():
                pe.wait_ge(s_setv, SV_ABS)
                wait_made(pe, s_fill, FILLS, "denom_own")
                pe.matmul(MB[2][:, 0:2], ones[:, :], wabs[:, :], start=True, stop=True).then_inc(s_setp, 1)

            def setup_bias_rows():
                pe.wait_ge(s_seta, 9)
                pe.wait_ge(s_setv, SV_BD)
                for i, (d_, w_) in enumerate(((bkd, Wq), (bvd, Wo))):
                    for c in range(C1):
                        last = pe.matmul(MB[1][0:H1, P * i:P * i + P], d_[:, c, :], w_[:, c, :], start=(c == 0),
                                         stop=(c == C1 - 1))
                last.then_inc(s_setp, 1)

            def setup_sum_rows():
                pe.wait_ge(s_setv, SV_ROWS)
                for k in range(8):
                    src = AT if k < 4 else BV
                    bank = MB[k % 2]
                    if k >= 2:
                        pe.wait_ge(s_setv, SV_ROWS + k - 1)
                    pe.matmul(bank[0:B, :], csum[:, :], src[:, 4 * (k % 4):4 * (k % 4) + 4, :], start=True, stop=True)\
                        .then_inc(s_setp, 1)
                pe.wait_ge(s_setv, SV_ROWS + 8)

            def iteration(t, stage1=True, stage2=True, nxt=True):
                if stage2:
                    ffn_in(t - 1)
                    mix(t - 1, 0, 2)
                    ffn_up(t - 1)
                    mix(t - 1, 2, 8)
                if stage1:
                    for k in range(2):
                        key_scores(t, k)
                if stage2:
                    mix(t - 1, 8, 12)
                if stage1:
                    for k in range(2, 4):
                        key_scores(t, k)
                    values(t, 0)
                    key_scores(t, 4)
                    key_scores(t, 5)
                if stage2:
                    ffn_turn(t - 1)
                if stage1:
                    values(t, 1)
                    key_scores(t, 6)
                    key_scores(t, 7)
                if stage2:
                    ffn_scale(t - 1)
                if stage1:
                    values(t, 2)
                if nxt:
                    front(t + 1)
                if stage1:
                    values(t, 3, 0, 1)
                if stage2:
                    ffn_down(t - 1)
                if stage1:
                    values(t, 3, 1, 2)
                if nxt:
                    qk_proj(t + 1)
                if stage1:
                    if not stage2:
                        pe.wait_ge(s_seta, 9)
                    gram(t)
                if stage2:
                    mix(t - 1, 12, H1)
                    turn3(t - 1)
                if nxt:
                    values_proj(t + 1)
                if stage2:
                    attend(t - 1)
                if stage1:
                    gram_values(t, 0)
                    gram_values(t, 1)
                    out_proj(t)
                    gram_values(t, 2)
                if stage2:
                    route(t - 1)
                if stage1:
                    gram_values(t, 3)
                if stage2:
                    logits(t - 1)
                    gate_up(t - 1, 0)
                    gate_up(t - 1, 1)
                if stage2:
                    experts(t - 1, t + 1 if nxt else None)
                elif nxt:
                    wait_made(pe, s_const, CONSTS, "pick")
                    setup_sum_rows()
                    row_scores(t + 1, 0, 8)
                    max_rows(t + 1)

            wait_made(pe, s_const, CONSTS, "identb")
            front(0)
            pe.wait_ge(loaded["l0"], N_L0)
            values_proj(0)
            qk_proj(0)
            setup_bo()
            setup_products(0, 2)
            wait_made(pe, s_const, CONSTS, "mask_t")
            row_scores(0, 0, 8)
            max_rows(0)
            setup_scales()
            setup_products(2, 4)
            setup_bias_rows()
            pe.wait_ge(s_setv, SV_SCALES)
            iteration(0, stage2=False)
            iteration(1)
            with pe.Fori(2, B - 1) as t:
                iteration(t)
            iteration(B - 1, nxt=False)
            iteration(B, stage1=False, nxt=False)

        @block.vector
        def _(dve):
            v = nc.vector
            setv = [0]

            def step(ins):
                setv[0] += 1
                ins.then_inc(s_setv, 1)

            def norm_stats(p, src, b, after=None):
                for t in range(T):
                    if after:
                        have(dve, after, b, t)
                    v.bn_stats(lst[p][:, t, :], src[:, t, :]).then_inc(sem[p + "_st"], 1)
                dve.drain()
                for t in range(T):
                    v.bn_aggr(lmv[p][:, t, :], lst[p][:, t, :]).then_inc(sem[p + "_mv"], 1)

            def norm_apply(p, src, b):
                have(dve, p + "_rs", b)
                for t in range(T):
                    v.tensor_scalar(xn[p][:, t, :], src[:, t, :], lmv[p][:, t, 0:1], lrs[p][:, t:t + 1],
                                    ALU.subtract, ALU.mult).then_inc(sem[p + "_xn"], 1)

            def front(b):
                have(dve, "x_in", b)
                norm_stats("l1", x_s, b)

            def front_apply(b):
                have(dve, "xnT_ps", b - 1)
                norm_apply("l1", x_s, b)

            def values_in(b):
                have(dve, "v_ps", b)
                have(dve, "pv_ps", b - 1)
                src = A[0][:, :].rearrange("p (w h d) -> p w h d", h=HG, d=D0)
                dst = V[:, :, :, :, :].rearrange("p n g h c -> p (n g) (h c)")
                for h in range(HG):
                    ins = v.tensor_copy(dst[:, :, (HG * D0 + D0) * h:(HG * D0 + D0) * h + D0], src[:, :, h, :])
                ins.then_inc(sem["v_sb"], 1)

            def row_max(b, k):
                t, hg = k // 4, k % 4
                have(dve, "s_ps", b, k)
                if k == 0:
                    have(dve, "maxT_ps", b - 1)
                v.tensor_reduce(mx[:, HG * hg:HG * hg + HG, t], A[(k + 1) % 2][:, 0:HG * KT]
                                .rearrange("p (h c) -> p h c", c=KT), AX.X, ALU.max).then_inc(sem["rowmax"], 1)

            def max_parts(b):
                have(dve, "maxT_ps", b)
                have(dve, "max_rows", b - 1)
                v.tensor_scalar(nhl[:, 0, :], A[1][0:H0 * T, 0:P], -1.0, None, ALU.mult).then_inc(sem["max_hi"], 1)
                have(dve, "max_hi", b)
                v.scalar_tensor_tensor(out=nhl[:, 1, :], in0=A[1][0:H0 * T, 0:P], scalar=-1.0, in1=nhl[:, 0, :],
                                       op0=ALU.mult, op1=ALU.subtract).then_inc(sem["max_lo"], 1)

            def attn_out(b, half):
                have(dve, "pv_ps", b, 2 * half + 1)
                cols = slice(2 * WIN * half, 2 * WIN * half + 2 * WIN)
                v.reciprocal(rden[:, cols], OV[half][:, 2 * WIN:4 * WIN]).then_inc(sem["rden"], 1)
                have(dve, "rden", b, half)
                if half == 0:
                    have(dve, "op_ps", b - 1)
                v.tensor_tensor(oT[:, cols], OV[half][:, 0:2 * WIN], rden[:, cols], ALU.mult).then_inc(sem["o_div"], 1)

            def add1(b):
                have(dve, "op_ps", b)
                have(dve, "xres", b)
                have(dve, "x1_kept", b - 1)
                v.tensor_tensor(x1[:, :, :], O[:, 0, :].rearrange("p (t d) -> p t d", t=T), xres[:, :, :], ALU.add)\
                    .then_inc(sem["x1"], 1)

            def ffn_norm(b):
                have(dve, "x1", b)
                norm_stats("l2", x1, b)

            def ffn_max(b):
                have(dve, "l2_xn", b)
                v.tensor_reduce(am1[:, :], xn["l2"][:, :, :], AX.X, ALU.max, apply_absolute_value=True)\
                    .then_inc(sem["q1_max"], 1)

            def ffn_quant(b):
                have(dve, "q1_max", b)
                v.tensor_scalar(cl1[:, :], am1[:, :], Q_EPS, None, ALU.max).then_inc(sem["q1_clip"], 1)
                have(dve, "q1_clip", b)
                v.reciprocal(rc1[:, :], cl1[:, :]).then_inc(sem["q1_rec"], 1)
                have(dve, "q1b_ps", b - 1)
                v.tensor_scalar(iv1[:, :], cl1[:, :], 1.0 / 127, wmean[:, 0:1], ALU.mult, ALU.mult)\
                    .then_inc(sem["q1_inv"], 1)
                have(dve, "q1_rec", b)
                v.tensor_scalar(s1[:, :], rc1[:, :], 127.0, None, ALU.mult).then_inc(sem["q1_s"], 1)
                have(dve, "q1_s", b)
                for t in range(T):
                    v.tensor_scalar(big1[:, t, :], xn["l2"][:, t, :], s1[:, t:t + 1], MAGIC, ALU.mult, ALU.add)\
                        .then_inc(sem["q1_big"], 1)
                have(dve, "q1_big", b)
                have(dve, "q1T_ps", b - 1)
                v.tensor_scalar(int1[:, :, :], big1[:, :, :], MAGIC, 127.0, ALU.subtract, ALU.min)\
                    .then_inc(sem["q1_int"], 1)

            def ffn_take(b):
                have(dve, "q1b_sb", b)
                have(dve, "c_all", b - 1)
                for f in range(2):
                    have(dve, "h_ps", b, f)
                    v.tensor_tensor(hs[:, 2 * f:2 * f + 2, 1:S + 1], F[f][:, :].rearrange("p (c s) -> p c s", c=2),
                                    q1b[:, None, :].broadcast_to([P, 2, S]), ALU.mult).then_inc(sem["h_sb"], 1)

            def ffn_conv(b, half):
                for c in (2 * half, 2 * half + 1):
                    have(dve, "c_mid", b, c)
                    v.scalar_tensor_tensor(out=hc[:, c, :], in0=hs[:, c, 0:S], scalar=cw[:, c, 0:1], in1=hc[:, c, :],
                                           op0=ALU.mult, op1=ALU.add).then_inc(sem["c_left"], 1)
                for c in (2 * half, 2 * half + 1):
                    have(dve, "c_left", b, c)
                    v.scalar_tensor_tensor(out=hc[:, c, :], in0=hs[:, c, 2:S + 2], scalar=cw[:, c, 2:3],
                                           in1=hc[:, c, :], op0=ALU.mult, op1=ALU.add).then_inc(sem["c_all"], 1)

            def ffn_silu(b, half):
                cs = slice(2 * half, 2 * half + 2)
                have(dve, "th", b, half)
                v.scalar_tensor_tensor(out=hc[:, cs, :], in0=th[:, cs, :], scalar=1.0, in1=hc[:, cs, :], op0=ALU.add,
                                       op1=ALU.mult).then_inc(sem["silu"], 1)

            def ffn_quant2(b):
                for t in range(T):
                    have(dve, "hT_ps", b, t)
                    v.tensor_reduce(am2[:, t:t + 1], F[t][:, :], AX.X, ALU.max, apply_absolute_value=True)\
                        .then_inc(sem["q2_max"], 1)
                have(dve, "q2_max", b)
                v.tensor_scalar(cl2[:, :], am2[:, :], 2 * Q_EPS, None, ALU.max).then_inc(sem["q2_clip"], 1)
                have(dve, "q2_clip", b)
                v.reciprocal(rc2[:, :], cl2[:, :]).then_inc(sem["q2_rec"], 1)
                v.tensor_scalar(iv2[:, :], cl2[:, :], 0.5 / 127, wmean[:, 1:2], ALU.mult, ALU.mult)\
                    .then_inc(sem["q2_inv"], 1)
                have(dve, "q2_rec", b)
                have(dve, "q2b_ps", b - 1)
                v.tensor_scalar(s2[:, :], rc2[:, :], 127.0, None, ALU.mult).then_inc(sem["q2_s"], 1)

            def ffn_round2(b):
                have(dve, "q2b_sb", b)
                for t in range(T):
                    cols = slice(P * t, P * t + P)
                    v.tensor_tensor(th[:, :, cols], hc[:, :, cols], q2b[:, None, cols].broadcast_to([P, HC, P]), ALU.mult)\
                        .then_inc(sem["q2_big"], 1)
                have(dve, "f_ps", b - 1)
                for t in range(T):
                    cols = slice(P * t, P * t + P)
                    have(dve, "q2_big", b, t)
                    v.tensor_scalar(int2[:, :, cols], th[:, :, cols], MAGIC, MAGIC, ALU.add, ALU.subtract)\
                        .then_inc(sem["q2_int"], 1)

            def add2(b):
                have(dve, "f_ps", b)
                have(dve, "q2_inv", b)
                have(dve, "x1_kept", b)
                have(dve, "x2res", b - 1)
                for t in range(T):
                    v.scalar_tensor_tensor(out=x2[:, t, :], in0=F[1][:, P * t:P * t + P], scalar=iv2[:, t:t + 1],
                                           in1=x1k[:, t, :], op0=ALU.mult, op1=ALU.add).then_inc(sem["x2"], 1)

            def mix_in(b):
                have(dve, "m_ps", b - 1)
                v.tensor_copy(uslot[:, :], urow[:, b, :]).then_inc(sem["u_slot"], 1)

            def mix_out(b):
                have(dve, "m_ps", b)
                have(dve, "a_ps", b - 1)
                v.tensor_copy(M[:, :], MB[0][:, 0:P]).then_inc(sem["m_sb"], 1)

            def norm3(b):
                norm_stats("l3", x2, b, "x2")

            def attend(b):
                have(dve, "a_ps", b)
                have(dve, "x2res", b)
                for t in range(T):
                    v.tensor_tensor(x3[:, t, :], MB[2][:, P * t:P * t + P], x2res[:, t, :], ALU.add).then_inc(sem["x3"], 1)
                norm_stats("l4", x3, b, "x3")

            def route(b, rows, quant):
                n = [0]
                between = {6: lambda: gate(b, 0), 7: lambda: gate_by_up(b, 0),
                           9: lambda: gate(b, 1), 10: lambda: gate_by_up(b, 1), 12: lambda: quant is None or ffn_max(quant),
                           16: lambda: rows is None or row_max(rows, 0), 18: lambda: gate(b, 2),
                           19: lambda: rows is None or row_max(rows, 1), 20: lambda: gate_by_up(b, 2)}

                def link(ins, wait=True):
                    ins.then_inc(sem["gate"], 1)
                    n[0] += 1
                    if n[0] in between:
                        between[n[0]]()
                    if wait and n[0] < COUNT["gate"]:
                        if n[0] in (6, 8, 11, 14):
                            dve.drain()
                        else:
                            have(dve, "gate", b, n[0] - 1)

                have(dve, "lg_th", b)
                link(v.scalar_tensor_tensor(out=sc[:, :, :], in0=lth[:, :, :], scalar=0.5,
                                            in1=gbh[:, None, :].broadcast_to([P, T, E]), op0=ALU.mult, op1=ALU.add))
                pairs = sc[:, :, :].rearrange("p t (g a b) -> p (t g) a b", g=GROUPS, b=2)
                link(v.tensor_tensor(pair_sum[:, :, :], pairs[:, :, :, 0], pairs[:, :, :, 1], ALU.add), False)
                link(v.tensor_tensor(pair_max[:, :, :], pairs[:, :, :, 0], pairs[:, :, :, 1], ALU.max))
                link(v.tensor_tensor(cross[:, :], pair_max[:, :, 0], pair_max[:, :, 1], ALU.add), False)
                link(v.tensor_tensor(same[:, :], pair_sum[:, :, 0], pair_sum[:, :, 1], ALU.max))
                link(v.tensor_tensor(gsum[:, :, 0:GROUPS], cross[:, :].rearrange("p (t g) -> p t g", t=T),
                                     same[:, :].rearrange("p (t g) -> p t g", t=T), ALU.max))
                for t in range(T):
                    ins = v.max(gtop[:, t, :], gsum[:, t, :])
                link(ins)
                link(v.tensor_copy(repg[:, :, 0:TOPG], gtop[:, :, 0:TOPG]))
                for t in range(T):
                    ins = v.match_replace(gmark[:, t, :], repg[:, t, :], gsum[:, t, :], PICKED)
                link(ins)
                link(v.tensor_scalar(gsel[:, :, :], gmark[:, :, 0:GROUPS], PICKED, None, ALU.is_equal))
                for t in range(T):
                    ins = v.tensor_tensor(emask[:, t, 0:E].rearrange("p (g e) -> p g e", g=GROUPS),
                                          sc[:, t, :].rearrange("p (g e) -> p g e", g=GROUPS),
                                          gsel[:, t, :, None].broadcast_to([P, GROUPS, EG]), ALU.mult)
                link(ins)
                for t in range(T):
                    ins = v.max(etop[:, t, :], emask[:, t, :])
                link(ins)
                link(v.tensor_copy(repe[:, :, 0:TOPK], etop[:, :, 0:TOPK]), False)
                link(v.tensor_reduce(tsum[:, :], etop[:, :, 0:TOPK], AX.X, ALU.add))
                link(v.tensor_scalar(trec[:, :], tsum[:, :], 1e-20, None, ALU.add), False)
                for t in range(T):
                    ins = v.match_replace(emark[:, t, :], repe[:, t, :], emask[:, t, :], PICKED)
                link(ins)
                link(v.reciprocal(tnorm[:, :], trec[:, :]), False)
                link(v.scalar_tensor_tensor(out=wsel[:, :, :], in0=emark[:, :, 0:E], scalar=PICKED, in1=emask[:, :, 0:E],
                                            op0=ALU.is_equal, op1=ALU.mult))
                for t in range(T):
                    ins = v.tensor_scalar(comb[:, t, :], wsel[:, t, :], tnorm[:, t:t + 1], 0.5 * GSCALE,
                                          ALU.mult, ALU.mult)
                link(ins)
                have(dve, "cT_ps", b - 1)
                link(v.tensor_copy(cparts[:, :, 0, 0:E], comb[:, :, :]))
                v.tensor_tensor(cr1[:, :, :], comb[:, :, :], cparts[:, :, 0, 0:E], ALU.subtract).then_inc(s_gate2, 1)
                dve.wait_ge(s_gate2, 3 * b + 1)
                v.tensor_copy(cparts[:, :, 1, 0:E], cr1[:, :, :]).then_inc(s_gate2, 1)
                dve.wait_ge(s_gate2, 3 * b + 2)
                v.tensor_tensor(cr2[:, :, :], cr1[:, :, :], cparts[:, :, 1, 0:E], ALU.subtract).then_inc(s_gate2, 1)
                dve.wait_ge(s_gate2, 3 * b + 3)
                link(v.tensor_copy(cparts[:, :, 2, 0:E], cr2[:, :, :]))
                assert n[0] == COUNT["gate"], n[0]

            def gate(b, c):
                have(dve, "g_th", b, c)
                if c == 0:
                    have(dve, "y_ps", b - 1)
                v.scalar_tensor_tensor(out=ga[:, c % RING, :], in0=gth[:, c % RING, :], scalar=1.0,
                                       in1=R[c % RING][:, 0:S], op0=ALU.add, op1=ALU.mult).then_inc(sem["m_a"], 1)

            def gate_by_up(b, c):
                have(dve, "m_a", b, c)
                if c < EC:
                    v.tensor_tensor(inter[:, c, :], ga[:, c % RING, :], R[c % RING][:, S:2 * S], ALU.mult)\
                        .then_inc(sem["m_b"], 1)
                else:
                    v.scalar_tensor_tensor(out=inter[:, c, :], in0=ga[:, c % RING, :], scalar=0.5,
                                           in1=R[c % RING][:, S:2 * S], op0=ALU.mult, op1=ALU.mult).then_inc(sem["m_b"], 1)

            def finish(b):
                have(dve, "y_ps", b)
                have(dve, "out_st", b - 1)
                v.tensor_tensor(y[:, :, :], Y[:, 0:S].rearrange("p (t d) -> p t d", t=T), x3[:, :, :], ALU.add)\
                    .then_inc(sem["out_sb"], 1)

            made = []

            def put(name, ap, value):
                made.append(name)
                v.memset(ap, value).then_inc(s_fill, 1)

            def fill_first():
                put("mhalf", mhalf[:, :], -0.5)
                put("eps", eps[:, :], LN_EPS)
                put("pad", ctxT[:, 0:WIN], 0.0)
                put("ident", ident[:, :], 0.0)
                put("identb", identb[:, :], 0.0)

            def fill_masks():
                put("K_empty", K[:, :, 0:WIN], 0.0)
                put("mask_s", mask_s[:, :, :], 0.0)
                put("mask_t", mask_t[:, :, :], 0.0)

            def fill_rest():
                put("K", K[32:ROWS + 2, :, WIN:], 1.0)
                put("V", V[:, :, :, :, :], 0.0)
                put("denom", denom[:, :, :], 0.0)
                put("ones", ones[:, :], 1.0)
                put("pick", pick[:, :, :, :], 1.0)
                put("cparts", cparts[:, :, :, :], 0.0)
                wait_made(dve, s_fill, FILLS, "cparts")
                for h in range(HG):
                    put("denom_own", denom[:, h, D0 * h:D0 * h + D0], 1.0)
                assert made == FILLS

            def setup_bo():
                dve.wait_ge(s_bias, 1)
                v.tensor_tensor(bo[:, :], bo[:, :], O[:, 0, 0:P], ALU.add).then_inc(s_bias, 1)

            def setup_queries():
                dve.wait_ge(loaded["queries"], 16)
                step(v.tensor_reduce(qsum[:, :], Wq[:, :, :], AX.X, ALU.add))
                dve.wait_ge(s_setv, 1)
                step(v.tensor_tensor(qshift[:, :], bq1, qsum[:, :], ALU.subtract))
                dve.wait_ge(s_setv, 2)
                step(v.tensor_scalar(qsum[:, :], qshift[:, :], 1.0 / P, None, ALU.mult))
                dve.wait_ge(s_setv, 3)
                for c in range(C1):
                    step(v.tensor_scalar(Wq[:, c, :], Wq[:, c, :], qsum[:, c:c + 1], None, ALU.add))
                assert setv[0] == SV_WQ

            def setup_magnitudes():
                dve.wait_ge(loaded["ffn"], N_FFN)
                for i, w_ in enumerate((w1, w2)):
                    step(v.tensor_reduce(wabs[:, i:i + 1], w_[:, :], AX.X, ALU.add, apply_absolute_value=True))
                assert setv[0] == SV_ABS

            def setup_scales():
                dve.wait_ge(s_setp, 3)
                step(v.tensor_scalar(wmean[:, :], MB[2][:, 0:2], 1.0 / (HC * P * P), Q_EPS, ALU.mult, ALU.max))
                dve.wait_ge(s_setv, setv[0])
                step(v.reciprocal(wrec[:, :], wmean[:, :]))
                assert setv[0] == SV_SCALES
                dve.wait_ge(s_setv, setv[0])

            def setup_weights():
                for i, w_ in enumerate((w1, w2)):
                    step(v.tensor_scalar(w_[:, :], w_[:, :], wrec[:, i:i + 1], MAGIC, ALU.mult, ALU.add))
                dve.wait_ge(s_setv, setv[0])
                for w_ in (w1, w2):
                    step(v.tensor_scalar(w_[:, :], w_[:, :], MAGIC, 1.0, ALU.subtract, ALU.min))
                dve.wait_ge(s_setv, setv[0])
                for w_, q_ in ((w1, w1q), (w2, w2q)):
                    step(v.tensor_scalar(q_[:, :], w_[:, :], -1.0, None, ALU.max))
                step(v.memset(hs[:, :, 0:1], 0.0))
                step(v.memset(hs[:, :, S + 1:S + 2], 0.0))
                for r_ in (gsum, emask, repg, repe):
                    step(v.memset(r_[:, :, :], GONE))
                step(v.memset(bkd[:, :, :], 0.0))
                step(v.memset(bvd[:, :, :], 0.0))
                dve.wait_ge(s_setv, setv[0])
                for d_, b_ in ((bkd, bk1), (bvd, bv1)):
                    flat = d_[:, :, :].rearrange("p c h -> p (c h)")
                    for half in range(2):
                        rows = slice(D1 * half, D1 * half + D1)
                        step(v.tensor_copy(flat[rows, half:half + (H1 + 2) * (C1 - 1) + 1:H1 + 2], b_[rows, :]))
                dve.wait_ge(loaded["sums"], N_SUMS)
                step(v.tensor_reduce(csum[:, :], ctx_all[:, :, :], AX.X, ALU.add))
                assert setv[0] == SV_BD

            def setup_bias_rows():
                dve.wait_ge(s_setp, 6)
                step(v.tensor_scalar(arow[:, :], MB[1][0:H1, 0:P], SCALE1, None, ALU.mult))
                step(v.tensor_copy(brow[:, :], MB[1][0:H1, P:2 * P]))
                step(v.tensor_scalar(brow_n[:, :], MB[1][0:H1, P:2 * P], float(S), None, ALU.mult))
                assert setv[0] == SV_ROWS, setv[0]

            def setup_sum_rows():
                for k in range(8):
                    dve.wait_ge(s_setp, 7 + k)
                    step(v.tensor_copy((uflat if k < 4 else pflat)[:, 4 * P * (k % 4):4 * P * (k % 4) + 4 * P],
                                       MB[k % 2][0:B, :]))

            def setup_rows():
                dve.wait_ge(s_rows, 16 * 2 * B)
                dve.wait_ge(s_setv, setv[0])
                step(v.tensor_tensor(prow[:, :, :], prow[:, :, :], brow_n[:, None, :].broadcast_to([H1, B, P]), ALU.add))
                dve.wait_ge(s_setv, setv[0])
                assert setv[0] == SV_END

            def iteration(t, stage1=True, stage2=True, nxt=True, second=False):
                if stage2:
                    ffn_take(t - 1)
                if second:
                    setup_rows()
                    dve.wait_ge(loaded["moe"], N_MOE)
                    step(v.tensor_scalar(gbh[:, :], gb[:, :], 0.5, None, ALU.add))
                    dve.wait_ge(s_setv, setv[0])
                if stage2:
                    ffn_conv(t - 1, 0)
                    ffn_conv(t - 1, 1)
                    mix_in(t - 1)
                if nxt:
                    front(t + 1)
                if stage2:
                    ffn_silu(t - 1, 0)
                    ffn_silu(t - 1, 1)
                if nxt:
                    front_apply(t + 1)
                if stage2:
                    ffn_quant2(t - 1)
                if stage1:
                    attn_out(t, 0)
                if stage2:
                    ffn_round2(t - 1)
                    add2(t - 1)
                    norm3(t - 1)
                if stage1:
                    attn_out(t, 1)
                if stage2:
                    norm_apply("l3", x2, t - 1)
                    mix_out(t - 1)
                    attend(t - 1)
                if nxt:
                    values_in(t + 1)
                if stage1:
                    add1(t)
                if stage2:
                    norm_apply("l4", x3, t - 1)
                if stage1:
                    ffn_norm(t)
                    norm_apply("l2", x1, t)
                if stage2:
                    route(t - 1, t + 1 if nxt else None, t if stage1 else None)
                    gate(t - 1, 3)
                    gate(t - 1, 4)
                    for c in (3, 4):
                        gate_by_up(t - 1, c)
                        if nxt:
                            row_max(t + 1, c - 1)
                    for c in range(AHEAD, MC):
                        gate(t - 1, c)
                        if nxt:
                            row_max(t + 1, c - 1)
                        gate_by_up(t - 1, c)
                        if stage1 and c == AHEAD:
                            ffn_quant(t)
                else:
                    ffn_max(t)
                    ffn_quant(t)
                    setup_sum_rows()
                    for k in range(8):
                        row_max(t + 1, k)
                if nxt:
                    max_parts(t + 1)
                if stage2:
                    finish(t - 1)

            fill_first()
            front(0)
            fill_masks()
            front_apply(0)
            fill_rest()
            dve.wait_ge(loaded["l0"], N_L0)
            setup_queries()
            values_in(0)
            setup_bo()
            setup_magnitudes()
            for k in range(8):
                row_max(0, k)
            max_parts(0)
            setup_scales()
            setup_weights()
            setup_bias_rows()
            iteration(0, stage2=False)
            iteration(1, second=True)
            with dve.Fori(2, B - 1) as t:
                iteration(t)
            iteration(B - 1, nxt=False)
            iteration(B, stage1=False, nxt=False)


def _layout(inp):
    f = {k: np.asarray(v) for k, v in inp.items()}

    def tr(w):
        return w.reshape(H0, D0, -1).transpose(1, 0, 2).reshape(P, -1)

    def chunks(w):
        return w.reshape(-1, P, w.shape[-1]).transpose(1, 0, 2)

    def wide(e, sh):
        return np.concatenate([e.transpose(1, 0, 2).reshape(P, E * M1), sh], axis=1).reshape(P, MC, P)

    return {
        "x": f["x"], "ctx": f["ctx_1024"], "ctxT": f["ctx_1024"].transpose(0, 2, 1),
        "w0": np.stack([tr(f["L0_xattn_wq"]).T, tr(f["L0_xattn_wk"]).T, f["L0_xattn_wv"].T, f["L0_xattn_wo"].T], axis=1),
        "columns": np.concatenate([
            tr(f["L0_xattn_bq"][:, None]), tr(f["L0_xattn_bk"][:, None]), f["L0_xattn_bv"][:, None],
            chunks(f["L0_ffn_conv_w"][:, 0, :]).reshape(P, HC * 3), chunks(f["L0_ffn_conv_b"][:, None])[:, :, 0],
            f["L1_xattn_bq"].reshape(C1, P).T, f["L1_xattn_bk"].reshape(C1, P).T, f["L1_xattn_bv"].reshape(C1, P).T],
            axis=1),
        "bo": f["L0_xattn_bo"], "w1": f["L0_ffn_w1"].T, "w2": chunks(f["L0_ffn_w2"].T).reshape(P, HC * P),
        "Wq": chunks(f["L1_xattn_Wq"].T), "Wk": chunks(f["L1_xattn_Wk"].T), "Wv": chunks(f["L1_xattn_Wv"].T),
        "Wo": chunks(f["L1_xattn_Wo"]), "bo1": f["L1_xattn_bo"],
        "gk": f["L1_ffn_gate_kernel"], "gb": f["L1_ffn_gate_bias"],
        "mg": wide(f["L1_ffn_w_gate"], f["L1_ffn_sw_gate"]), "mu": wide(f["L1_ffn_w_up"], f["L1_ffn_sw_up"]),
        "md": chunks(np.concatenate([f["L1_ffn_w_down"].reshape(E * M1, P), f["L1_ffn_sw_down"]])),
    }


def kernel(**inputs):
    import concourse.bacc as bacc
    from concourse.bass_utils import run_bass_kernel_spmd

    nc = bacc.Bacc("TRN2", target_bir_lowering=False, num_devices=1)
    laid = _layout(inputs)
    arrays, a = {}, {}
    for name in INPUTS:
        arr = np.ascontiguousarray(laid[name])
        arrays["in_" + name] = arr
        a[name] = nc.dram_tensor("in_" + name, arr.shape, mybir.dt.from_np(arr.dtype), kind="ExternalInput").ap()
    out = nc.dram_tensor("out", (B, S, P), F32, kind="ExternalOutput").ap()
    layers_kernel(nc, a, out)
    r = run_bass_kernel_spmd(nc, [arrays], core_ids=[0])
    return r.results[0]["out"]
```
